# Optimizing a Trainium2 kernel written in Bass

```python
import numpy as np
import jax
import jax.numpy as jnp

def _softmax(x, axis=-1):
    return jax.nn.softmax(x, axis=axis)

def _gelu(x):
    return jax.nn.gelu(x, approximate=True)

def _silu(x):
    return jax.nn.silu(x)

def _sigmoid(x):
    return jax.nn.sigmoid(x)

def _layernorm(x, axis=-1, eps=1e-05):
    m = jnp.mean(x, axis=axis, keepdims=True)
    v = jnp.var(x, axis=axis, keepdims=True)
    return (x - m) / jnp.sqrt(v + eps)

def _scatter_add(tgt, idx, src, axis=0):
    return tgt.at[idx].add(src)

def _segment_sum(src, seg, n):
    return jax.ops.segment_sum(src, seg, n)
kernel_name = 'mk_macaron_d1_jaxref_r4_2db4b9'

def setup_inputs(seed: int=0):
    np.random.seed(seed)
    _w = jnp.asarray

    def _L0_attn_setup():
        import jax, jax.numpy as jnp
        import numpy as np
        import math
        DIM = 256
        ATTN_DIM = 256
        B, S = (2, 1024)
        key = jax.random.key(seed)
        k1, k2, k3 = jax.random.split(key, 3)
        x = jax.random.normal(k1, (B, S, DIM), dtype=jnp.float32)
        W_qkv = jax.random.normal(k2, (3 * ATTN_DIM, DIM), dtype=jnp.float32) * (1.0 / math.sqrt(DIM))
        b_qkv = jax.random.normal(k3, (3 * ATTN_DIM,), dtype=jnp.float32) * 0.01
        return {'x': x, 'W_qkv': W_qkv, 'b_qkv': b_qkv}
    _L0_attn_in = _L0_attn_setup()

    def _L0_ffn_setup():
        import jax, jax.numpy as jnp
        import numpy as np
        D_MODEL = 256
        D_FF = 512
        NUM_EXPERTS = 16
        TOP_K = 2
        CAPACITY_FACTOR = 1.25
        BATCH, SEQ = (4, 512)
        key = jax.random.key(seed)
        k0, k1, k2, k3 = jax.random.split(key, 4)
        x = jax.random.normal(k0, (BATCH, SEQ, D_MODEL), jnp.float32)
        gate_w = jax.random.normal(k1, (NUM_EXPERTS, D_MODEL), jnp.float32) / np.float32(np.sqrt(D_MODEL))
        w1 = jax.random.normal(k2, (NUM_EXPERTS, D_MODEL, D_FF), jnp.float32) / np.float32(np.sqrt(D_MODEL))
        w2 = jax.random.normal(k3, (NUM_EXPERTS, D_FF, D_MODEL), jnp.float32) / np.float32(np.sqrt(D_FF))
        return {'x': x, 'gate_w': gate_w, 'w1': w1, 'w2': w2}
    _L0_ffn_in = _L0_ffn_setup()
    _d = {'L0_attn_x': _L0_attn_in['x'], 'L0_attn_W_qkv': _L0_attn_in['W_qkv'], 'L0_attn_b_qkv': _L0_attn_in['b_qkv'], 'L0_ffn_gate_w': _L0_ffn_in['gate_w'], 'L0_ffn_w1': _L0_ffn_in['w1'], 'L0_ffn_w2': _L0_ffn_in['w2']}
    _x0 = _d['L0_attn_x']
    _d['L0_attn_x'] = jax.random.normal(jax.random.fold_in(jax.random.key(seed), 1), (8, 1024, 256), dtype=_x0.dtype)
    del _x0
    return _d

def reference(L0_attn_x, L0_attn_W_qkv, L0_attn_b_qkv, L0_ffn_gate_w, L0_ffn_w1, L0_ffn_w2):

    def _L0_attn_ref(x, W_qkv, b_qkv):
        import jax, jax.numpy as jnp
        import numpy as np
        import math
        DIM = 256
        ATTN_DIM = 256
        B, S = (2, 1024)
        b, s, d = x.shape
        qkv = jnp.einsum('bsd,ed->bse', x, W_qkv) + b_qkv
        q, k, v = jnp.split(qkv, 3, axis=-1)
        score = jnp.einsum('bqd,bkd->bqk', q, k)
        causal = jnp.tril(jnp.ones((s, s), dtype=bool))
        score = jnp.where(causal, score, -jnp.inf)
        attn = jax.nn.softmax(score / math.sqrt(ATTN_DIM), axis=-1)
        y = jnp.einsum('bqk,bkd->bqd', attn, v)
        return y

    def _L0_ffn_ref(x, gate_w, w1, w2):
        import jax, jax.numpy as jnp
        import numpy as np
        D_MODEL = 256
        D_FF = 512
        NUM_EXPERTS = 16
        TOP_K = 2
        CAPACITY_FACTOR = 1.25
        BATCH, SEQ = (4, 512)
        B, S, d = x.shape
        T = B * S
        E, K = (NUM_EXPERTS, TOP_K)
        capacity = int(CAPACITY_FACTOR * T * K / E)
        xf = x.reshape(T, d)
        logits = xf @ gate_w.T
        probs = jax.nn.sigmoid(logits)
        top_vals, sel = jax.lax.top_k(probs, K)
        weights = top_vals / (top_vals.sum(-1, keepdims=True) + 1e-06)
        flat_sel = sel.reshape(-1)
        onehot = jax.nn.one_hot(flat_sel, E, dtype=jnp.int32)
        ranks = jnp.take_along_axis(jnp.cumsum(onehot, axis=0), flat_sel[:, None], axis=1)[:, 0] - 1
        valid = ranks < capacity
        sentinel = E * capacity
        slot = jnp.where(valid, flat_sel * capacity + ranks, sentinel)
        x_rep = jnp.repeat(xf, K, axis=0)
        padded = jnp.zeros((sentinel + 1, d), xf.dtype).at[slot].set(x_rep)
        padded = padded[:sentinel].reshape(E, capacity, d)
        h = jax.nn.gelu(jnp.einsum('ecd,edf->ecf', padded, w1), approximate=False)
        out_padded = jnp.einsum('ecf,efd->ecd', h, w2).reshape(sentinel, d)
        gathered = out_padded[jnp.minimum(slot, sentinel - 1)]
        gathered = jnp.where(valid[:, None], gathered, jnp.zeros((), xf.dtype))
        out = (gathered * weights.reshape(-1)[:, None]).reshape(T, K, d).sum(axis=1)
        return out.reshape(B, S, d)
    x = L0_attn_x
    x = x + 0.5 * _L0_ffn_ref(_layernorm(x, axis=-1), L0_ffn_gate_w, L0_ffn_w1, L0_ffn_w2)
    x = x + _L0_attn_ref(_layernorm(x, axis=-1), L0_attn_W_qkv, L0_attn_b_qkv)
    x = x + 0.5 * _L0_ffn_ref(_layernorm(x, axis=-1), L0_ffn_gate_w, L0_ffn_w1, L0_ffn_w2)
    return x

_drawn_inputs = setup_inputs


def setup_inputs(seed=0):
    import zlib

    import numpy as np

    out = dict(_drawn_inputs(seed))
    spreads = {}
    factors = {}
    for name, (base, spread) in spreads.items():
        noise = np.random.default_rng([zlib.crc32(name.encode()), seed]).standard_normal(out[name].shape)
        drawn = base * np.exp(spread * noise) if base else spread * noise
        out[name] = jnp.asarray(drawn.astype(out[name].dtype))
    for name, factor in factors.items():
        out[name] = (out[name] * factor).astype(out[name].dtype)
    return out
```

```python
from contextlib import ExitStack

import numpy as np
import concourse.bass as bass
from concourse import mybir

F32 = mybir.dt.float32
F32R = mybir.dt.float32r
BF16 = mybir.dt.bfloat16
F16 = mybir.dt.float16
I32 = mybir.dt.int32
U32 = mybir.dt.uint32
ALU = mybir.AluOpType
ACT = mybir.ActivationFunctionType
AX = mybir.AxisListType

P = 128
BATCH, SEQ, D = 8, 1024, 256
T = BATCH * SEQ
E, FF, TOPK = 16, 512, 2
CAP = int(1.25 * T * TOPK / E)
DC = D // P
FC = FF // P
TPC = SEQ // P
CHUNKS = T // SEQ
TPE = CAP // P
NST = E * TPE
GRP = 2
GPE = TPE // GRP
GT = GRP * P
PAIR = 2 * GPE
NPAIR = E // 2
ROW = D + E
EPS = 1e-5
SCALE = 1.0 / 16.0
MASKED = -1e30
BANK = 512
NXG = 10
NYO = 5
AHEAD = 7
assert CAP % P == 0 and TPE % GRP == 0 and PAIR % NXG == 0 and PAIR % NYO == 0


def after(eng, sem, n):
    if not (isinstance(n, int) and n <= 0):
        eng.wait_ge(sem, n)


def stand_alone(eng, s):
    eng.sem_inc(s.stood_alone, 1)


def in_turn(eng, first, last, body):
    body(first)
    with eng.Fori(first + 1, last) as i:
        body(i)
    body(last)


class Shared:
    pass


def setup_constants(nc, ctx, s, gate_wT):
    def sb(name, shape, dt):
        return ctx.enter_context(nc.sbuf_tensor(name, shape, dt))

    s.ident = sb("ident", [P, P], F32)
    s.ident_bf = sb("ident_bf", [P, P], BF16)
    s.earlier = sb("earlier", [P, P], BF16)
    s.ones_bf = sb("ones_bf", [P, P], BF16)
    s.causal = sb("causal", [P, P], BF16)
    s.iota_tile = sb("iota_tile", [P, NST], F16)
    s.iota_e = sb("iota_e", [P, E], F32)
    s.token = sb("token", [P, TPC], F32)
    s.spare = sb("spare", [P, NST], F32)
    s.gw = sb("gw", [P, DC, E], F32)
    s.zeros = sb("zeros", [P, D], F32)
    s.minus_half = sb("minus_half", [P, TPC], F32)
    s.chunk_at = sb("chunk_at", [P, 1], F32)
    s.carry = sb("carry", [P, E], BF16)
    s.slots = sb("slots", [P, NST], F32)
    s.gather_idx = sb("gather_idx", [P, NST], U32)
    s.scatter_idx = sb("scatter_idx", [P, NST], U32)
    s.psum = ctx.enter_context(nc.psum_tensor("psum", [P, 8 * BANK], F32))

    tmp = ExitStack()
    iota_i = tmp.enter_context(nc.sbuf_tensor("iota_i", [P, NST], I32))
    spare_i = tmp.enter_context(nc.sbuf_tensor("spare_i", [P, NST], I32))
    token_i = tmp.enter_context(nc.sbuf_tensor("token_i", [P, TPC], I32))
    filled = ctx.enter_context(nc.semaphore("const_filled"))
    iotas = ctx.enter_context(nc.semaphore("const_iotas"))
    loaded = ctx.enter_context(nc.semaphore("const_loaded"))
    spare_zeroed = ctx.enter_context(nc.semaphore("const_spare_zeroed"))
    zeroed = ctx.enter_context(nc.semaphore("const_zeroed"))
    s.stood_alone = ctx.enter_context(nc.semaphore("stood_alone"))
    s.constants_ok = ctx.enter_context(nc.semaphore("constants_ok"))
    with nc.Block() as block:
        @block.sync
        def _(sp):
            sp.dma_start(s.gw[:], gate_wT.rearrange("(c p) e -> p c e", p=P)).then_inc(loaded, 16)
            sp.wait_ge(zeroed, 1)
            for stream in (s.x1, s.out):
                for t in range(TPE):
                    sp.dma_start(stream[T + t * P:T + (t + 1) * P, :], s.zeros[:]).then_inc(spare_zeroed, 16)
            sp.wait_ge(loaded, 16)
            sp.wait_ge(spare_zeroed, 16 * 2 * TPE)

        @block.gpsimd
        def _(pool):
            pool.iota(iota_i[:], [[1, NST]], base=0, channel_multiplier=0).then_inc(iotas, 1)
            pool.iota(spare_i[:], [[0, E], [P, TPE]], base=T + 1, channel_multiplier=1).then_inc(iotas, 1)
            pool.iota(token_i[:], [[P, TPC]], base=1, channel_multiplier=1).then_inc(iotas, 1)
            pool.wait_ge(filled, 5)
            for m, fill, op, step, mult in (
                (s.ident, 1.0, ALU.not_equal, -1, 1),
                (s.ident_bf, 1.0, ALU.not_equal, -1, 1),
                (s.earlier, 0.0, ALU.is_gt, 1, -1),
                (s.causal, MASKED, ALU.is_ge, -1, 1),
            ):
                pool.affine_select(out=m[:], in_=m[:], compare_op=op, fill=fill, base=0,
                                   pattern=[[step, P]], channel_multiplier=mult)

        @block.vector
        def _(dve):
            dve.memset(s.ident[:], 0.0).then_inc(filled, 1)
            dve.memset(s.ident_bf[:], 0.0).then_inc(filled, 1)
            dve.memset(s.earlier[:], 1.0).then_inc(filled, 1)
            dve.memset(s.causal[:], 0.0).then_inc(filled, 1)
            dve.memset(s.ones_bf[:], 1.0).then_inc(filled, 1)
            dve.memset(s.minus_half[:], -0.5)
            dve.memset(s.zeros[:], 0.0).then_inc(zeroed, 1)
            dve.memset(s.carry[:], 0.0)
            dve.memset(s.slots[:], 0.0)
            dve.wait_ge(iotas, 3)
            dve.tensor_copy(s.iota_tile[:], iota_i[:])
            dve.tensor_copy(s.iota_e[:], iota_i[:, 0:E])
            dve.tensor_copy(s.token[:], token_i[:])
            dve.memset(s.chunk_at[:], 0.0)
            dve.tensor_copy(s.spare[:], spare_i[:]).then_inc(s.constants_ok, 1)
            dve.wait_ge(s.constants_ok, 1)
    tmp.close()


NORM_STEPS = 4


def norm_factors(pool, s, mv, vareps, rstd, shift, sem, c):
    n = c * NORM_STEPS
    stand_alone(pool, s)
    pool.tensor_scalar(vareps[:], mv[:, :, 1], EPS, None, ALU.add).then_inc(sem, 1)
    pool.wait_ge(sem, n + 1)
    pool.tensor_tensor(rstd[:], vareps[:], s.minus_half[:], ALU.pow).then_inc(sem, 1)
    pool.wait_ge(sem, n + 2)
    pool.tensor_tensor(vareps[:], mv[:, :, 0], rstd[:], ALU.mult).then_inc(sem, 1)
    pool.wait_ge(sem, n + 3)
    stand_alone(pool, s)
    pool.tensor_scalar(shift[:], vareps[:], -1.0, None, ALU.mult).then_inc(sem, 1)


class Router:

    PLACED = 12
    CHAIN = 13

    def __init__(self, nc, ctx, s, name, source, banks):
        def sb(n, shape, dt):
            return ctx.enter_context(nc.sbuf_tensor(f"{name}_{n}", shape, dt))

        def sem(n):
            return s.sems.enter_context(nc.semaphore(f"{name}_{n}"))

        self.nc, self.s, self.source, self.banks = nc, s, source, banks
        self.xc = sb("xc", [P, TPC, D], F32)
        self.xn = sb("xn", [P, TPC, D], F32)
        self.xnT = sb("xnT", [P, DC, SEQ], F32)
        self.stats = sb("stats", [P, TPC, 6], F32)
        self.mv = sb("mv", [P, TPC, 2], F32)
        self.vareps = sb("vareps", [P, TPC], F32)
        self.rstd = sb("rstd", [P, TPC], F32)
        self.shift = sb("shift", [P, TPC], F32)
        self.ex = sb("ex", [P, TPC * E], F32)
        self.ex1 = sb("ex1", [P, TPC * E], F32)
        self.prob = sb("prob", [P, TPC * E], F32)
        self.top = sb("top", [P, TPC, 8], F32)
        self.idx = sb("idx", [P, TPC, 8], U32)
        self.idf = sb("idf", [P, TOPK, TPC], F32)
        self.sum1 = sb("sum1", [P, TPC], F32)
        self.sum2 = sb("sum2", [P, TPC], F32)
        self.rsum = sb("rsum", [P, TPC], F32)
        self.wt = sb("wt", [P, TOPK, TPC], F32)
        self.oh = sb("oh", [P, TOPK, TPC, E], F32)
        self.chosen = sb("chosen", [P, TPC, E], BF16)
        self.gt = sb("gt", [P, TOPK, TPC, E], F32)
        self.gate = sb("gate", [P, TPC, E], F32)
        self.taken = sb("taken", [P, E], BF16)
        self.rk = sb("rk", [P, TOPK, TPC, E], F32)
        self.rank = sb("rank", [P, TOPK, TPC], F32)
        self.rank_i = sb("rank_i", [P, TOPK, TPC], I32)
        self.high = sb("high", [P, TOPK, TPC], I32)
        self.low = sb("low", [P, TOPK, TPC], I32)
        self.lowf = sb("lowf", [P, TOPK, TPC], F32)
        self.over = sb("over", [P, TOPK, TPC], F32)
        self.tile1 = sb("tile1", [P, TOPK, TPC], F32)
        self.tilef = sb("tilef", [P, TOPK, TPC], F32)
        self.onehot_row = sb("onehot_row", [P, TPC, TOPK, P], F16)
        self.onehot_tile = sb("onehot_tile", [P, TPC, TOPK, NST], F16)
        self.taken_slot = sb("taken_slot", [P, NST], F32)

        self.x_in = sem("x_in")
        self.stat = sem("stat")
        self.meanvar = sem("meanvar")
        self.scaled = sem("scaled")
        self.normed = sem("normed")
        self.xn_out = sem("xn_out")
        self.turned = sem("turned")
        self.logits = sem("logits")
        self.chain = sem("chain")
        self.chosen_ok = sem("chosen_ok")
        self.gate_ok = sem("gate_ok")
        self.gate_out = sem("gate_out")
        self.ranked = sem("ranked")
        self.onehots = sem("onehots")
        self.row_onehots = sem("row_onehots")
        self.listed = sem("listed")
        self.carried = sem("carried")
        self.read = [sem(f"read{u}") for u in range(7)]

    def bank(self, u):
        b = self.banks[u % len(self.banks)]
        return self.s.psum[:, b * BANK:(b + 1) * BANK]

    def wait_bank(self, pe, u, c):
        if len(self.banks) == 1 and u > 0:
            after(pe, self.read[u - 1], c + 1)
        else:
            after(pe, self.read[u if len(self.banks) > 1 else 6], c)

    def load(self, sp, c):
        after(sp, self.normed, c * TPC)
        src = self.source[bass.ds(c * SEQ, SEQ), :]
        sp.dma_start(self.xc[:], src.rearrange("(j p) d -> p j d", p=P)).then_inc(self.x_in, 16)

    def store_rows(self, sp, c):
        sp.wait_ge(self.normed, c * TPC + TPC)
        dst = self.s.rows[bass.ds(c * SEQ, SEQ), 0:D]
        sp.dma_start(dst.rearrange("(j p) d -> p j d", p=P), self.xn[:]).then_inc(self.xn_out, 16)

    def store_gates(self, sp, c):
        sp.wait_ge(self.gate_ok, c + 1)
        dst = self.s.rows[bass.ds(c * SEQ, SEQ), D:ROW]
        sp.dma_start(dst.rearrange("(j p) d -> p j d", p=P), self.gate[:]).then_inc(self.gate_out, 16)

    def dve_stats(self, dve, c):
        dve.wait_ge(self.x_in, c * 16 + 16)
        for j in range(TPC):
            last = dve.bn_stats(self.stats[:, j, :], self.xc[:, j, :])
        last.then_inc(self.stat, 1)
        dve.wait_ge(self.stat, c + 1)
        after(dve, self.normed, c * TPC)
        stand_alone(dve, self.s)
        for j in range(TPC):
            last = dve.bn_aggr(self.mv[:, j, :], self.stats[:, j, :])
        last.then_inc(self.meanvar, 1)

    def pool_scale(self, pool, c):
        pool.wait_ge(self.meanvar, c + 1)
        norm_factors(pool, self.s, self.mv, self.vareps, self.rstd, self.shift, self.scaled, c)

    def act_norm(self, act, c):
        act.wait_ge(self.scaled, c * NORM_STEPS + NORM_STEPS)
        after(act, self.turned, c * 4)
        after(act, self.xn_out, c * 16)
        for j in range(TPC):
            act.activation(self.xn[:, j, :], self.xc[:, j, :], ACT.Identity, bias=self.shift[:, j:j + 1],
                           scale=self.rstd[:, j:j + 1]).then_inc(self.normed, 1)

    def pe_turn(self, pe, c):
        for u in range(4):
            pe.wait_ge(self.normed, c * TPC + 2 * u + 2)
            self.wait_bank(pe, u, c)
            bank = self.bank(u)
            for k in range(4):
                d, j = k // 2, 2 * u + k % 2
                last = pe.transpose(bank[:, k * P:(k + 1) * P], self.xn[:, j, d * P:(d + 1) * P], self.s.ident[:])
            last.then_inc(self.turned, 1)

    def act_turn(self, act, c):
        after(act, self.logits, c)
        for u in range(4):
            act.wait_ge(self.turned, c * 4 + u + 1)
            act.activation(self.xnT[:, :, 2 * u * P:(2 * u + 2) * P],
                           self.bank(u).rearrange("p (d t) -> p d t", d=DC), ACT.Copy).then_inc(self.read[u], 1)

    def pe_logits(self, pe, c):
        for u in range(4):
            pe.wait_ge(self.read[u], c + 1)
        self.wait_bank(pe, 4, c)
        for j in range(TPC):
            for d in range(DC):
                last = pe.matmul(self.bank(4)[:, j * E:(j + 1) * E], self.xnT[:, d, j * P:(j + 1) * P],
                                 self.s.gw[:, d, :], start=(d == 0), stop=(d == DC - 1))
        last.then_inc(self.logits, 1)

    def act_exp(self, act, c):
        act.wait_ge(self.logits, c + 1)
        after(act, self.carried, c)
        act.activation(self.ex[:], self.bank(4)[:, 0:TPC * E], ACT.Exp, scale=-1.0).then_inc(self.read[4], 1)

    def dve_choose(self, dve, c):
        self.links = 0

        def link(ins):
            self.links += 1
            ins.then_inc(self.chain, 1)
            dve.wait_ge(self.chain, c * self.CHAIN + self.links)

        s = self.s
        dve.wait_ge(self.read[4], c + 1)
        link(dve.tensor_scalar(self.ex1[:], self.ex[:], 1.0, None, ALU.add))
        link(dve.reciprocal(self.prob[:], self.ex1[:]))
        stand_alone(dve, s)
        for j in range(TPC):
            last = dve.max(self.top[:, j, :], self.prob[:, j * E:(j + 1) * E])
        link(last)
        dve.tensor_tensor(self.sum1[:], self.top[:, :, 0], self.top[:, :, 1], ALU.add)
        for j in range(TPC):
            last = dve.max_index(self.idx[:, j, :], self.top[:, j, :], self.prob[:, j * E:(j + 1) * E])
        link(last)
        dve.tensor_copy(self.idf[:], self.idx[:, :, 0:TOPK].rearrange("p j k -> p k j"))
        link(dve.tensor_scalar(self.sum2[:], self.sum1[:], 1e-6, None, ALU.add))
        link(dve.reciprocal(self.rsum[:], self.sum2[:]))
        dve.scalar_tensor_tensor(self.wt[:], self.top[:, :, 0:TOPK].rearrange("p j k -> p k j"), 0.5,
                                 self.rsum[:].unsqueeze(1).to_broadcast([P, TOPK, TPC]), ALU.mult, ALU.mult)
        link(dve.tensor_tensor(
            self.oh[:].rearrange("p k j e -> p (k j) e"),
            s.iota_e[:].unsqueeze(1).to_broadcast([P, TOPK * TPC, E]),
            self.idf[:].rearrange("p k j -> p (k j)").unsqueeze(2).to_broadcast([P, TOPK * TPC, E]), ALU.is_equal))
        dve.tensor_tensor(self.chosen[:], self.oh[:, 0], self.oh[:, 1], ALU.add).then_inc(self.chosen_ok, 1)
        link(dve.tensor_tensor(
            self.gt[:].rearrange("p k j e -> p (k j) e"), self.oh[:].rearrange("p k j e -> p (k j) e"),
            self.wt[:].rearrange("p k j -> p (k j)").unsqueeze(2).to_broadcast([P, TOPK * TPC, E]), ALU.mult))
        after(dve, self.gate_out, c * 16)
        dve.tensor_tensor(self.gate[:], self.gt[:, 0], self.gt[:, 1], ALU.add).then_inc(self.gate_ok, 1)

    def pe_rank(self, pe, c):
        s = self.s
        pe.wait_ge(self.chosen_ok, c + 1)
        after(pe, self.carried, c)
        self.wait_bank(pe, 5, c)
        n = TPC * E
        bank = self.bank(5)
        pe.matmul(bank[:, 0:n], s.earlier[:], self.chosen[:].rearrange("p j e -> p (j e)"), start=True, stop=False)
        for j in range(TPC - 1):
            pe.matmul(bank[:, (j + 1) * E:n].rearrange("p (j e) -> p j e", e=E), s.ones_bf[:],
                      self.chosen[:, j:j + 1, :].to_broadcast([P, TPC - 1 - j, E]),
                      start=False, stop=False, skip_group_check=True)
        pe.matmul(bank[:, 0:n].rearrange("p (j e) -> p j e", e=E), s.ones_bf[:],
                  s.carry[:].unsqueeze(1).to_broadcast([P, TPC, E]), start=False, stop=True).then_inc(self.ranked, 1)

    def dve_place(self, dve, c):
        def link(ins):
            self.links += 1
            ins.then_inc(self.chain, 1)
            dve.wait_ge(self.chain, c * self.CHAIN + self.links)

        s = self.s
        dve.wait_ge(self.ranked, c + 1)
        counts = self.bank(5)[:, 0:TPC * E].rearrange("p (j e) -> p j e", e=E)
        for k in range(TOPK):
            last = dve.tensor_tensor(self.rk[:, k], self.oh[:, k], counts, ALU.mult)
        last.then_inc(self.read[5], 1)
        dve.wait_ge(self.read[5], c + 1)
        with self.nc.allow_low_precision("counts up to TPC per partition, exact in bfloat16"):
            dve.tensor_reduce(self.taken[:], self.chosen[:].rearrange("p j e -> p e j"), AX.X, ALU.add)
        link(dve.tensor_reduce(self.rank[:].rearrange("p k j -> p (k j)"),
                               self.rk[:].rearrange("p k j e -> p (k j) e"), AX.X, ALU.add))
        dve.tensor_tensor(s.carry[:], s.carry[:], self.taken[:], ALU.add).then_inc(self.carried, 1)
        dve.tensor_scalar(self.over[:], self.rank[:], float(CAP), 1000.0, ALU.is_ge, ALU.mult)
        link(dve.tensor_copy(self.rank_i[:], self.rank[:]))
        dve.tensor_scalar(self.high[:], self.rank_i[:], 7, None, ALU.arith_shift_right)
        dve.scalar_tensor_tensor(self.tile1[:], self.idf[:], float(TPE), self.over[:], ALU.mult, ALU.add)
        link(dve.tensor_scalar(self.low[:], self.rank_i[:], P - 1, None, ALU.bitwise_and))
        dve.tensor_copy(self.lowf[:], self.low[:])
        link(dve.tensor_tensor(self.tilef[:], self.high[:], self.tile1[:], ALU.add))
        assert self.links == self.PLACED

    def dve_onehots(self, dve, c):
        s = self.s
        after(dve, self.listed, c)
        for j in range(TPC):
            dve.tensor_scalar(self.onehot_row[:, j, 0, :], s.iota_tile[:, 0:P], self.lowf[:, 0, j:j + 1],
                              None, ALU.is_equal)
            for k in range(TOPK):
                dve.tensor_scalar(self.onehot_tile[:, j, k, :], s.iota_tile[:], self.tilef[:, k, j:j + 1],
                                  s.token[:, j:j + 1], ALU.is_equal, ALU.mult).then_inc(self.onehots, 1)

    def pool_onehots(self, pool, c):
        pool.wait_ge(self.chain, c * self.CHAIN + self.PLACED)
        after(pool, self.listed, c)
        stand_alone(pool, self.s)
        for j in range(TPC):
            pool.tensor_scalar(self.onehot_row[:, j, 1, :], self.s.iota_tile[:, 0:P],
                               self.lowf[:, 1, j:j + 1], None, ALU.is_equal).then_inc(self.row_onehots, 1)

    def pe_list(self, pe, c):
        self.wait_bank(pe, 6, c)
        n = TPC * TOPK
        for i in range(n):
            j, k = i // TOPK, i % TOPK
            pe.wait_ge(self.onehots, c * n + i + 1)
            if k == 1:
                pe.wait_ge(self.row_onehots, c * TPC + j + 1)
            last = pe.matmul(self.bank(6)[:, 0:NST], self.onehot_row[:, j, k, :], self.onehot_tile[:, j, k, :],
                             start=(i == 0), stop=(i == n - 1))
        last.then_inc(self.listed, 1)

    def dve_list(self, dve, c):
        s = self.s
        dve.wait_ge(self.listed, c + 1)
        found = self.bank(6)[:, 0:NST]
        dve.tensor_scalar(self.taken_slot[:], found, 1.0, s.chunk_at[:, 0:1], ALU.min, ALU.mult)
        dve.tensor_tensor(s.slots[:], found, s.slots[:], ALU.add).then_inc(self.read[6], 1)
        dve.wait_ge(self.read[6], c + 1)
        dve.tensor_scalar(s.chunk_at[:], s.chunk_at[:], float(SEQ), None, ALU.add)
        self.links += 1
        dve.tensor_tensor(s.slots[:], s.slots[:], self.taken_slot[:], ALU.add).then_inc(self.chain, 1)
        dve.wait_ge(self.chain, c * self.CHAIN + self.CHAIN)
        assert self.links == self.CHAIN, self.links

    def dve_finish(self, dve, scratch):
        s = self.s
        tok, gat, emp = scratch
        base = CHUNKS * self.CHAIN
        n = 0

        def link(ins):
            nonlocal n
            n += 1
            ins.then_inc(self.chain, 1)
            dve.wait_ge(self.chain, base + n)

        dve.tensor_scalar(gat[:], s.slots[:], -1.0, 0.0, ALU.add, ALU.max)
        link(dve.scalar_tensor_tensor(emp[:], s.slots[:], 0.0, s.spare[:], ALU.is_equal, ALU.mult))
        dve.tensor_copy(s.gather_idx[:], gat[:])
        link(dve.scalar_tensor_tensor(tok[:], s.slots[:], -1.0, emp[:], ALU.add, ALU.add))
        dve.tensor_copy(s.scatter_idx[:], tok[:])
        dve.memset(s.carry[:], 0.0)
        dve.memset(s.chunk_at[:], 0.0)
        link(dve.memset(s.slots[:], 0.0))


def route_phase(nc, s, name, source, stream):
    with ExitStack() as ctx:
        r = Router(nc, ctx, s, name, source, banks=list(range(7)))
        scratch = [ctx.enter_context(nc.sbuf_tensor(f"{name}_fin{i}", [P, NST], F32)) for i in range(3)]
        stream_init = ctx.enter_context(nc.semaphore(f"{name}_stream_init"))
        end = CHUNKS - 1

        def there(c, n):
            return not isinstance(c, int) or c + n <= end

        def chunks(eng, step):
            step(0)
            with eng.Fori(1, end - 1) as c:
                step(c)
            step(end - 1)
            step(end)

        with nc.Block() as block:
            @block.sync
            def _(sp):
                def step(c):
                    if there(c, 1):
                        r.store_rows(sp, c + 1)
                    if there(c, 2):
                        r.load(sp, c + 2)
                    r.store_gates(sp, c)

                r.load(sp, 0)
                r.store_rows(sp, 0)
                r.load(sp, 1)
                sp.dma_start(stream[0:T, :], source[:, :]).then_inc(stream_init, 16)
                chunks(sp, step)
                sp.wait_ge(stream_init, 16)
                sp.wait_ge(r.xn_out, 16 * CHUNKS)
                sp.wait_ge(r.gate_out, 16 * CHUNKS)

            @block.gpsimd
            def _(pool):
                def step(c):
                    if there(c, 2):
                        r.pool_scale(pool, c + 2)
                    r.pool_onehots(pool, c)

                r.pool_scale(pool, 0)
                r.pool_scale(pool, 1)
                chunks(pool, step)

            @block.scalar
            def _(act):
                def step(c):
                    r.act_exp(act, c)
                    if there(c, 1):
                        r.act_turn(act, c + 1)
                    if there(c, 2):
                        r.act_norm(act, c + 2)

                r.act_norm(act, 0)
                r.act_turn(act, 0)
                r.act_norm(act, 1)
                chunks(act, step)

            @block.vector
            def _(dve):
                def step(c):
                    r.dve_choose(dve, c)
                    if there(c, 2):
                        r.dve_stats(dve, c + 2)
                    r.dve_place(dve, c)
                    r.dve_onehots(dve, c)
                    r.dve_list(dve, c)

                r.dve_stats(dve, 0)
                r.dve_stats(dve, 1)
                chunks(dve, step)
                r.dve_finish(dve, scratch)

            @block.tensor
            def _(pe):
                def step(c):
                    if there(c, 1):
                        r.pe_turn(pe, c + 1)
                    r.pe_rank(pe, c)
                    if there(c, 1):
                        r.pe_logits(pe, c + 1)
                    r.pe_list(pe, c)

                r.pe_turn(pe, 0)
                r.pe_logits(pe, 0)
                chunks(pe, step)


def expert_phase(nc, s, name, stream):
    with ExitStack() as ctx:
        def sb(n, shape, dt):
            return ctx.enter_context(nc.sbuf_tensor(f"{name}_{n}", shape, dt))

        def sem(n):
            return s.sems.enter_context(nc.semaphore(f"{name}_{n}"))

        raw1 = [sb(f"raw1_{i}", [P, DC, FF], F32) for i in range(2)]
        raw2 = [sb(f"raw2_{i}", [P, FC, D], F32) for i in range(2)]
        w1h = [sb(f"w1h{i}", [P, DC, FF], F32R) for i in range(2)]
        w1l = [sb(f"w1l{i}", [P, DC, FF], F32R) for i in range(2)]
        w2h = [sb(f"w2h{i}", [P, FC, D], F32R) for i in range(2)]
        w2l = [sb(f"w2l{i}", [P, FC, D], F32R) for i in range(2)]
        xg = [sb(f"xg{i}", [P, GRP, ROW], F32) for i in range(NXG)]
        xh = [sb(f"xh{i}", [P, DC, GT], F32R) for i in range(2)]
        xl = [sb(f"xl{i}", [P, DC, GT], F32R) for i in range(2)]
        h = [sb(f"h{i}", [P, FC, GT], F32) for i in range(2)]
        hh = [sb(f"hh{i}", [P, FC, GT], F32R) for i in range(2)]
        hl = [sb(f"hl{i}", [P, FC, GT], F32R) for i in range(2)]
        yo = [sb(f"yo{i}", [P, GRP, D], F32) for i in range(NYO)]
        half = GPE * GRP
        gidx = [sb(f"gidx{i}", [P, half], U32) for i in range(2)]
        sidx = [sb(f"sidx{i}", [P, half], U32) for i in range(2)]

        w_in = [sem(f"w_in{i}") for i in range(2)]
        w_split = sem("w_split")
        gathered = [sem(f"gathered{i}") for i in range(NXG)]
        gidx_ok = sem("gidx_ok")
        sidx_ok = sem("sidx_ok")
        turned = sem("turned")
        x_hi = sem("x_hi")
        x_lo = sem("x_lo")
        up = sem("up")
        act_h = sem("act_h")
        h_hi = sem("h_hi")
        h_lo = sem("h_lo")
        down = sem("down")
        weighted = sem("weighted")
        scattered = [sem(f"scattered{i}") for i in range(NYO)]

        psum = s.psum
        px = [psum[:, i * BANK:(i + 1) * BANK] for i in (0, 1)]
        ph = [psum[:, (2 + 2 * i) * BANK:(4 + 2 * i) * BANK] for i in (0, 1)]
        po = [psum[:, i * BANK:(i + 1) * BANK] for i in (6, 7)]
        end = NPAIR - 1

        def ahead(i, j, n, part):
            if j + n < PAIR:
                part(i, j + n)
            elif i is not end:
                part(i + 1, j + n - PAIR)

        with nc.Block() as block:
            @block.sync
            def _(sp):
                def load(e, p):
                    after(sp, w_split, e * 4 - 4)
                    w1 = s.w1[bass.ds(e * D, D), :].rearrange("(c p) f -> p c f", p=P)
                    w2 = s.w2[bass.ds(e * FF, FF), :].rearrange("(c p) d -> p c d", p=P)
                    sp.dma_start(raw1[p][:], w1).then_inc(w_in[p], 16)
                    sp.dma_start(raw2[p][:], w2).then_inc(w_in[p], 16)

                def step(i):
                    load(i * 2, 0)
                    load(i * 2 + 1, 1)

                load(0, 0)
                load(1, 1)
                with sp.Fori(1, NPAIR) as i:
                    step(i)

            @block.gpsimd
            def _(pool):
                def gather(i, j):
                    b = j % NXG
                    after(pool, weighted, (i * PAIR + j + 1 - NXG) * GRP)
                    stand_alone(pool, s)
                    for t in range(GRP):
                        k = (j % GPE) * GRP + t
                        pool.indirect_dma_start(
                            xg[b][:, t, :], None, s.rows[:, :],
                            bass.IndirectOffsetOnAxis(gidx[j // GPE][:, k:k + 1], axis=0),
                        ).then_inc(gathered[b], 16)

                def scatter(i, j):
                    b = j % NYO
                    pool.wait_ge(weighted, (i * PAIR + j + 1) * GRP)
                    stand_alone(pool, s)
                    for t in range(GRP):
                        k = (j % GPE) * GRP + t
                        pool.indirect_dma_start(
                            stream[:, :],
                            bass.IndirectOffsetOnAxis(sidx[j // GPE][:, k:k + 1], axis=0),
                            yo[b][:, t, :], None, compute_op=ALU.add,
                        ).then_inc(scattered[b], 16)

                def gather_columns(i, w):
                    for q in gathered[w * GPE:(w + 1) * GPE]:
                        after(pool, q, i * 16 * GRP)
                    pool.tensor_copy(gidx[w][:], s.gather_idx[:, bass.ds((i * 2 + w) * half, half)]).then_inc(gidx_ok, 1)
                    pool.wait_ge(gidx_ok, i * 2 + w + 1)

                def scatter_columns(i, w):
                    for q in scattered:
                        after(pool, q, (i * 2 + w) * 16 * GRP)
                    pool.tensor_copy(sidx[w][:], s.scatter_idx[:, bass.ds((i * 2 + w) * half, half)]).then_inc(sidx_ok, 1)
                    pool.wait_ge(sidx_ok, i * 2 + w + 1)

                def body(i):
                    for j in range(PAIR):
                        if (j + AHEAD) % PAIR == GPE and (i is not end or j + AHEAD < PAIR):
                            gather_columns(i + (j + AHEAD) // PAIR, 1)
                        if (j + AHEAD) % PAIR == 0 and i is not end:
                            gather_columns(i + 1, 0)
                        ahead(i, j, AHEAD, gather)
                        if j % GPE == 0:
                            scatter_columns(i, j // GPE)
                        scatter(i, j)

                gather_columns(0, 0)
                for j in range(AHEAD):
                    if j == GPE:
                        gather_columns(0, 1)
                    gather(0, j)
                in_turn(pool, 0, end, body)
                for q in scattered:
                    pool.wait_ge(q, E * 16 * GRP)

            @block.tensor
            def _(pe):
                def turn(i, j):
                    b = j % NXG
                    pe.wait_ge(gathered[b], (i + 1) * 16 * GRP)
                    after(pe, x_lo, i * PAIR + j - 1)
                    for k in range(DC * GRP):
                        d, t = k // GRP, k % GRP
                        last = pe.transpose(px[j % 2][:, k * P:(k + 1) * P], xg[b][:, t, d * P:(d + 1) * P],
                                            s.ident[:])
                    last.then_inc(turned, 1)

                def mm_up(i, j):
                    p, w = j % 2, j // GPE
                    pe.wait_ge(x_lo, i * PAIR + j + 1)
                    if j % GPE == 0:
                        pe.wait_ge(w_split, (i * 2 + w) * 4 + 2)
                    for f in range(FC):
                        if f % 2 == 0:
                            after(pe, act_h, (i * PAIR + j - 2) * 2 + f // 2 + 1)
                        out = ph[p][:, f * GT:(f + 1) * GT]
                        n = 0
                        for a, b in ((w1h, xh), (w1h, xl), (w1l, xh)):
                            for d in range(DC):
                                last = pe.matmul(out, a[w][:, d, f * P:(f + 1) * P], b[p][:, d, :],
                                                 start=(n == 0), stop=(n == 3 * DC - 1))
                                n += 1
                        if f % 2:
                            last.then_inc(up, 1)

                def mm_down(i, j):
                    p, w = j % 2, j // GPE
                    pe.wait_ge(h_lo, (i * PAIR + j + 1) * 2)
                    after(pe, weighted, (i * PAIR + j - 1) * GRP)
                    if j % GPE == 0:
                        pe.wait_ge(w_split, (i * 2 + w) * 4 + 4)
                    for t in range(GRP):
                        out = po[p][:, t * D:(t + 1) * D]
                        n = 0
                        for f in range(FC):
                            for a, b in ((hh, w2h), (hh, w2l), (hl, w2h)):
                                last = pe.matmul(out, a[p][:, f, t * P:(t + 1) * P], b[w][:, f, :],
                                                 start=(n == 0), stop=(n == 3 * FC - 1))
                                n += 1
                    last.then_inc(down, 1)

                def body(i):
                    for j in range(PAIR):
                        ahead(i, j, 2, turn)
                        ahead(i, j, 1, mm_up)
                        mm_down(i, j)

                turn(0, 0)
                turn(0, 1)
                mm_up(0, 0)
                in_turn(pe, 0, end, body)

            @block.scalar
            def _(act):
                def x_high(i, j):
                    act.wait_ge(turned, i * PAIR + j + 1)
                    after(act, up, (i * PAIR + j - 1) * 2)
                    act.activation(xh[j % 2][:], px[j % 2].rearrange("p (d t) -> p d t", d=DC),
                                   ACT.Copy).then_inc(x_hi, 1)

                def gelu(i, j):
                    p = j % 2
                    for q in range(2):
                        act.wait_ge(up, (i * PAIR + j) * 2 + q + 1)
                        after(act, h_lo, (i * PAIR + j - 2) * 2 + q + 1)
                        act.activation(h[p][:, 2 * q:2 * q + 2, :],
                                       ph[p][:, q * BANK:(q + 1) * BANK].rearrange("p (f t) -> p f t", f=2),
                                       ACT.Gelu).then_inc(act_h, 1)

                def weight(i, j):
                    b, y, w = j % NXG, j % NYO, j // GPE
                    act.wait_ge(down, i * PAIR + j + 1)
                    after(act, scattered[y], (i * 2 + j // NYO) * 16 * GRP)
                    for t in range(GRP):
                        act.activation(yo[y][:, t, :], po[j % 2][:, t * D:(t + 1) * D], ACT.Copy,
                                       scale=xg[b][:, t, bass.ds(i * 2 + D + w, 1)]).then_inc(weighted, 1)

                def body(i):
                    for j in range(PAIR):
                        ahead(i, j, 2, x_high)
                        ahead(i, j, 1, gelu)
                        weight(i, j)

                x_high(0, 0)
                x_high(0, 1)
                gelu(0, 0)
                in_turn(act, 0, end, body)

            @block.vector
            def _(dve):
                def x_low(i, j):
                    dve.wait_ge(x_hi, i * PAIR + j + 1)
                    dve.tensor_tensor(xl[j % 2][:].rearrange("p d t -> p (d t)"), px[j % 2],
                                      xh[j % 2][:].bitcast(F32).rearrange("p d t -> p (d t)"),
                                      ALU.subtract).then_inc(x_lo, 1)

                def split_h(i, j):
                    p = j % 2
                    after(dve, down, i * PAIR + j - 1)
                    for q in range(2):
                        rows = slice(2 * q, 2 * q + 2)
                        dve.wait_ge(act_h, (i * PAIR + j) * 2 + q + 1)
                        dve.tensor_copy(hh[p][:, rows, :], h[p][:, rows, :]).then_inc(h_hi, 1)
                        dve.wait_ge(h_hi, (i * PAIR + j) * 2 + q + 1)
                        dve.tensor_tensor(hl[p][:, rows, :], h[p][:, rows, :], hh[p][:, rows, :].bitcast(F32),
                                          ALU.subtract).then_inc(h_lo, 1)

                def split_w(i, w, part):
                    if part == 0:
                        dve.wait_ge(w_in[w], i * 32 + 32)
                        after(dve, down, (i * 2 + w - 1) * GPE)
                    raw, hi, lo = ((raw1, w1h, w1l), (raw2, w2h, w2l))[part // 2]
                    if part % 2 == 0:
                        dve.tensor_copy(hi[w][:], raw[w][:]).then_inc(w_split, 1)
                    else:
                        dve.wait_ge(w_split, (i * 2 + w) * 4 + part)
                        dve.tensor_tensor(lo[w][:], raw[w][:], hi[w][:].bitcast(F32),
                                          ALU.subtract).then_inc(w_split, 1)

                def body(i):
                    for j in range(PAIR):
                        ahead(i, j, 2, x_low)
                        ahead(i, j, 1, split_h)
                        part = j % GPE - 1
                        if part >= 0 and j < GPE:
                            split_w(i, 1, part)
                        elif part >= 0 and i is not end:
                            split_w(i + 1, 0, part)

                for part in range(4):
                    split_w(0, 0, part)
                x_low(0, 0)
                x_low(0, 1)
                split_h(0, 0)
                in_turn(dve, 0, end, body)


def attention_phase(nc, s, name):
    with ExitStack() as ctx:
        def sb(n, shape, dt):
            return ctx.enter_context(nc.sbuf_tensor(f"{name}_{n}", shape, dt))

        def sem(n):
            return s.sems.enter_context(nc.semaphore(f"{name}_{n}"))

        r = Router(nc, ctx, s, f"{name}_route", s.out, banks=[7])
        xa = sb("xa", [P, TPC, D], F32)
        stats = sb("stats", [P, TPC, 6], F32)
        mv = sb("mv", [P, TPC, 2], F32)
        vareps = sb("vareps", [P, TPC], F32)
        rstd = sb("rstd", [P, TPC], F32)
        shift = sb("shift", [P, TPC], F32)
        xTh = sb("xTh", [P, DC, SEQ], F32R)
        xTl = sb("xTl", [P, DC, SEQ], F32R)
        wh = sb("wh", [P, DC, 3 * D], F32R)
        wl = sb("wl", [P, DC, 3 * D], F32R)
        bqk = sb("bqk", [P, 2 * DC], F32)
        bv = sb("bv", [P, 2, D], F32)
        full = [sb(f"full{i}", [P, BANK], F32) for i in range(2)]
        qkh = sb("qkh", [P, 2 * DC, SEQ], F32R)
        qkl = sb("qkl", [P, 2 * DC, SEQ], F32R)
        vh = sb("vh", [P, TPC, D], F32R)
        vl = sb("vl", [P, TPC, D], F32R)
        prob = [sb(f"prob{i}", [P, SEQ], F32) for i in range(2)]
        pTh = [sb(f"pTh{i}", [P, TPC, P], F32R) for i in range(2)]
        pTl = [sb(f"pTl{i}", [P, TPC, P], F32R) for i in range(2)]
        negmax = sb("negmax", [P, TPC], F32)
        rsum = sb("rsum", [P, TPC], F32)
        rinv = sb("rinv", [P, TPC], F32)
        xr = [sb(f"xr{i}", [P, D], F32) for i in range(2)]
        x2 = [sb(f"x2_{i}", [P, D], F32) for i in range(2)]
        raw_w = sb("raw_w", [P, DC, 3 * D], F32)
        scratch = [sb(f"fin{i}", [P, NST], F32) for i in range(3)]

        w_in = sem("w_in")
        w_ok = sem("w_ok")
        xa_in = sem("xa_in")
        stat = sem("stat")
        meanvar = sem("meanvar")
        scaled = sem("scaled")
        normed = sem("normed")
        turned = sem("turned")
        turned_hi = sem("turned_hi")
        turned_lo = sem("turned_lo")
        projected = sem("projected")
        qk_full = sem("qk_full")
        v_full = sem("v_full")
        split_hi = sem("split_hi")
        split_lo = sem("split_lo")
        scored = sem("scored")
        maxed = sem("maxed")
        exped = sem("exped")
        inverted = sem("inverted")
        mixed = sem("mixed")
        summed = sem("summed")
        xr_in = [sem(f"xr_in{i}") for i in range(2)]
        x2_out = [sem(f"x2_out{i}") for i in range(2)]

        psum = s.psum
        bank = [psum[:, i * BANK:(i + 1) * BANK] for i in range(8)]
        score = [psum[:, 2 * i * BANK:2 * (i + 1) * BANK] for i in range(2)]
        tp = bank[4:6]
        po = bank[6]
        end = BATCH - 1

        PROJ_QK, PROJ_V = 2 * DC * 2, TPC // 2
        PROJ = PROJ_QK + PROJ_V
        XT = TPC // 2
        XT_STEP = 5
        PT = [(i + 4) // 4 for i in range(TPC)]
        TURNS = sum(PT) + XT

        def pt_first(b, i):
            n = sum(PT[:i])
            if b is not end and i > XT_STEP:
                n += XT
            return b * TURNS + XT + n

        def xt_first(b):
            return (b - 1) * TURNS + XT + sum(PT[:XT_STEP + 1]) if not (isinstance(b, int) and b == 0) else 0

        def parity(b, i, k):
            assert TURNS % 2 == 0 and XT % 2 == 0
            return (sum(PT[:i]) + k) % 2

        xt_parity = sum(PT[:XT_STEP + 1]) % 2
        assert xt_parity == 0

        def bodies(eng, body):
            body(0)
            body(1)
            with eng.Fori(2, end) as b:
                body(b)
            body(end)

        def routed(b):
            return not (isinstance(b, int) and b == 0)

        with nc.Block() as block:
            @block.sync
            def _(sp):
                def load_xa(b):
                    after(sp, projected, (b - 1) * PROJ + PROJ_QK)
                    src = s.x1[bass.ds(b * SEQ, SEQ), :]
                    sp.dma_start(xa[:], src.rearrange("(j p) d -> p j d", p=P)).then_inc(xa_in, 16)

                def load_xr(b, i):
                    after(sp, summed, b * TPC + i - 1)
                    sp.dma_start(xr[i % 2][:], s.x1[bass.ds(b * SEQ + i * P, P), :]).then_inc(xr_in[i % 2], 16)

                def body(b):
                    load_xr(b, 0)
                    load_xr(b, 1)
                    if routed(b):
                        for q in x2_out:
                            sp.wait_ge(q, b * (TPC // 2) * 16)
                        r.load(sp, b - 1)
                    if b is not end:
                        load_xa(b + 1)
                    for i in range(TPC):
                        sp.wait_ge(summed, b * TPC + i + 1)
                        sp.dma_start(s.out[bass.ds(b * SEQ + i * P, P), :], x2[i % 2][:]).then_inc(x2_out[i % 2], 16)
                        if i + 2 < TPC:
                            load_xr(b, i + 2)
                        if routed(b) and i == 2:
                            r.store_rows(sp, b - 1)
                        if routed(b) and i == 5:
                            r.store_gates(sp, b - 1)

                load_xa(0)
                sp.dma_start(raw_w[:], s.wqkvT.rearrange("(c p) e -> p c e", p=P)).then_inc(w_in, 16)
                with nc.allow_non_contiguous_dma("a bias per partition, once"):
                    sp.dma_start(bqk[:], s.bqkv[0:2 * D].rearrange("(m p) -> p m", p=P)).then_inc(w_in, 16)
                for t in range(2):
                    sp.dma_start(bv[:, t, :], s.bqkv[2 * D:3 * D].partition_broadcast(P)).then_inc(w_in, 16)
                bodies(sp, body)
                for q in x2_out:
                    sp.wait_ge(q, BATCH * (TPC // 2) * 16)
                r.load(sp, end)
                r.store_rows(sp, end)
                r.store_gates(sp, end)
                sp.wait_ge(r.xn_out, 16 * CHUNKS)
                sp.wait_ge(r.gate_out, 16 * CHUNKS)

            @block.gpsimd
            def _(pool):
                def scale(b):
                    pool.wait_ge(meanvar, b + 1)
                    norm_factors(pool, s, mv, vareps, rstd, shift, scaled, b)

                def body(b):
                    if routed(b):
                        r.pool_scale(pool, b - 1)
                    if b is not end:
                        scale(b + 1)
                    if routed(b):
                        r.pool_onehots(pool, b - 1)

                scale(0)
                bodies(pool, body)
                r.pool_scale(pool, end)
                r.pool_onehots(pool, end)

            @block.tensor
            def _(pe):
                def turn_x(b):
                    for u in range(XT):
                        pe.wait_ge(normed, b * TPC + 2 * u + 2)
                        after(pe, turned_lo, xt_first(b) + u - 1)
                        out = tp[(xt_parity + u) % 2]
                        for k in range(4):
                            d, j = k // 2, 2 * u + k % 2
                            last = pe.transpose(out[:, k * P:(k + 1) * P], xa[:, j, d * P:(d + 1) * P], s.ident[:])
                        last.then_inc(turned, 1)

                def split_product(out, stat, mov, extra=None):
                    n, total = 0, 3 * len(stat)
                    for a, b in zip(stat, mov):
                        for x, y in ((0, 0), (0, 1), (1, 0)):
                            last = pe.matmul(out, a[x], b[y], start=(n == 0), stop=(n == total - 1))
                            if n == 0 and extra is not None:
                                pe.matmul(*extra, start=False, stop=False, skip_group_check=True)
                            n += 1
                    return last

                def qk(b):
                    pe.wait_ge(turned_lo, xt_first(b) + XT)
                    after(pe, exped, b * TPC - 1)
                    for u in range(PROJ_QK):
                        m, t = u // 2, u % 2
                        if u >= 2:
                            pe.wait_ge(qk_full, b * PROJ_QK + u - 1)
                        cols = slice(t * BANK, (t + 1) * BANK)
                        split_product(bank[u % 2],
                                      [(wh[:, d, m * P:(m + 1) * P], wl[:, d, m * P:(m + 1) * P]) for d in range(DC)],
                                      [(xTh[:, d, cols], xTl[:, d, cols]) for d in range(DC)]).then_inc(projected, 1)

                def v(b):
                    for u in range(PROJ_V):
                        if u < 2:
                            pe.wait_ge(qk_full, b * PROJ_QK + PROJ_QK)
                        else:
                            pe.wait_ge(v_full, b * PROJ_V + u - 1)
                        for k in range(2):
                            t = slice((2 * u + k) * P, (2 * u + k + 1) * P)
                            last = split_product(bank[u % 2][:, k * D:(k + 1) * D],
                                                 [(xTh[:, d, t], xTl[:, d, t]) for d in range(DC)],
                                                 [(wh[:, d, 2 * D:3 * D], wl[:, d, 2 * D:3 * D]) for d in range(DC)])
                        last.then_inc(projected, 1)

                def scores(b, i):
                    if i == 0:
                        pe.wait_ge(v_full, b * PROJ_V + PROJ_V)
                        pe.wait_ge(split_lo, b * PROJ + PROJ_QK)
                    after(pe, exped, b * TPC + i - 1)
                    q = slice(i * P, (i + 1) * P)
                    n = (i + 1) * P
                    for c in range(0, n, BANK):
                        w = min(BANK, n - c)
                        diagonal = (score[i % 2][:, n - P:n], s.ident_bf[:], s.causal[:]) if c + w == n else None
                        last = split_product(score[i % 2][:, c:c + w],
                                             [(qkh[:, d, q], qkl[:, d, q]) for d in range(DC)],
                                             [(qkh[:, DC + d, c:c + w], qkl[:, DC + d, c:c + w]) for d in range(DC)],
                                             extra=diagonal)
                    last.then_inc(scored, 1)

                def turn_p(b, i):
                    pe.wait_ge(exped, b * TPC + i + 1)
                    for u in range(PT[i]):
                        after(pe, turned_lo, pt_first(b, i) + u - 1)
                        out = tp[parity(b, i, u)]
                        for k in range(4 * u, min(4 * u + 4, i + 1)):
                            last = pe.transpose(out[:, (k % 4) * P:(k % 4 + 1) * P],
                                                prob[i % 2][:, k * P:(k + 1) * P], s.ident[:])
                        last.then_inc(turned, 1)

                def mix(b, i):
                    if i == 0:
                        pe.wait_ge(split_lo, b * PROJ + PROJ)
                    pe.wait_ge(turned_lo, pt_first(b, i) + PT[i])
                    after(pe, summed, b * TPC + i)
                    split_product(po[:, 0:D], [(pTh[i % 2][:, k, :], pTl[i % 2][:, k, :]) for k in range(i + 1)],
                                  [(vh[:, k, :], vl[:, k, :]) for k in range(i + 1)]).then_inc(mixed, 1)

                def body(b):
                    v(b)
                    scores(b, 0)
                    scores(b, 1)
                    for i in range(TPC):
                        turn_p(b, i)
                        if i + 2 < TPC:
                            scores(b, i + 2)
                        if i == XT_STEP and b is not end:
                            turn_x(b + 1)
                        if routed(b):
                            if i == 3:
                                r.pe_turn(pe, b - 1)
                            if i == 4:
                                r.pe_logits(pe, b - 1)
                            if i == 6:
                                r.pe_rank(pe, b - 1)
                            if i == 7:
                                r.pe_list(pe, b - 1)
                        if i == TPC - 1 and b is not end:
                            qk(b + 1)
                        mix(b, i)

                pe.wait_ge(w_ok, 3)
                turn_x(0)
                qk(0)
                bodies(pe, body)
                r.pe_turn(pe, end)
                r.pe_logits(pe, end)
                r.pe_rank(pe, end)
                r.pe_list(pe, end)

            @block.scalar
            def _(act):
                def norm(b):
                    act.wait_ge(scaled, b * NORM_STEPS + NORM_STEPS)
                    for j in range(TPC):
                        act.activation(xa[:, j, :], xa[:, j, :], ACT.Identity, bias=shift[:, j:j + 1],
                                       scale=rstd[:, j:j + 1]).then_inc(normed, 1)

                def high_x(b):
                    after(act, projected, b * PROJ)
                    for u in range(XT):
                        act.wait_ge(turned, xt_first(b) + u + 1)
                        act.activation(xTh[:, :, 2 * u * P:(2 * u + 2) * P],
                                       tp[(xt_parity + u) % 2].rearrange("p (d t) -> p d t", d=DC),
                                       ACT.Copy).then_inc(turned_hi, 1)

                def qk_bias(b):
                    for u in range(PROJ_QK):
                        m = u // 2
                        act.wait_ge(projected, b * PROJ + u + 1)
                        after(act, split_lo, b * PROJ + u - 1 if u >= 2 else b * PROJ)
                        act.activation(full[u % 2][:], bank[u % 2], ACT.Identity, bias=bqk[:, m:m + 1],
                                       scale=SCALE if m < DC else 1.0).then_inc(qk_full, 1)

                def exp(b, i):
                    act.wait_ge(maxed, b * TPC + i + 1)
                    if i >= 2:
                        act.wait_ge(turned, pt_first(b, i - 2) + PT[i - 2])
                    n = (i + 1) * P
                    act.activation(prob[i % 2][:, 0:n], score[i % 2][:, 0:n], ACT.Exp, bias=negmax[:, i:i + 1],
                                   scale=1.0, accum_out=rsum[:, i:i + 1]).then_inc(exped, 1)

                def high_p(b, i):
                    after(act, mixed, b * TPC + i - 1)
                    for u in range(PT[i]):
                        act.wait_ge(turned, pt_first(b, i) + u + 1)
                        w = min(4, i + 1 - 4 * u)
                        act.activation(pTh[i % 2][:, 4 * u:4 * u + w, :],
                                       tp[parity(b, i, u)][:, 0:w * P].rearrange("p (k q) -> p k q", q=P),
                                       ACT.Copy).then_inc(turned_hi, 1)

                def body(b):
                    exp(b, 0)
                    exp(b, 1)
                    for i in range(TPC):
                        high_p(b, i)
                        if i + 2 < TPC:
                            exp(b, i + 2)
                        if i == 3 and b is not end:
                            norm(b + 1)
                        if i == XT_STEP and b is not end:
                            high_x(b + 1)
                        if routed(b):
                            if i == 2:
                                r.act_norm(act, b - 1)
                            if i == 3:
                                r.act_turn(act, b - 1)
                            if i == 4:
                                r.act_exp(act, b - 1)
                        if i == TPC - 1 and b is not end:
                            qk_bias(b + 1)

                norm(0)
                high_x(0)
                act.wait_ge(w_ok, 3)
                qk_bias(0)
                bodies(act, body)
                r.act_norm(act, end)
                r.act_turn(act, end)
                r.act_exp(act, end)

            @block.vector
            def _(dve):
                def norm_stats(b):
                    dve.wait_ge(xa_in, b * 16 + 16)
                    for j in range(TPC):
                        last = dve.bn_stats(stats[:, j, :], xa[:, j, :])
                    last.then_inc(stat, 1)
                    dve.wait_ge(stat, b + 1)
                    after(dve, normed, b * TPC)
                    stand_alone(dve, s)
                    for j in range(TPC):
                        last = dve.bn_aggr(mv[:, j, :], stats[:, j, :])
                    last.then_inc(meanvar, 1)

                def low_x(b):
                    for u in range(XT):
                        dve.wait_ge(turned_hi, xt_first(b) + u + 1)
                        cols = slice(2 * u * P, (2 * u + 2) * P)
                        dve.tensor_tensor(xTl[:, :, cols],
                                          tp[(xt_parity + u) % 2].rearrange("p (d t) -> p d t", d=DC),
                                          xTh[:, :, cols].bitcast(F32), ALU.subtract).then_inc(turned_lo, 1)

                def split(b, u, hi, lo, src):
                    dve.tensor_copy(hi, src).then_inc(split_hi, 1)
                    dve.wait_ge(split_hi, b * PROJ + u + 1)
                    dve.tensor_tensor(lo, src, hi.bitcast(F32), ALU.subtract).then_inc(split_lo, 1)

                def split_qk(b):
                    after(dve, scored, b * TPC)
                    for u in range(PROJ_QK):
                        dve.wait_ge(qk_full, b * PROJ_QK + u + 1)
                        m, cols = u // 2, slice((u % 2) * BANK, (u % 2 + 1) * BANK)
                        split(b, u, qkh[:, m, cols], qkl[:, m, cols], full[u % 2][:])

                def split_v(b):
                    after(dve, mixed, b * TPC)
                    for u in range(PROJ_V):
                        dve.wait_ge(projected, b * PROJ + PROJ_QK + u + 1)
                        dve.wait_ge(split_lo, b * PROJ + PROJ_QK + u)
                        dve.tensor_tensor(full[u % 2][:], bank[u % 2], bv[:].rearrange("p t d -> p (t d)"),
                                          ALU.add).then_inc(v_full, 1)
                        dve.wait_ge(v_full, b * PROJ_V + u + 1)
                        tiles = slice(2 * u, 2 * u + 2)
                        split(b, PROJ_QK + u, vh[:, tiles, :], vl[:, tiles, :],
                              full[u % 2][:].rearrange("p (t d) -> p t d", d=D))

                def maximum(b, i):
                    dve.wait_ge(scored, b * TPC + i + 1)
                    dve.tensor_reduce(negmax[:, i:i + 1], score[i % 2][:, 0:(i + 1) * P], AX.X, ALU.max,
                                      negate=True).then_inc(maxed, 1)

                def low_p(b, i):
                    for u in range(PT[i]):
                        dve.wait_ge(turned_hi, pt_first(b, i) + u + 1)
                        w = min(4, i + 1 - 4 * u)
                        dve.tensor_tensor(pTl[i % 2][:, 4 * u:4 * u + w, :],
                                          tp[parity(b, i, u)][:, 0:w * P].rearrange("p (k q) -> p k q", q=P),
                                          pTh[i % 2][:, 4 * u:4 * u + w, :].bitcast(F32),
                                          ALU.subtract).then_inc(turned_lo, 1)

                def residual(b, i):
                    dve.wait_ge(exped, b * TPC + i + 1)
                    dve.reciprocal(rinv[:, i:i + 1], rsum[:, i:i + 1]).then_inc(inverted, 1)
                    dve.wait_ge(inverted, b * TPC + i + 1)
                    dve.wait_ge(xr_in[i % 2], b * (TPC // 2) * 16 + (i // 2 + 1) * 16)
                    after(dve, x2_out[i % 2], b * (TPC // 2) * 16 + (i // 2) * 16)
                    dve.wait_ge(mixed, b * TPC + i + 1)
                    dve.scalar_tensor_tensor(x2[i % 2][:], po[:, 0:D], rinv[:, i:i + 1], xr[i % 2][:],
                                             ALU.mult, ALU.add).then_inc(summed, 1)

                def body(b):
                    split_v(b)
                    maximum(b, 0)
                    maximum(b, 1)
                    for i in range(TPC):
                        low_p(b, i)
                        if i + 2 < TPC:
                            maximum(b, i + 2)
                        if i == 2 and b is not end:
                            norm_stats(b + 1)
                        if i == XT_STEP and b is not end:
                            low_x(b + 1)
                        if routed(b):
                            if i == 1:
                                r.dve_stats(dve, b - 1)
                            if i == 5:
                                r.dve_choose(dve, b - 1)
                            if i == 6:
                                r.dve_place(dve, b - 1)
                                r.dve_onehots(dve, b - 1)
                            if i == 7:
                                r.dve_list(dve, b - 1)
                        if i == TPC - 1 and b is not end:
                            split_qk(b + 1)
                        residual(b, i)

                dve.wait_ge(w_in, 16 * 4)
                dve.tensor_scalar(bqk[:, 0:DC], bqk[:, 0:DC], SCALE, None, ALU.mult).then_inc(w_ok, 1)
                dve.tensor_copy(wh[:], raw_w[:]).then_inc(w_ok, 1)
                dve.wait_ge(w_ok, 2)
                dve.tensor_tensor(wl[:], raw_w[:], wh[:].bitcast(F32), ALU.subtract).then_inc(w_ok, 1)
                norm_stats(0)
                low_x(0)
                split_qk(0)
                bodies(dve, body)
                r.dve_stats(dve, end)
                r.dve_choose(dve, end)
                r.dve_place(dve, end)
                r.dve_onehots(dve, end)
                r.dve_list(dve, end)
                r.dve_finish(dve, scratch)


def macaron(nc, x, wqkvT, bqkv, gate_wT, w1, w2, rows, x1, out):
    s = Shared()
    s.x, s.wqkvT, s.bqkv, s.w1, s.w2, s.rows, s.x1, s.out = x, wqkvT, bqkv, w1, w2, rows, x1, out
    with ExitStack() as ctx:
        s.sems = ctx
        setup_constants(nc, ctx, s, gate_wT)
        route_phase(nc, s, "r1", s.x, s.x1)
        expert_phase(nc, s, "m1", s.x1)
        attention_phase(nc, s, "at")
        expert_phase(nc, s, "m2", s.out)


def kernel(L0_attn_x, L0_attn_W_qkv, L0_attn_b_qkv, L0_ffn_gate_w, L0_ffn_w1, L0_ffn_w2):
    import concourse.bacc as bacc
    from concourse.bass_utils import run_bass_kernel_spmd

    arrays = {
        "x": np.ascontiguousarray(L0_attn_x).reshape(T, D),
        "wqkvT": np.ascontiguousarray(np.asarray(L0_attn_W_qkv).T),
        "bqkv": np.ascontiguousarray(L0_attn_b_qkv),
        "gate_wT": np.ascontiguousarray(np.asarray(L0_ffn_gate_w).T),
        "w1": np.ascontiguousarray(L0_ffn_w1).reshape(E * D, FF),
        "w2": np.ascontiguousarray(L0_ffn_w2).reshape(E * FF, D),
    }
    nc = bacc.Bacc("TRN2", target_bir_lowering=False, num_devices=1)
    aps = {n: nc.dram_tensor(n, a.shape, F32, kind="ExternalInput").ap() for n, a in arrays.items()}
    rows = nc.dram_tensor("rows", (T, ROW), F32, kind="Internal").ap()
    x1 = nc.dram_tensor("x1", (T + CAP, D), F32, kind="Internal").ap()
    out = nc.dram_tensor("out", (T + CAP, D), F32, kind="ExternalOutput").ap()
    macaron(nc, rows=rows, x1=x1, out=out, **aps)
    result = run_bass_kernel_spmd(nc, [arrays], core_ids=[0])
    return result.results[0]["out"][:T].reshape(BATCH, SEQ, D)
```

```python
from contextlib import ExitStack

import numpy as np
import concourse.bass as bass
from concourse import mybir

F32 = mybir.dt.float32
F32R = mybir.dt.float32r
BF16 = mybir.dt.bfloat16
F16 = mybir.dt.float16
I32 = mybir.dt.int32
U32 = mybir.dt.uint32
ALU = mybir.AluOpType
ACT = mybir.ActivationFunctionType
AX = mybir.AxisListType

P = 128
BATCH, SEQ, D = 8, 1024, 256
T = BATCH * SEQ
E, FF, TOPK = 16, 512, 2
CAP = int(1.25 * T * TOPK / E)
DC = D // P
FC = FF // P
TPC = SEQ // P
CHUNKS = T // SEQ
TPE = CAP // P
NST = E * TPE
GRP = 2
GPE = TPE // GRP
GT = GRP * P
PAIR = 2 * GPE
NPAIR = E // 2
ROW = D + E
EPS = 1e-5
SCALE = 1.0 / 16.0
MASKED = -1e30
BANK = 512
NXG = 10
NYO = 5
AHEAD = 7
assert CAP % P == 0 and TPE % GRP == 0 and PAIR % NXG == 0 and PAIR % NYO == 0


def after(eng, sem, n):
    if not (isinstance(n, int) and n <= 0):
        eng.wait_ge(sem, n)


def stand_alone(eng, s):
    eng.sem_inc(s.stood_alone, 1)


def in_turn(eng, first, last, body):
    body(first)
    with eng.Fori(first + 1, last) as i:
        body(i)
    body(last)


class Shared:
    pass


def setup_constants(nc, ctx, s, gate_wT):
    def sb(name, shape, dt):
        return ctx.enter_context(nc.sbuf_tensor(name, shape, dt))

    s.ident = sb("ident", [P, P], F32)
    s.ident_bf = sb("ident_bf", [P, P], BF16)
    s.earlier = sb("earlier", [P, P], BF16)
    s.ones_bf = sb("ones_bf", [P, P], BF16)
    s.causal = sb("causal", [P, P], BF16)
    s.iota_tile = sb("iota_tile", [P, NST], F16)
    s.iota_e = sb("iota_e", [P, E], F32)
    s.token = sb("token", [P, TPC], F32)
    s.spare = sb("spare", [P, NST], F32)
    s.gw = sb("gw", [P, DC, E], F32)
    s.zeros = sb("zeros", [P, D], F32)
    s.minus_half = sb("minus_half", [P, TPC], F32)
    s.chunk_at = sb("chunk_at", [P, 1], F32)
    s.carry = sb("carry", [P, E], BF16)
    s.slots = sb("slots", [P, NST], F32)
    s.gather_idx = sb("gather_idx", [P, NST], U32)
    s.scatter_idx = sb("scatter_idx", [P, NST], U32)
    s.psum = ctx.enter_context(nc.psum_tensor("psum", [P, 8 * BANK], F32))

    tmp = ExitStack()
    iota_i = tmp.enter_context(nc.sbuf_tensor("iota_i", [P, NST], I32))
    spare_i = tmp.enter_context(nc.sbuf_tensor("spare_i", [P, NST], I32))
    token_i = tmp.enter_context(nc.sbuf_tensor("token_i", [P, TPC], I32))
    filled = ctx.enter_context(nc.semaphore("const_filled"))
    iotas = ctx.enter_context(nc.semaphore("const_iotas"))
    loaded = ctx.enter_context(nc.semaphore("const_loaded"))
    spare_zeroed = ctx.enter_context(nc.semaphore("const_spare_zeroed"))
    zeroed = ctx.enter_context(nc.semaphore("const_zeroed"))
    s.stood_alone = ctx.enter_context(nc.semaphore("stood_alone"))
    s.constants_ok = ctx.enter_context(nc.semaphore("constants_ok"))
    with nc.Block() as block:
        @block.sync
        def _(sp):
            sp.dma_start(s.gw[:], gate_wT.rearrange("(c p) e -> p c e", p=P)).then_inc(loaded, 16)
            sp.wait_ge(zeroed, 1)
            for stream in (s.x1, s.out):
                for t in range(TPE):
                    sp.dma_start(stream[T + t * P:T + (t + 1) * P, :], s.zeros[:]).then_inc(spare_zeroed, 16)
            sp.wait_ge(loaded, 16)
            sp.wait_ge(spare_zeroed, 16 * 2 * TPE)

        @block.gpsimd
        def _(pool):
            pool.iota(iota_i[:], [[1, NST]], base=0, channel_multiplier=0).then_inc(iotas, 1)
            pool.iota(spare_i[:], [[0, E], [P, TPE]], base=T + 1, channel_multiplier=1).then_inc(iotas, 1)
            pool.iota(token_i[:], [[P, TPC]], base=1, channel_multiplier=1).then_inc(iotas, 1)
            pool.wait_ge(filled, 5)
            for m, fill, op, step, mult in (
                (s.ident, 1.0, ALU.not_equal, -1, 1),
                (s.ident_bf, 1.0, ALU.not_equal, -1, 1),
                (s.earlier, 0.0, ALU.is_gt, 1, -1),
                (s.causal, MASKED, ALU.is_ge, -1, 1),
            ):
                pool.affine_select(out=m[:], in_=m[:], compare_op=op, fill=fill, base=0,
                                   pattern=[[step, P]], channel_multiplier=mult)

        @block.vector
        def _(dve):
            dve.memset(s.ident[:], 0.0).then_inc(filled, 1)
            dve.memset(s.ident_bf[:], 0.0).then_inc(filled, 1)
            dve.memset(s.earlier[:], 1.0).then_inc(filled, 1)
            dve.memset(s.causal[:], 0.0).then_inc(filled, 1)
            dve.memset(s.ones_bf[:], 1.0).then_inc(filled, 1)
            dve.memset(s.minus_half[:], -0.5)
            dve.memset(s.zeros[:], 0.0).then_inc(zeroed, 1)
            dve.memset(s.carry[:], 0.0)
            dve.memset(s.slots[:], 0.0)
            dve.wait_ge(iotas, 3)
            dve.tensor_copy(s.iota_tile[:], iota_i[:])
            dve.tensor_copy(s.iota_e[:], iota_i[:, 0:E])
            dve.tensor_copy(s.token[:], token_i[:])
            dve.memset(s.chunk_at[:], 0.0)
            dve.tensor_copy(s.spare[:], spare_i[:]).then_inc(s.constants_ok, 1)
            dve.wait_ge(s.constants_ok, 1)
    tmp.close()


NORM_STEPS = 4


def norm_factors(pool, s, mv, vareps, rstd, shift, sem, c):
    n = c * NORM_STEPS
    stand_alone(pool, s)
    pool.tensor_scalar(vareps[:], mv[:, :, 1], EPS, None, ALU.add).then_inc(sem, 1)
    pool.wait_ge(sem, n + 1)
    pool.tensor_tensor(rstd[:], vareps[:], s.minus_half[:], ALU.pow).then_inc(sem, 1)
    pool.wait_ge(sem, n + 2)
    pool.tensor_tensor(vareps[:], mv[:, :, 0], rstd[:], ALU.mult).then_inc(sem, 1)
    pool.wait_ge(sem, n + 3)
    stand_alone(pool, s)
    pool.tensor_scalar(shift[:], vareps[:], -1.0, None, ALU.mult).then_inc(sem, 1)


class Router:

    PLACED = 12
    CHAIN = 13

    def __init__(self, nc, ctx, s, name, source, banks):
        def sb(n, shape, dt):
            return ctx.enter_context(nc.sbuf_tensor(f"{name}_{n}", shape, dt))

        def sem(n):
            return s.sems.enter_context(nc.semaphore(f"{name}_{n}"))

        self.nc, self.s, self.source, self.banks = nc, s, source, banks
        self.xc = sb("xc", [P, TPC, D], F32)
        self.xn = sb("xn", [P, TPC, D], F32)
        self.xnT = sb("xnT", [P, DC, SEQ], F32)
        self.stats = sb("stats", [P, TPC, 6], F32)
        self.mv = sb("mv", [P, TPC, 2], F32)
        self.vareps = sb("vareps", [P, TPC], F32)
        self.rstd = sb("rstd", [P, TPC], F32)
        self.shift = sb("shift", [P, TPC], F32)
        self.ex = sb("ex", [P, TPC * E], F32)
        self.ex1 = sb("ex1", [P, TPC * E], F32)
        self.prob = sb("prob", [P, TPC * E], F32)
        self.top = sb("top", [P, TPC, 8], F32)
        self.idx = sb("idx", [P, TPC, 8], U32)
        self.idf = sb("idf", [P, TOPK, TPC], F32)
        self.sum1 = sb("sum1", [P, TPC], F32)
        self.sum2 = sb("sum2", [P, TPC], F32)
        self.rsum = sb("rsum", [P, TPC], F32)
        self.wt = sb("wt", [P, TOPK, TPC], F32)
        self.oh = sb("oh", [P, TOPK, TPC, E], F32)
        self.chosen = sb("chosen", [P, TPC, E], BF16)
        self.gt = sb("gt", [P, TOPK, TPC, E], F32)
        self.gate = sb("gate", [P, TPC, E], F32)
        self.taken = sb("taken", [P, E], BF16)
        self.rk = sb("rk", [P, TOPK, TPC, E], F32)
        self.rank = sb("rank", [P, TOPK, TPC], F32)
        self.rank_i = sb("rank_i", [P, TOPK, TPC], I32)
        self.high = sb("high", [P, TOPK, TPC], I32)
        self.low = sb("low", [P, TOPK, TPC], I32)
        self.lowf = sb("lowf", [P, TOPK, TPC], F32)
        self.over = sb("over", [P, TOPK, TPC], F32)
        self.tile1 = sb("tile1", [P, TOPK, TPC], F32)
        self.tilef = sb("tilef", [P, TOPK, TPC], F32)
        self.onehot_row = sb("onehot_row", [P, TPC, TOPK, P], F16)
        self.onehot_tile = sb("onehot_tile", [P, TPC, TOPK, NST], F16)
        self.taken_slot = sb("taken_slot", [P, NST], F32)

        self.x_in = sem("x_in")
        self.stat = sem("stat")
        self.meanvar = sem("meanvar")
        self.scaled = sem("scaled")
        self.normed = sem("normed")
        self.xn_out = sem("xn_out")
        self.turned = sem("turned")
        self.logits = sem("logits")
        self.chain = sem("chain")
        self.chosen_ok = sem("chosen_ok")
        self.gate_ok = sem("gate_ok")
        self.gate_out = sem("gate_out")
        self.ranked = sem("ranked")
        self.onehots = sem("onehots")
        self.row_onehots = sem("row_onehots")
        self.listed = sem("listed")
        self.carried = sem("carried")
        self.read = [sem(f"read{u}") for u in range(7)]

    def bank(self, u):
        b = self.banks[u % len(self.banks)]
        return self.s.psum[:, b * BANK:(b + 1) * BANK]

    def wait_bank(self, pe, u, c):
        if len(self.banks) == 1 and u > 0:
            after(pe, self.read[u - 1], c + 1)
        else:
            after(pe, self.read[u if len(self.banks) > 1 else 6], c)

    def load(self, sp, c):
        after(sp, self.normed, c * TPC)
        src = self.source[bass.ds(c * SEQ, SEQ), :]
        sp.dma_start(self.xc[:], src.rearrange("(j p) d -> p j d", p=P)).then_inc(self.x_in, 16)

    def store_rows(self, sp, c):
        sp.wait_ge(self.normed, c * TPC + TPC)
        dst = self.s.rows[bass.ds(c * SEQ, SEQ), 0:D]
        sp.dma_start(dst.rearrange("(j p) d -> p j d", p=P), self.xn[:]).then_inc(self.xn_out, 16)

    def store_gates(self, sp, c):
        sp.wait_ge(self.gate_ok, c + 1)
        dst = self.s.rows[bass.ds(c * SEQ, SEQ), D:ROW]
        sp.dma_start(dst.rearrange("(j p) d -> p j d", p=P), self.gate[:]).then_inc(self.gate_out, 16)

    def dve_stats(self, dve, c):
        dve.wait_ge(self.x_in, c * 16 + 16)
        for j in range(TPC):
            last = dve.bn_stats(self.stats[:, j, :], self.xc[:, j, :])
        last.then_inc(self.stat, 1)
        self.dve_mean_var(dve, c)

    def dve_mean_var(self, dve, c):
        dve.wait_ge(self.stat, c + 1)
        after(dve, self.normed, c * TPC)
        stand_alone(dve, self.s)
        for j in range(TPC):
            last = dve.bn_aggr(self.mv[:, j, :], self.stats[:, j, :])
        last.then_inc(self.meanvar, 1)

    def pool_scale(self, pool, c):
        pool.wait_ge(self.meanvar, c + 1)
        norm_factors(pool, self.s, self.mv, self.vareps, self.rstd, self.shift, self.scaled, c)

    def act_norm(self, act, c, tiles=range(TPC)):
        if 0 in tiles:
            act.wait_ge(self.scaled, c * NORM_STEPS + NORM_STEPS)
            after(act, self.turned, c * 4)
            after(act, self.xn_out, c * 16)
        for j in tiles:
            act.activation(self.xn[:, j, :], self.xc[:, j, :], ACT.Identity, bias=self.shift[:, j:j + 1],
                           scale=self.rstd[:, j:j + 1]).then_inc(self.normed, 1)

    def pe_turn(self, pe, c, units=range(4)):
        for u in units:
            pe.wait_ge(self.normed, c * TPC + 2 * u + 2)
            self.wait_bank(pe, u, c)
            bank = self.bank(u)
            for k in range(4):
                d, j = k // 2, 2 * u + k % 2
                last = pe.transpose(bank[:, k * P:(k + 1) * P], self.xn[:, j, d * P:(d + 1) * P], self.s.ident[:])
            last.then_inc(self.turned, 1)

    def act_turn(self, act, c, units=range(4)):
        if 0 in units:
            after(act, self.logits, c)
        for u in units:
            act.wait_ge(self.turned, c * 4 + u + 1)
            act.activation(self.xnT[:, :, 2 * u * P:(2 * u + 2) * P],
                           self.bank(u).rearrange("p (d t) -> p d t", d=DC), ACT.Copy).then_inc(self.read[u], 1)

    def pe_logits(self, pe, c):
        for u in range(4):
            pe.wait_ge(self.read[u], c + 1)
        self.wait_bank(pe, 4, c)
        for j in range(TPC):
            for d in range(DC):
                last = pe.matmul(self.bank(4)[:, j * E:(j + 1) * E], self.xnT[:, d, j * P:(j + 1) * P],
                                 self.s.gw[:, d, :], start=(d == 0), stop=(d == DC - 1))
        last.then_inc(self.logits, 1)

    def act_exp(self, act, c):
        act.wait_ge(self.logits, c + 1)
        after(act, self.carried, c)
        act.activation(self.ex[:], self.bank(4)[:, 0:TPC * E], ACT.Exp, scale=-1.0).then_inc(self.read[4], 1)

    def dve_link(self, dve, c):
        def link(ins):
            self.links += 1
            ins.then_inc(self.chain, 1)
            dve.wait_ge(self.chain, c * self.CHAIN + self.links)
        return link

    def dve_largest(self, dve, c):
        self.links = 0
        link = self.dve_link(dve, c)

        s = self.s
        dve.wait_ge(self.read[4], c + 1)
        link(dve.tensor_scalar(self.ex1[:], self.ex[:], 1.0, None, ALU.add))
        link(dve.reciprocal(self.prob[:], self.ex1[:]))
        stand_alone(dve, s)
        for j in range(TPC):
            last = dve.max(self.top[:, j, :], self.prob[:, j * E:(j + 1) * E])
        link(last)

    def dve_choose(self, dve, c):
        link = self.dve_link(dve, c)
        s = self.s
        dve.tensor_tensor(self.sum1[:], self.top[:, :, 0], self.top[:, :, 1], ALU.add)
        for j in range(TPC):
            last = dve.max_index(self.idx[:, j, :], self.top[:, j, :], self.prob[:, j * E:(j + 1) * E])
        link(last)
        dve.tensor_copy(self.idf[:], self.idx[:, :, 0:TOPK].rearrange("p j k -> p k j"))
        link(dve.tensor_scalar(self.sum2[:], self.sum1[:], 1e-6, None, ALU.add))
        link(dve.reciprocal(self.rsum[:], self.sum2[:]))
        dve.scalar_tensor_tensor(self.wt[:], self.top[:, :, 0:TOPK].rearrange("p j k -> p k j"), 0.5,
                                 self.rsum[:].unsqueeze(1).to_broadcast([P, TOPK, TPC]), ALU.mult, ALU.mult)
        link(dve.tensor_tensor(
            self.oh[:].rearrange("p k j e -> p (k j) e"),
            s.iota_e[:].unsqueeze(1).to_broadcast([P, TOPK * TPC, E]),
            self.idf[:].rearrange("p k j -> p (k j)").unsqueeze(2).to_broadcast([P, TOPK * TPC, E]), ALU.is_equal))
        dve.tensor_tensor(self.chosen[:], self.oh[:, 0], self.oh[:, 1], ALU.add).then_inc(self.chosen_ok, 1)
        link(dve.tensor_tensor(
            self.gt[:].rearrange("p k j e -> p (k j) e"), self.oh[:].rearrange("p k j e -> p (k j) e"),
            self.wt[:].rearrange("p k j -> p (k j)").unsqueeze(2).to_broadcast([P, TOPK * TPC, E]), ALU.mult))
        after(dve, self.gate_out, c * 16)
        dve.tensor_tensor(self.gate[:], self.gt[:, 0], self.gt[:, 1], ALU.add).then_inc(self.gate_ok, 1)

    def pe_rank(self, pe, c):
        s = self.s
        pe.wait_ge(self.chosen_ok, c + 1)
        after(pe, self.carried, c)
        self.wait_bank(pe, 5, c)
        n = TPC * E
        bank = self.bank(5)
        pe.matmul(bank[:, 0:n], s.earlier[:], self.chosen[:].rearrange("p j e -> p (j e)"), start=True, stop=False)
        for j in range(TPC - 1):
            pe.matmul(bank[:, (j + 1) * E:n].rearrange("p (j e) -> p j e", e=E), s.ones_bf[:],
                      self.chosen[:, j:j + 1, :].to_broadcast([P, TPC - 1 - j, E]),
                      start=False, stop=False, skip_group_check=True)
        pe.matmul(bank[:, 0:n].rearrange("p (j e) -> p j e", e=E), s.ones_bf[:],
                  s.carry[:].unsqueeze(1).to_broadcast([P, TPC, E]), start=False, stop=True).then_inc(self.ranked, 1)

    def dve_place(self, dve, c):
        link = self.dve_link(dve, c)
        s = self.s
        dve.wait_ge(self.ranked, c + 1)
        counts = self.bank(5)[:, 0:TPC * E].rearrange("p (j e) -> p j e", e=E)
        for k in range(TOPK):
            last = dve.tensor_tensor(self.rk[:, k], self.oh[:, k], counts, ALU.mult)
        last.then_inc(self.read[5], 1)
        dve.wait_ge(self.read[5], c + 1)
        with self.nc.allow_low_precision("counts up to TPC per partition, exact in bfloat16"):
            dve.tensor_reduce(self.taken[:], self.chosen[:].rearrange("p j e -> p e j"), AX.X, ALU.add)
        link(dve.tensor_reduce(self.rank[:].rearrange("p k j -> p (k j)"),
                               self.rk[:].rearrange("p k j e -> p (k j) e"), AX.X, ALU.add))
        dve.tensor_tensor(s.carry[:], s.carry[:], self.taken[:], ALU.add).then_inc(self.carried, 1)
        dve.tensor_scalar(self.over[:], self.rank[:], float(CAP), 1000.0, ALU.is_ge, ALU.mult)
        link(dve.tensor_copy(self.rank_i[:], self.rank[:]))
        dve.tensor_scalar(self.high[:], self.rank_i[:], 7, None, ALU.arith_shift_right)
        dve.scalar_tensor_tensor(self.tile1[:], self.idf[:], float(TPE), self.over[:], ALU.mult, ALU.add)
        link(dve.tensor_scalar(self.low[:], self.rank_i[:], P - 1, None, ALU.bitwise_and))
        dve.tensor_copy(self.lowf[:], self.low[:])
        link(dve.tensor_tensor(self.tilef[:], self.high[:], self.tile1[:], ALU.add))
        assert self.links == self.PLACED

    def dve_onehots(self, dve, c, tiles=range(TPC)):
        s = self.s
        if 0 in tiles:
            after(dve, self.listed, c)
        for j in tiles:
            dve.tensor_scalar(self.onehot_row[:, j, 0, :], s.iota_tile[:, 0:P], self.lowf[:, 0, j:j + 1],
                              None, ALU.is_equal)
            for k in range(TOPK):
                dve.tensor_scalar(self.onehot_tile[:, j, k, :], s.iota_tile[:], self.tilef[:, k, j:j + 1],
                                  s.token[:, j:j + 1], ALU.is_equal, ALU.mult).then_inc(self.onehots, 1)

    def pool_onehots(self, pool, c):
        pool.wait_ge(self.chain, c * self.CHAIN + self.PLACED)
        after(pool, self.listed, c)
        stand_alone(pool, self.s)
        for j in range(TPC):
            pool.tensor_scalar(self.onehot_row[:, j, 1, :], self.s.iota_tile[:, 0:P],
                               self.lowf[:, 1, j:j + 1], None, ALU.is_equal).then_inc(self.row_onehots, 1)

    def pe_list(self, pe, c):
        self.wait_bank(pe, 6, c)
        n = TPC * TOPK
        for i in range(n):
            j, k = i // TOPK, i % TOPK
            pe.wait_ge(self.onehots, c * n + i + 1)
            if k == 1:
                pe.wait_ge(self.row_onehots, c * TPC + j + 1)
            last = pe.matmul(self.bank(6)[:, 0:NST], self.onehot_row[:, j, k, :], self.onehot_tile[:, j, k, :],
                             start=(i == 0), stop=(i == n - 1))
        last.then_inc(self.listed, 1)

    def dve_list(self, dve, c):
        s = self.s
        dve.wait_ge(self.listed, c + 1)
        found = self.bank(6)[:, 0:NST]
        dve.tensor_scalar(self.taken_slot[:], found, 1.0, s.chunk_at[:, 0:1], ALU.min, ALU.mult)
        dve.tensor_tensor(s.slots[:], found, s.slots[:], ALU.add).then_inc(self.read[6], 1)
        dve.wait_ge(self.read[6], c + 1)
        dve.tensor_scalar(s.chunk_at[:], s.chunk_at[:], float(SEQ), None, ALU.add)
        self.links += 1
        dve.tensor_tensor(s.slots[:], s.slots[:], self.taken_slot[:], ALU.add).then_inc(self.chain, 1)
        dve.wait_ge(self.chain, c * self.CHAIN + self.CHAIN)
        assert self.links == self.CHAIN, self.links

    def dve_finish(self, dve, scratch):
        s = self.s
        tok, gat, emp = scratch
        base = CHUNKS * self.CHAIN
        n = 0

        def link(ins):
            nonlocal n
            n += 1
            ins.then_inc(self.chain, 1)
            dve.wait_ge(self.chain, base + n)

        dve.tensor_scalar(gat[:], s.slots[:], -1.0, 0.0, ALU.add, ALU.max)
        link(dve.scalar_tensor_tensor(emp[:], s.slots[:], 0.0, s.spare[:], ALU.is_equal, ALU.mult))
        dve.tensor_copy(s.gather_idx[:], gat[:])
        link(dve.scalar_tensor_tensor(tok[:], s.slots[:], -1.0, emp[:], ALU.add, ALU.add))
        dve.tensor_copy(s.scatter_idx[:], tok[:])
        dve.memset(s.carry[:], 0.0)
        dve.memset(s.chunk_at[:], 0.0)
        link(dve.memset(s.slots[:], 0.0))


def route_phase(nc, s, name, source, stream):
    with ExitStack() as ctx:
        r = Router(nc, ctx, s, name, source, banks=list(range(7)))
        scratch = [ctx.enter_context(nc.sbuf_tensor(f"{name}_fin{i}", [P, NST], F32)) for i in range(3)]
        kept = ctx.enter_context(nc.semaphore(f"{name}_kept"))
        end = CHUNKS - 1

        def there(c, n):
            return not isinstance(c, int) or c + n <= end

        def chunks(eng, step):
            step(0)
            with eng.Fori(1, end - 1) as c:
                step(c)
            step(end - 1)
            step(end)

        with nc.Block() as block:
            @block.sync
            def _(sp):
                def keep(c):
                    sp.wait_ge(r.x_in, c * 16 + 16)
                    dst = stream[bass.ds(c * SEQ, SEQ), :]
                    sp.dma_start(dst.rearrange("(j p) d -> p j d", p=P), r.xc[:]).then_inc(kept, 16)

                def load(c):
                    after(sp, kept, c * 16)
                    stand_alone(sp, s)
                    r.load(sp, c)

                def step(c):
                    if there(c, 1):
                        keep(c + 1)
                        r.store_rows(sp, c + 1)
                    if there(c, 2):
                        load(c + 2)
                    r.store_gates(sp, c)

                load(0)
                keep(0)
                r.store_rows(sp, 0)
                load(1)
                chunks(sp, step)
                sp.wait_ge(kept, 16 * CHUNKS)
                sp.wait_ge(r.xn_out, 16 * CHUNKS)
                sp.wait_ge(r.gate_out, 16 * CHUNKS)

            @block.gpsimd
            def _(pool):
                def step(c):
                    if there(c, 2):
                        r.pool_scale(pool, c + 2)
                    r.pool_onehots(pool, c)

                r.pool_scale(pool, 0)
                r.pool_scale(pool, 1)
                chunks(pool, step)

            @block.scalar
            def _(act):
                def step(c):
                    r.act_exp(act, c)
                    if there(c, 1):
                        r.act_turn(act, c + 1)
                    if there(c, 2):
                        r.act_norm(act, c + 2)

                r.act_norm(act, 0)
                r.act_turn(act, 0)
                r.act_norm(act, 1)
                chunks(act, step)

            @block.vector
            def _(dve):
                def step(c):
                    r.dve_largest(dve, c)
                    r.dve_choose(dve, c)
                    if there(c, 2):
                        r.dve_stats(dve, c + 2)
                    r.dve_place(dve, c)
                    r.dve_onehots(dve, c)
                    r.dve_list(dve, c)

                r.dve_stats(dve, 0)
                r.dve_stats(dve, 1)
                chunks(dve, step)
                r.dve_finish(dve, scratch)

            @block.tensor
            def _(pe):
                def step(c):
                    if there(c, 1):
                        r.pe_turn(pe, c + 1)
                    r.pe_rank(pe, c)
                    if there(c, 1):
                        r.pe_logits(pe, c + 1)
                    r.pe_list(pe, c)

                r.pe_turn(pe, 0)
                r.pe_logits(pe, 0)
                chunks(pe, step)


def expert_phase(nc, s, name, stream):
    with ExitStack() as ctx:
        def sb(n, shape, dt):
            return ctx.enter_context(nc.sbuf_tensor(f"{name}_{n}", shape, dt))

        def sem(n):
            return s.sems.enter_context(nc.semaphore(f"{name}_{n}"))

        raw1 = [sb(f"raw1_{i}", [P, DC, FF], F32) for i in range(2)]
        raw2 = [sb(f"raw2_{i}", [P, FC, D], F32) for i in range(2)]
        w1h = [sb(f"w1h{i}", [P, DC, FF], F32R) for i in range(2)]
        w1l = [sb(f"w1l{i}", [P, DC, FF], F32R) for i in range(2)]
        w2h = [sb(f"w2h{i}", [P, FC, D], F32R) for i in range(2)]
        w2l = [sb(f"w2l{i}", [P, FC, D], F32R) for i in range(2)]
        xg = [sb(f"xg{i}", [P, GRP, ROW], F32) for i in range(NXG)]
        xh = [sb(f"xh{i}", [P, DC, GT], F32R) for i in range(2)]
        xl = [sb(f"xl{i}", [P, DC, GT], F32R) for i in range(2)]
        h = [sb(f"h{i}", [P, FC, GT], F32) for i in range(2)]
        hh = [sb(f"hh{i}", [P, FC, GT], F32R) for i in range(2)]
        hl = [sb(f"hl{i}", [P, FC, GT], F32R) for i in range(2)]
        yo = [sb(f"yo{i}", [P, GRP, D], F32) for i in range(NYO)]
        half = GPE * GRP
        gidx = [sb(f"gidx{i}", [P, half], U32) for i in range(2)]
        sidx = [sb(f"sidx{i}", [P, half], U32) for i in range(2)]

        w_in = [sem(f"w_in{i}") for i in range(2)]
        w_split = sem("w_split")
        gathered = [sem(f"gathered{i}") for i in range(NXG)]
        gidx_ok = sem("gidx_ok")
        sidx_ok = sem("sidx_ok")
        turned = sem("turned")
        x_hi = sem("x_hi")
        x_lo = sem("x_lo")
        up = sem("up")
        act_h = sem("act_h")
        h_hi = sem("h_hi")
        h_lo = sem("h_lo")
        down = sem("down")
        weighted = sem("weighted")
        scattered = [sem(f"scattered{i}") for i in range(NYO)]

        psum = s.psum
        px = [psum[:, i * BANK:(i + 1) * BANK] for i in (0, 1)]
        ph = [psum[:, (2 + 2 * i) * BANK:(4 + 2 * i) * BANK] for i in (0, 1)]
        po = [psum[:, i * BANK:(i + 1) * BANK] for i in (6, 7)]
        end = NPAIR - 1

        def ahead(i, j, n, part):
            if j + n < PAIR:
                part(i, j + n)
            elif i is not end:
                part(i + 1, j + n - PAIR)

        with nc.Block() as block:
            @block.sync
            def _(sp):
                def load(e, p):
                    after(sp, w_split, e * 4 - 4)
                    w1 = s.w1[bass.ds(e * D, D), :].rearrange("(c p) f -> p c f", p=P)
                    w2 = s.w2[bass.ds(e * FF, FF), :].rearrange("(c p) d -> p c d", p=P)
                    sp.dma_start(raw1[p][:], w1).then_inc(w_in[p], 16)
                    sp.dma_start(raw2[p][:], w2).then_inc(w_in[p], 16)

                def step(i):
                    load(i * 2, 0)
                    load(i * 2 + 1, 1)

                load(0, 0)
                load(1, 1)
                with sp.Fori(1, NPAIR) as i:
                    step(i)

            @block.gpsimd
            def _(pool):
                def gather(i, j):
                    b = j % NXG
                    after(pool, weighted, (i * PAIR + j + 1 - NXG) * GRP)
                    stand_alone(pool, s)
                    for t in range(GRP):
                        k = (j % GPE) * GRP + t
                        pool.indirect_dma_start(
                            xg[b][:, t, :], None, s.rows[:, :],
                            bass.IndirectOffsetOnAxis(gidx[j // GPE][:, k:k + 1], axis=0),
                        ).then_inc(gathered[b], 16)

                def scatter(i, j):
                    b = j % NYO
                    pool.wait_ge(weighted, (i * PAIR + j + 1) * GRP)
                    stand_alone(pool, s)
                    for t in range(GRP):
                        k = (j % GPE) * GRP + t
                        pool.indirect_dma_start(
                            stream[:, :],
                            bass.IndirectOffsetOnAxis(sidx[j // GPE][:, k:k + 1], axis=0),
                            yo[b][:, t, :], None, compute_op=ALU.add,
                        ).then_inc(scattered[b], 16)

                def gather_columns(i, w):
                    for q in gathered[w * GPE:(w + 1) * GPE]:
                        after(pool, q, i * 16 * GRP)
                    pool.tensor_copy(gidx[w][:], s.gather_idx[:, bass.ds((i * 2 + w) * half, half)]).then_inc(gidx_ok, 1)
                    pool.wait_ge(gidx_ok, i * 2 + w + 1)

                def scatter_columns(i, w):
                    for q in scattered:
                        after(pool, q, (i * 2 + w) * 16 * GRP)
                    pool.tensor_copy(sidx[w][:], s.scatter_idx[:, bass.ds((i * 2 + w) * half, half)]).then_inc(sidx_ok, 1)
                    pool.wait_ge(sidx_ok, i * 2 + w + 1)

                def body(i):
                    for j in range(PAIR):
                        if (j + AHEAD) % PAIR == GPE and (i is not end or j + AHEAD < PAIR):
                            gather_columns(i + (j + AHEAD) // PAIR, 1)
                        if (j + AHEAD) % PAIR == 0 and i is not end:
                            gather_columns(i + 1, 0)
                        ahead(i, j, AHEAD, gather)
                        if j % GPE == 0:
                            scatter_columns(i, j // GPE)
                        scatter(i, j)

                gather_columns(0, 0)
                for j in range(AHEAD):
                    if j == GPE:
                        gather_columns(0, 1)
                    gather(0, j)
                in_turn(pool, 0, end, body)
                for q in scattered:
                    pool.wait_ge(q, E * 16 * GRP)

            @block.tensor
            def _(pe):
                def turn(i, j):
                    b = j % NXG
                    pe.wait_ge(gathered[b], (i + 1) * 16 * GRP)
                    after(pe, x_lo, i * PAIR + j - 1)
                    for k in range(DC * GRP):
                        d, t = k // GRP, k % GRP
                        last = pe.transpose(px[j % 2][:, k * P:(k + 1) * P], xg[b][:, t, d * P:(d + 1) * P],
                                            s.ident[:])
                    last.then_inc(turned, 1)

                def mm_up(i, j):
                    p, w = j % 2, j // GPE
                    pe.wait_ge(x_lo, i * PAIR + j + 1)
                    if j % GPE == 0:
                        pe.wait_ge(w_split, (i * 2 + w) * 4 + 2)
                    for f in range(FC):
                        if f % 2 == 0:
                            after(pe, act_h, (i * PAIR + j - 2) * 2 + f // 2 + 1)
                        out = ph[p][:, f * GT:(f + 1) * GT]
                        n = 0
                        for a, b in ((w1h, xh), (w1h, xl), (w1l, xh)):
                            for d in range(DC):
                                last = pe.matmul(out, a[w][:, d, f * P:(f + 1) * P], b[p][:, d, :],
                                                 start=(n == 0), stop=(n == 3 * DC - 1))
                                n += 1
                        if f % 2:
                            last.then_inc(up, 1)

                def mm_down(i, j):
                    p, w = j % 2, j // GPE
                    pe.wait_ge(h_lo, (i * PAIR + j + 1) * 2)
                    after(pe, weighted, (i * PAIR + j - 1) * GRP)
                    if j % GPE == 0:
                        pe.wait_ge(w_split, (i * 2 + w) * 4 + 4)
                    for t in range(GRP):
                        out = po[p][:, t * D:(t + 1) * D]
                        n = 0
                        for f in range(FC):
                            for a, b in ((hh, w2h), (hh, w2l), (hl, w2h)):
                                last = pe.matmul(out, a[p][:, f, t * P:(t + 1) * P], b[w][:, f, :],
                                                 start=(n == 0), stop=(n == 3 * FC - 1))
                                n += 1
                    last.then_inc(down, 1)

                def body(i):
                    for j in range(PAIR):
                        ahead(i, j, 2, turn)
                        ahead(i, j, 1, mm_up)
                        mm_down(i, j)

                turn(0, 0)
                turn(0, 1)
                mm_up(0, 0)
                in_turn(pe, 0, end, body)

            @block.scalar
            def _(act):
                def x_high(i, j):
                    act.wait_ge(turned, i * PAIR + j + 1)
                    after(act, up, (i * PAIR + j - 1) * 2)
                    act.activation(xh[j % 2][:], px[j % 2].rearrange("p (d t) -> p d t", d=DC),
                                   ACT.Copy).then_inc(x_hi, 1)

                def gelu(i, j):
                    p = j % 2
                    for q in range(2):
                        act.wait_ge(up, (i * PAIR + j) * 2 + q + 1)
                        after(act, h_lo, (i * PAIR + j - 2) * 2 + q + 1)
                        act.activation(h[p][:, 2 * q:2 * q + 2, :],
                                       ph[p][:, q * BANK:(q + 1) * BANK].rearrange("p (f t) -> p f t", f=2),
                                       ACT.Gelu).then_inc(act_h, 1)

                def weight(i, j):
                    b, y, w = j % NXG, j % NYO, j // GPE
                    act.wait_ge(down, i * PAIR + j + 1)
                    after(act, scattered[y], (i * 2 + j // NYO) * 16 * GRP)
                    for t in range(GRP):
                        act.activation(yo[y][:, t, :], po[j % 2][:, t * D:(t + 1) * D], ACT.Copy,
                                       scale=xg[b][:, t, bass.ds(i * 2 + D + w, 1)]).then_inc(weighted, 1)

                def body(i):
                    for j in range(PAIR):
                        ahead(i, j, 2, x_high)
                        ahead(i, j, 1, gelu)
                        weight(i, j)

                x_high(0, 0)
                x_high(0, 1)
                gelu(0, 0)
                in_turn(act, 0, end, body)

            @block.vector
            def _(dve):
                def x_low(i, j):
                    dve.wait_ge(x_hi, i * PAIR + j + 1)
                    dve.tensor_tensor(xl[j % 2][:].rearrange("p d t -> p (d t)"), px[j % 2],
                                      xh[j % 2][:].bitcast(F32).rearrange("p d t -> p (d t)"),
                                      ALU.subtract).then_inc(x_lo, 1)

                def split_h(i, j):
                    p = j % 2
                    after(dve, down, i * PAIR + j - 1)
                    for q in range(2):
                        rows = slice(2 * q, 2 * q + 2)
                        dve.wait_ge(act_h, (i * PAIR + j) * 2 + q + 1)
                        dve.tensor_copy(hh[p][:, rows, :], h[p][:, rows, :]).then_inc(h_hi, 1)
                        dve.wait_ge(h_hi, (i * PAIR + j) * 2 + q + 1)
                        dve.tensor_tensor(hl[p][:, rows, :], h[p][:, rows, :], hh[p][:, rows, :].bitcast(F32),
                                          ALU.subtract).then_inc(h_lo, 1)

                def split_w(i, w, part):
                    if part == 0:
                        dve.wait_ge(w_in[w], i * 32 + 32)
                        after(dve, down, (i * 2 + w - 1) * GPE)
                    raw, hi, lo = ((raw1, w1h, w1l), (raw2, w2h, w2l))[part // 2]
                    if part % 2 == 0:
                        dve.tensor_copy(hi[w][:], raw[w][:]).then_inc(w_split, 1)
                    else:
                        dve.wait_ge(w_split, (i * 2 + w) * 4 + part)
                        dve.tensor_tensor(lo[w][:], raw[w][:], hi[w][:].bitcast(F32),
                                          ALU.subtract).then_inc(w_split, 1)

                def body(i):
                    for j in range(PAIR):
                        ahead(i, j, 2, x_low)
                        ahead(i, j, 1, split_h)
                        part = j % GPE - 1
                        if part >= 0 and j < GPE:
                            split_w(i, 1, part)
                        elif part >= 0 and i is not end:
                            split_w(i + 1, 0, part)

                for part in range(4):
                    split_w(0, 0, part)
                x_low(0, 0)
                x_low(0, 1)
                split_h(0, 0)
                in_turn(dve, 0, end, body)


def attention_phase(nc, s, name):
    with ExitStack() as ctx:
        def sb(n, shape, dt):
            return ctx.enter_context(nc.sbuf_tensor(f"{name}_{n}", shape, dt))

        def sem(n):
            return s.sems.enter_context(nc.semaphore(f"{name}_{n}"))

        r = Router(nc, ctx, s, f"{name}_route", s.out, banks=[7])
        xa = sb("xa", [P, TPC, D], F32)
        stats = sb("stats", [P, TPC, 6], F32)
        mv = sb("mv", [P, TPC, 2], F32)
        vareps = sb("vareps", [P, TPC], F32)
        rstd = sb("rstd", [P, TPC], F32)
        shift = sb("shift", [P, TPC], F32)
        xTh = sb("xTh", [P, DC, SEQ], F32R)
        xTl = sb("xTl", [P, DC, SEQ], F32R)
        wh = sb("wh", [P, DC, 3 * D], F32R)
        wl = sb("wl", [P, DC, 3 * D], F32R)
        bqk = sb("bqk", [P, 2 * DC], F32)
        bv = sb("bv", [P, D], F32)
        qkh = sb("qkh", [P, 2 * DC, SEQ], F32R)
        qkl = sb("qkl", [P, 2 * DC, SEQ], F32R)
        vh = sb("vh", [P, TPC, D], F32R)
        vl = sb("vl", [P, TPC, D], F32R)
        prob = [sb(f"prob{i}", [P, SEQ], F32) for i in range(2)]
        pTh = [sb(f"pTh{i}", [P, TPC, P], F32R) for i in range(2)]
        pTl = [sb(f"pTl{i}", [P, TPC, P], F32R) for i in range(2)]
        negmax = sb("negmax", [P, TPC], F32)
        rsum = sb("rsum", [P, TPC], F32)
        rinv = sb("rinv", [P, TPC], F32)
        xr = sb("xr", [P, TPC, D], F32)
        x2 = r.xc
        raw_w = sb("raw_w", [P, DC, 3 * D], F32)
        scratch = [sb(f"fin{i}", [P, NST], F32) for i in range(3)]

        w_in = sem("w_in")
        w_ok = sem("w_ok")
        xa_in = sem("xa_in")
        stat = sem("stat")
        meanvar = sem("meanvar")
        scaled = sem("scaled")
        normed = sem("normed")
        turned = sem("turned")
        turned_hi = sem("turned_hi")
        turned_lo = sem("turned_lo")
        projected = sem("projected")
        split_hi = sem("split_hi")
        split_lo = sem("split_lo")
        scored = sem("scored")
        maxed = sem("maxed")
        exped = sem("exped")
        inverted = sem("inverted")
        mixed = sem("mixed")
        summed = sem("summed")
        xr_in = [sem(f"xr_in{h}") for h in range(2)]
        xr_biased = [sem(f"xr_biased{h}") for h in range(2)]
        x2_out = [sem(f"x2_out{h}") for h in range(2)]

        psum = s.psum
        bank = [psum[:, i * BANK:(i + 1) * BANK] for i in range(8)]
        score = [psum[:, 2 * i * BANK:2 * (i + 1) * BANK] for i in range(2)]
        tp = bank[4:6]
        po = bank[6]
        v_bank = [bank[1], bank[3]]
        end = BATCH - 1

        PROJ_QK, PROJ_V = 2 * DC * 2, TPC // 2
        PROJ = PROJ_QK + PROJ_V
        XT = TPC // 2
        XT_STEPS = (6, 7)
        PT = [(i + 4) // 4 for i in range(TPC)]
        TURNS = sum(PT) + XT

        def pt_first(b, i):
            n = sum(PT[:i])
            if b is not end:
                n += sum(XT // 2 for step in XT_STEPS if i > step)
            return b * TURNS + XT + n

        def xt_number(b, u):
            if isinstance(b, int) and b == 0:
                return u
            step = XT_STEPS[2 * u // XT]
            return (b - 1) * TURNS + XT + sum(PT[:step + 1]) + u

        def tp_of(b, i, k):
            return tp[(sum(PT[:i]) + k) % 2]

        assert TURNS % 2 == 0 and (XT // 2) % 2 == 0 and all(sum(PT[:i + 1]) % 2 == 0 for i in XT_STEPS)

        def xt_units(i):
            k = XT_STEPS.index(i)
            return range(k * XT // 2, (k + 1) * XT // 2)

        def bodies(eng, body):
            body(0)
            body(1)
            with eng.Fori(2, end) as b:
                body(b)
            body(end)

        def routed(b):
            return not (isinstance(b, int) and b == 0)

        def listed_in(b):
            return not (isinstance(b, int) and b <= 1)

        HALF = TPC // 2

        def half(dram, b, h):
            return dram[bass.ds(b * SEQ + h * HALF * P, HALF * P), :].rearrange("(j p) d -> p j d", p=P)

        with nc.Block() as block:
            @block.sync
            def _(sp):
                def load_xa(b):
                    if not (isinstance(b, int) and b == 0):
                        sp.wait_ge(turned, xt_number(b - 1, XT - 1) + 1)
                    src = s.x1[bass.ds(b * SEQ, SEQ), :]
                    sp.dma_start(xa[:], src.rearrange("(j p) d -> p j d", p=P)).then_inc(xa_in, 16)

                def load_xr(b, h):
                    after(sp, summed, (b - 1) * TPC + (h + 1) * HALF)
                    sp.dma_start(xr[:, h * HALF:(h + 1) * HALF, :], half(s.x1, b, h)).then_inc(xr_in[h], 16)

                def store_x2(b, h):
                    sp.wait_ge(summed, b * TPC + (h + 1) * HALF)
                    sp.dma_start(half(s.out, b, h), x2[:, h * HALF:(h + 1) * HALF, :]).then_inc(x2_out[h], 16)

                def body(b):
                    load_xr(b, 1)
                    if routed(b):
                        r.store_rows(sp, b - 1)
                    store_x2(b, 0)
                    if b is not end:
                        load_xr(b + 1, 0)
                    if routed(b):
                        r.store_gates(sp, b - 1)
                    if not (isinstance(b, int) and b >= end - 1):
                        load_xa(b + 2)
                    store_x2(b, 1)

                load_xa(0)
                sp.dma_start(raw_w[:], s.wqkvT.rearrange("(c p) e -> p c e", p=P)).then_inc(w_in, 16)
                with nc.allow_non_contiguous_dma("a bias per partition, once"):
                    sp.dma_start(bqk[:], s.bqkv[0:2 * D].rearrange("(m p) -> p m", p=P)).then_inc(w_in, 16)
                sp.dma_start(bv[:], s.bqkv[2 * D:3 * D].partition_broadcast(P)).then_inc(w_in, 16)
                load_xr(0, 0)
                load_xa(1)
                bodies(sp, body)
                for q in x2_out:
                    sp.wait_ge(q, BATCH * 16)
                r.store_rows(sp, end)
                r.store_gates(sp, end)
                sp.wait_ge(r.xn_out, 16 * CHUNKS)
                sp.wait_ge(r.gate_out, 16 * CHUNKS)

            @block.gpsimd
            def _(pool):
                def scale(b):
                    pool.wait_ge(meanvar, b + 1)
                    norm_factors(pool, s, mv, vareps, rstd, shift, scaled, b)

                def bias(b, h):
                    pool.wait_ge(xr_in[h], b * 16 + 16)
                    rows = slice(h * HALF, (h + 1) * HALF)
                    pool.tensor_tensor(xr[:, rows, :], xr[:, rows, :],
                                       bv[:].unsqueeze(1).to_broadcast([P, HALF, D]),
                                       ALU.add).then_inc(xr_biased[h], 1)

                def body(b):
                    if routed(b):
                        r.pool_scale(pool, b - 1)
                    bias(b, 1)
                    if b is not end:
                        scale(b + 1)
                        bias(b + 1, 0)
                    if routed(b):
                        r.pool_onehots(pool, b - 1)

                scale(0)
                pool.wait_ge(w_in, 16 * 3)
                bias(0, 0)
                bodies(pool, body)
                r.pool_scale(pool, end)
                r.pool_onehots(pool, end)

            @block.tensor
            def _(pe):
                def turn_x(b, units=range(XT)):
                    for u in units:
                        pe.wait_ge(normed, b * TPC + 2 * u + 2)
                        after(pe, turned_lo, xt_number(b, u) - 1)
                        out = tp[u % 2]
                        for k in range(4):
                            d, j = k // 2, 2 * u + k % 2
                            last = pe.transpose(out[:, k * P:(k + 1) * P], xa[:, j, d * P:(d + 1) * P], s.ident[:])
                        last.then_inc(turned, 1)

                def split_product(out, stat, mov, extra=None):
                    n, total = 0, 3 * len(stat)
                    for a, b in zip(stat, mov):
                        for x, y in ((0, 0), (0, 1), (1, 0)):
                            last = pe.matmul(out, a[x], b[y], start=(n == 0), stop=(n == total - 1))
                            if n == 0 and extra is not None:
                                pe.matmul(*extra, start=False, stop=False, skip_group_check=True)
                            n += 1
                    return last

                def qk(b, units=range(PROJ_QK)):
                    if 0 in units:
                        after(pe, exped, b * TPC)
                    for u in units:
                        m, t = u % (2 * DC), u // (2 * DC)
                        if m == 0:
                            pe.wait_ge(turned_lo, xt_number(b, (t + 1) * XT // 2 - 1) + 1)
                        if u >= 4:
                            pe.wait_ge(split_lo, b * PROJ + u - 3)
                        cols = slice(t * BANK, (t + 1) * BANK)
                        split_product(bank[u % 4],
                                      [(wh[:, d, m * P:(m + 1) * P], wl[:, d, m * P:(m + 1) * P]) for d in range(DC)],
                                      [(xTh[:, d, cols], xTl[:, d, cols]) for d in range(DC)]).then_inc(projected, 1)

                def v(b, units):
                    for u in units:
                        if u == 0:
                            pe.wait_ge(split_lo, b * PROJ + PROJ_QK)
                        if u >= 2:
                            pe.wait_ge(split_lo, b * PROJ + PROJ_QK + u - 1)
                        for k in range(2):
                            t = slice((2 * u + k) * P, (2 * u + k + 1) * P)
                            last = split_product(v_bank[u % 2][:, k * D:(k + 1) * D],
                                                 [(xTh[:, d, t], xTl[:, d, t]) for d in range(DC)],
                                                 [(wh[:, d, 2 * D:3 * D], wl[:, d, 2 * D:3 * D]) for d in range(DC)])
                        last.then_inc(projected, 1)

                def scores(b, i):
                    if i == BANK // P:
                        pe.wait_ge(split_lo, b * PROJ + PROJ)
                    if i >= 2:
                        pe.wait_ge(exped, b * TPC + i - 1)
                    q = slice(i * P, (i + 1) * P)
                    n = (i + 1) * P
                    for c in range(0, n, BANK):
                        w = min(BANK, n - c)
                        diagonal = (score[i % 2][:, n - P:n], s.ident_bf[:], s.causal[:]) if c + w == n else None
                        last = split_product(score[i % 2][:, c:c + w],
                                             [(qkh[:, d, q], qkl[:, d, q]) for d in range(DC)],
                                             [(qkh[:, DC + d, c:c + w], qkl[:, DC + d, c:c + w]) for d in range(DC)],
                                             extra=diagonal)
                    last.then_inc(scored, 1)

                def turn_p(b, i):
                    pe.wait_ge(exped, b * TPC + i + 1)
                    for u in range(PT[i]):
                        after(pe, turned_lo, pt_first(b, i) + u - 1)
                        out = tp_of(b, i, u)
                        for k in range(4 * u, min(4 * u + 4, i + 1)):
                            last = pe.transpose(out[:, (k % 4) * P:(k % 4 + 1) * P],
                                                prob[i % 2][:, k * P:(k + 1) * P], s.ident[:])
                        last.then_inc(turned, 1)

                def mix(b, i):
                    if i == 0:
                        pe.wait_ge(split_lo, b * PROJ + PROJ)
                    pe.wait_ge(turned_lo, pt_first(b, i) + PT[i])
                    after(pe, summed, b * TPC + i)
                    split_product(po[:, 0:D], [(pTh[i % 2][:, k, :], pTl[i % 2][:, k, :]) for k in range(i + 1)],
                                  [(vh[:, k, :], vl[:, k, :]) for k in range(i + 1)]).then_inc(mixed, 1)

                def body(b):
                    v(b, range(0, 2))
                    scores(b, 0)
                    scores(b, 1)
                    v(b, range(2, PROJ_V))
                    for i in range(TPC):
                        turn_p(b, i)
                        if routed(b) and i == 5:
                            r.pe_logits(pe, b - 1)
                        if i + 2 < TPC:
                            scores(b, i + 2)
                        if listed_in(b) and i == 0:
                            r.pe_list(pe, b - 2)
                        if i > 0:
                            mix(b, i - 1)
                        if routed(b) and 1 <= i < 5:
                            r.pe_turn(pe, b - 1, [i - 1])
                        if i in XT_STEPS and b is not end:
                            turn_x(b + 1, xt_units(i))
                    if b is not end:
                        qk(b + 1, range(0, 4))
                    if routed(b):
                        r.pe_rank(pe, b - 1)
                    if b is not end:
                        qk(b + 1, range(4, PROJ_QK))
                    mix(b, TPC - 1)

                turn_x(0)
                pe.wait_ge(w_ok, 3)
                qk(0)
                bodies(pe, body)
                r.pe_list(pe, end - 1)
                r.pe_turn(pe, end)
                r.pe_logits(pe, end)
                r.pe_rank(pe, end)
                r.pe_list(pe, end)

            @block.scalar
            def _(act):
                def norm(b, tiles):
                    if 0 in tiles:
                        act.wait_ge(scaled, b * NORM_STEPS + NORM_STEPS)
                    for j in tiles:
                        act.activation(xa[:, j, :], xa[:, j, :], ACT.Identity, bias=shift[:, j:j + 1],
                                       scale=rstd[:, j:j + 1]).then_inc(normed, 1)

                def high_x(b, units=range(XT)):
                    if 0 in units:
                        after(act, projected, b * PROJ)
                    for u in units:
                        act.wait_ge(turned, xt_number(b, u) + 1)
                        act.activation(xTh[:, :, 2 * u * P:(2 * u + 2) * P],
                                       tp[u % 2].rearrange("p (d t) -> p d t", d=DC),
                                       ACT.Copy).then_inc(turned_hi, 1)

                def high_qk(b):
                    after(act, scored, b * TPC)
                    for u in range(PROJ_QK):
                        m, t = u % (2 * DC), u // (2 * DC)
                        cols = slice(t * BANK, (t + 1) * BANK)
                        act.wait_ge(projected, b * PROJ + u + 1)
                        act.activation(qkh[:, m, cols], bank[u % 4], ACT.Identity, bias=bqk[:, m:m + 1],
                                       scale=1.0).then_inc(split_hi, 1)

                def high_v(b, units):
                    if 0 in units:
                        after(act, mixed, b * TPC)
                    for u in units:
                        act.wait_ge(projected, b * PROJ + PROJ_QK + u + 1)
                        act.activation(vh[:, 2 * u:2 * u + 2, :],
                                       v_bank[u % 2].rearrange("p (t d) -> p t d", d=D),
                                       ACT.Copy).then_inc(split_hi, 1)

                def exp(b, i):
                    act.wait_ge(maxed, b * TPC + i + 1)
                    if i >= 2:
                        act.wait_ge(turned, pt_first(b, i - 2) + PT[i - 2])
                    n = (i + 1) * P
                    act.activation(prob[i % 2][:, 0:n], score[i % 2][:, 0:n], ACT.Exp, bias=negmax[:, i:i + 1],
                                   scale=1.0, accum_out=rsum[:, i:i + 1]).then_inc(exped, 1)

                def high_p(b, i):
                    after(act, mixed, b * TPC + i - 1)
                    for u in range(PT[i]):
                        act.wait_ge(turned, pt_first(b, i) + u + 1)
                        w = min(4, i + 1 - 4 * u)
                        act.activation(pTh[i % 2][:, 4 * u:4 * u + w, :],
                                       tp_of(b, i, u)[:, 0:w * P].rearrange("p (k q) -> p k q", q=P),
                                       ACT.Copy).then_inc(turned_hi, 1)

                def body(b):
                    high_v(b, range(0, 2))
                    exp(b, 0)
                    exp(b, 1)
                    high_v(b, range(2, PROJ_V))
                    for i in range(TPC):
                        high_p(b, i)
                        if routed(b) and i < 4:
                            r.act_norm(act, b - 1, range(2 * i, 2 * i + 2))
                        if routed(b) and 1 <= i < 5:
                            r.act_turn(act, b - 1, [i - 1])
                        if routed(b) and i == 5:
                            r.act_exp(act, b - 1)
                        if i in (4, 5) and b is not end:
                            norm(b + 1, range((i - 4) * HALF, (i - 3) * HALF))
                        if i + 2 < TPC:
                            exp(b, i + 2)
                        if i in XT_STEPS and b is not end:
                            high_x(b + 1, xt_units(i))
                    if b is not end:
                        high_qk(b + 1)

                norm(0, range(TPC))
                high_x(0)
                act.wait_ge(w_ok, 1)
                high_qk(0)
                bodies(act, body)
                r.act_norm(act, end)
                r.act_turn(act, end)
                r.act_exp(act, end)

            @block.vector
            def _(dve):
                def norm_stats(b, tiles):
                    if 0 in tiles:
                        dve.wait_ge(xa_in, b * 16 + 16)
                    for j in tiles:
                        last = dve.bn_stats(stats[:, j, :], xa[:, j, :])
                    if TPC - 1 in tiles:
                        last.then_inc(stat, 1)

                def norm_mean_var(b):
                    dve.wait_ge(stat, b + 1)
                    after(dve, normed, b * TPC)
                    stand_alone(dve, s)
                    for j in range(TPC):
                        last = dve.bn_aggr(mv[:, j, :], stats[:, j, :])
                    last.then_inc(meanvar, 1)

                def low_x(b, units=range(XT)):
                    for u in units:
                        dve.wait_ge(turned_hi, xt_number(b, u) + 1)
                        cols = slice(2 * u * P, (2 * u + 2) * P)
                        dve.tensor_tensor(xTl[:, :, cols],
                                          tp[u % 2].rearrange("p (d t) -> p d t", d=DC),
                                          xTh[:, :, cols].bitcast(F32), ALU.subtract).then_inc(turned_lo, 1)

                def low_qk(b, units=range(PROJ_QK)):
                    for u in units:
                        dve.wait_ge(split_hi, b * PROJ + u + 1)
                        m, t = u % (2 * DC), u // (2 * DC)
                        cols = slice(t * BANK, (t + 1) * BANK)
                        dve.scalar_tensor_tensor(qkl[:, m, cols], bank[u % 4], bqk[:, m:m + 1],
                                                 qkh[:, m, cols].bitcast(F32), ALU.add,
                                                 ALU.subtract).then_inc(split_lo, 1)

                def low_v(b, units):
                    for u in units:
                        dve.wait_ge(split_hi, b * PROJ + PROJ_QK + u + 1)
                        tiles = slice(2 * u, 2 * u + 2)
                        dve.tensor_tensor(vl[:, tiles, :], v_bank[u % 2].rearrange("p (t d) -> p t d", d=D),
                                          vh[:, tiles, :].bitcast(F32), ALU.subtract).then_inc(split_lo, 1)

                def maximum(b, i):
                    dve.wait_ge(scored, b * TPC + i + 1)
                    dve.tensor_reduce(negmax[:, i:i + 1], score[i % 2][:, 0:(i + 1) * P], AX.X, ALU.max,
                                      negate=True).then_inc(maxed, 1)

                def low_p(b, i):
                    for u in range(PT[i]):
                        dve.wait_ge(turned_hi, pt_first(b, i) + u + 1)
                        w = min(4, i + 1 - 4 * u)
                        dve.tensor_tensor(pTl[i % 2][:, 4 * u:4 * u + w, :],
                                          tp_of(b, i, u)[:, 0:w * P].rearrange("p (k q) -> p k q", q=P),
                                          pTh[i % 2][:, 4 * u:4 * u + w, :].bitcast(F32),
                                          ALU.subtract).then_inc(turned_lo, 1)

                def residual(b, i):
                    dve.wait_ge(exped, b * TPC + i + 1)
                    dve.reciprocal(rinv[:, i:i + 1], rsum[:, i:i + 1]).then_inc(inverted, 1)
                    dve.wait_ge(inverted, b * TPC + i + 1)
                    dve.wait_ge(xr_biased[i // HALF], b + 1)
                    if i % HALF == 0:
                        after(dve, x2_out[i // HALF], b * 16)
                    if routed(b):
                        dve.wait_ge(r.normed, (b - 1) * TPC + i + 1)
                    dve.wait_ge(mixed, b * TPC + i + 1)
                    dve.scalar_tensor_tensor(x2[:, i, :], po[:, 0:D], rinv[:, i:i + 1], xr[:, i, :],
                                             ALU.mult, ALU.add).then_inc(summed, 1)

                def route_stats(b, i):
                    dve.wait_ge(summed, b * TPC + i + 1)
                    last = dve.bn_stats(r.stats[:, i, :], x2[:, i, :])
                    if i == TPC - 1:
                        last.then_inc(r.stat, 1)
                        r.dve_mean_var(dve, b)

                def body(b):
                    for u in range(PROJ_V):
                        low_v(b, [u])
                        if u == 1:
                            maximum(b, 0)
                            maximum(b, 1)
                        if listed_in(b) and u < 3:
                            r.dve_onehots(dve, b - 2, range(2 + 2 * u, 4 + 2 * u))
                    for i in range(TPC):
                        low_p(b, i)
                        if routed(b) and i == 5:
                            r.dve_largest(dve, b - 1)
                        if i + 2 < TPC:
                            maximum(b, i + 2)
                        if listed_in(b) and i == 0:
                            r.dve_list(dve, b - 2)
                        if i > 0:
                            residual(b, i - 1)
                        if i in (2, 3) and b is not end:
                            norm_stats(b + 1, range((i - 2) * HALF, (i - 1) * HALF))
                            if i == 3:
                                norm_mean_var(b + 1)
                        if routed(b) and i == 7:
                            r.dve_choose(dve, b - 1)
                        if i in XT_STEPS and b is not end:
                            low_x(b + 1, xt_units(i))
                        if i > 1:
                            route_stats(b, i - 2)
                    if b is not end:
                        low_qk(b + 1, range(0, 4))
                    if routed(b):
                        r.dve_place(dve, b - 1)
                    if b is not end:
                        low_qk(b + 1, range(4, PROJ_QK))
                    if routed(b):
                        r.dve_onehots(dve, b - 1, range(0, 2))
                    route_stats(b, TPC - 2)
                    residual(b, TPC - 1)
                    route_stats(b, TPC - 1)

                norm_stats(0, range(TPC))
                norm_mean_var(0)
                dve.wait_ge(w_in, 16 * 3)
                dve.tensor_scalar(bqk[:, 0:DC], bqk[:, 0:DC], SCALE, None, ALU.mult)
                dve.tensor_scalar(raw_w[:, :, 0:D], raw_w[:, :, 0:D], SCALE, None, ALU.mult).then_inc(w_ok, 1)
                dve.wait_ge(w_ok, 1)
                dve.tensor_copy(wh[:], raw_w[:]).then_inc(w_ok, 1)
                dve.wait_ge(w_ok, 2)
                dve.tensor_tensor(wl[:], raw_w[:], wh[:].bitcast(F32), ALU.subtract).then_inc(w_ok, 1)
                low_x(0)
                low_qk(0)
                bodies(dve, body)
                r.dve_onehots(dve, end - 1, range(2, TPC))
                r.dve_list(dve, end - 1)
                r.dve_largest(dve, end)
                r.dve_choose(dve, end)
                r.dve_place(dve, end)
                r.dve_onehots(dve, end)
                r.dve_list(dve, end)
                r.dve_finish(dve, scratch)


def macaron(nc, x, wqkvT, bqkv, gate_wT, w1, w2, rows, x1, out):
    s = Shared()
    s.x, s.wqkvT, s.bqkv, s.w1, s.w2, s.rows, s.x1, s.out = x, wqkvT, bqkv, w1, w2, rows, x1, out
    with ExitStack() as ctx:
        s.sems = ctx
        setup_constants(nc, ctx, s, gate_wT)
        route_phase(nc, s, "r1", s.x, s.x1)
        expert_phase(nc, s, "m1", s.x1)
        attention_phase(nc, s, "at")
        expert_phase(nc, s, "m2", s.out)


def kernel(L0_attn_x, L0_attn_W_qkv, L0_attn_b_qkv, L0_ffn_gate_w, L0_ffn_w1, L0_ffn_w2):
    import concourse.bacc as bacc
    from concourse.bass_utils import run_bass_kernel_spmd

    arrays = {
        "x": np.ascontiguousarray(L0_attn_x).reshape(T, D),
        "wqkvT": np.ascontiguousarray(np.asarray(L0_attn_W_qkv).T),
        "bqkv": np.ascontiguousarray(L0_attn_b_qkv),
        "gate_wT": np.ascontiguousarray(np.asarray(L0_ffn_gate_w).T),
        "w1": np.ascontiguousarray(L0_ffn_w1).reshape(E * D, FF),
        "w2": np.ascontiguousarray(L0_ffn_w2).reshape(E * FF, D),
    }
    nc = bacc.Bacc("TRN2", target_bir_lowering=False, num_devices=1)
    aps = {n: nc.dram_tensor(n, a.shape, F32, kind="ExternalInput").ap() for n, a in arrays.items()}
    rows = nc.dram_tensor("rows", (T, ROW), F32, kind="Internal").ap()
    x1 = nc.dram_tensor("x1", (T + CAP, D), F32, kind="Internal").ap()
    out = nc.dram_tensor("out", (T + CAP, D), F32, kind="ExternalOutput").ap()
    macaron(nc, rows=rows, x1=x1, out=out, **aps)
    result = run_bass_kernel_spmd(nc, [arrays], core_ids=[0])
    return result.results[0]["out"][:T].reshape(BATCH, SEQ, D)
```

```python
from contextlib import ExitStack

import numpy as np
import concourse.bass as bass
from concourse import mybir

F32 = mybir.dt.float32
F32R = mybir.dt.float32r
BF16 = mybir.dt.bfloat16
F16 = mybir.dt.float16
I32 = mybir.dt.int32
U32 = mybir.dt.uint32
ALU = mybir.AluOpType
ACT = mybir.ActivationFunctionType
AX = mybir.AxisListType

P = 128
BATCH, SEQ, D = 8, 1024, 256
T = BATCH * SEQ
E, FF, TOPK = 16, 512, 2
CAP = int(1.25 * T * TOPK / E)
DC = D // P
FC = FF // P
TPC = SEQ // P
HALF = TPC // 2
CHUNKS = T // SEQ
TPE = CAP // P
NST = E * TPE
GRP = 2
GPE = TPE // GRP
GT = GRP * P
PAIR = 2 * GPE
NPAIR = E // 2
ROW = D + E
EPS = 1e-5
SCALE = 1.0 / 16.0
MASKED = -1e30
BANK = 512
NXG = 10
NYO = 5
WIDE = 4
AHEAD = 7
assert CAP % P == 0 and TPE % GRP == 0 and PAIR % NXG == 0 and PAIR % NYO == 0


def after(eng, sem, n):
    if not (isinstance(n, int) and n <= 0):
        eng.wait_ge(sem, n)


def stand_alone(eng, s):
    eng.sem_inc(s.stood_alone, 1)


def in_turn(eng, first, last, body):
    body(first)
    with eng.Fori(first + 1, last) as i:
        body(i)
    body(last)


class Shared:

    def preload(self, sp):
        sp.dma_start(self.raw1_0[:], self.w1[0:D, :].rearrange("(c p) f -> p c f", p=P)).then_inc(self.preloaded, 16)
        sp.dma_start(self.raw2_0[:], self.w2[0:FF, :].rearrange("(c p) d -> p c d", p=P)).then_inc(self.preloaded, 16)


def setup_constants(nc, ctx, s, gate_wT):
    def sb(name, shape, dt):
        return ctx.enter_context(nc.sbuf_tensor(name, shape, dt))

    s.ident = sb("ident", [P, P], F32)
    s.ident_bf = sb("ident_bf", [P, P], BF16)
    s.earlier = sb("earlier", [P, P], BF16)
    s.ones_bf = sb("ones_bf", [P, P], BF16)
    s.causal = sb("causal", [P, P], BF16)
    s.iota_tile = sb("iota_tile", [P, NST], F16)
    s.gw_in = ctx.enter_context(nc.semaphore("const_gw_in"))
    s.iota_e = sb("iota_e", [P, E], F32)
    s.token = sb("token", [P, TPC], F32)
    s.spare = sb("spare", [P, NST], F32)
    s.gw = sb("gw", [P, DC, E], F32)
    s.zeros = sb("zeros", [P, D], F32)
    s.minus_half = sb("minus_half", [P, TPC], F32)
    s.chunk_at = sb("chunk_at", [P, 1], F32)
    s.carry = sb("carry", [P, E], BF16)
    s.slots = sb("slots", [P, NST], F32)
    s.chosen_by = sb("chosen_by", [P, E], I32)
    s.gather_idx = sb("gather_idx", [P, NST], U32)
    s.scatter_idx = sb("scatter_idx", [P, NST], U32)
    s.raw1_0 = sb("raw1_0", [P, DC, FF], F32)
    s.raw2_0 = sb("raw2_0", [P, FC, D], F32)
    s.preloaded = ctx.enter_context(nc.semaphore("preloaded"))
    s.psum = ctx.enter_context(nc.psum_tensor("psum", [P, 8 * BANK], F32))

    tmp = ExitStack()
    iota_i = tmp.enter_context(nc.sbuf_tensor("iota_i", [P, NST], I32))
    spare_i = tmp.enter_context(nc.sbuf_tensor("spare_i", [P, NST], I32))
    token_i = tmp.enter_context(nc.sbuf_tensor("token_i", [P, TPC], I32))
    filled = ctx.enter_context(nc.semaphore("const_filled"))
    iotas = ctx.enter_context(nc.semaphore("const_iotas"))
    s.stood_alone = ctx.enter_context(nc.semaphore("stood_alone"))
    s.constants_ok = ctx.enter_context(nc.semaphore("constants_ok"))
    with nc.Block() as block:
        @block.sync
        def _(sp):
            sp.dma_start(s.gw[:], gate_wT.rearrange("(c p) e -> p c e", p=P)).then_inc(s.gw_in, 16)

        @block.gpsimd
        def _(pool):
            pool.iota(iota_i[:], [[1, NST]], base=0, channel_multiplier=0).then_inc(iotas, 1)
            pool.iota(spare_i[:], [[0, E], [P, TPE]], base=T + 1, channel_multiplier=1).then_inc(iotas, 1)
            pool.iota(token_i[:], [[P, TPC]], base=1, channel_multiplier=1).then_inc(iotas, 1)
            pool.wait_ge(filled, 5)
            for m, fill, op, step, mult in (
                (s.ident, 1.0, ALU.not_equal, -1, 1),
                (s.ident_bf, 1.0, ALU.not_equal, -1, 1),
                (s.earlier, 0.0, ALU.is_gt, 1, -1),
                (s.causal, MASKED, ALU.is_ge, -1, 1),
            ):
                pool.affine_select(out=m[:], in_=m[:], compare_op=op, fill=fill, base=0,
                                   pattern=[[step, P]], channel_multiplier=mult)

        @block.vector
        def _(dve):
            dve.memset(s.ident[:], 0.0).then_inc(filled, 1)
            dve.memset(s.ident_bf[:], 0.0).then_inc(filled, 1)
            dve.memset(s.earlier[:], 1.0).then_inc(filled, 1)
            dve.memset(s.causal[:], 0.0).then_inc(filled, 1)
            dve.memset(s.ones_bf[:], 1.0).then_inc(filled, 1)
            dve.memset(s.minus_half[:], -0.5)
            dve.memset(s.zeros[:], 0.0)
            dve.memset(s.carry[:], 0.0)
            dve.memset(s.slots[:], 0.0)
            dve.wait_ge(iotas, 3)
            dve.tensor_copy(s.iota_tile[:], iota_i[:])
            dve.tensor_copy(s.iota_e[:], iota_i[:, 0:E])
            dve.tensor_copy(s.token[:], token_i[:])
            dve.memset(s.chunk_at[:], 0.0)
            dve.tensor_copy(s.spare[:], spare_i[:]).then_inc(s.constants_ok, 1)
            dve.wait_ge(s.constants_ok, 1)
    tmp.close()


NORM_STEPS = 4


def norm_factors(pool, s, mv, vareps, rstd, shift, sem, c):
    n = c * NORM_STEPS
    stand_alone(pool, s)
    pool.tensor_scalar(vareps[:], mv[:, :, 1], EPS, None, ALU.add).then_inc(sem, 1)
    pool.wait_ge(sem, n + 1)
    pool.tensor_tensor(rstd[:], vareps[:], s.minus_half[:], ALU.pow).then_inc(sem, 1)
    pool.wait_ge(sem, n + 2)
    pool.tensor_tensor(vareps[:], mv[:, :, 0], rstd[:], ALU.mult).then_inc(sem, 1)
    pool.wait_ge(sem, n + 3)
    stand_alone(pool, s)
    pool.tensor_scalar(shift[:], vareps[:], -1.0, None, ALU.mult).then_inc(sem, 1)


class Router:

    CHOSEN, CHAIN = 7, 11

    def __init__(self, nc, ctx, s, name, source, banks, last_banks=None):
        def sb(n, shape, dt):
            return ctx.enter_context(nc.sbuf_tensor(f"{name}_{n}", shape, dt))

        def sem(n):
            return s.sems.enter_context(nc.semaphore(f"{name}_{n}"))

        self.nc, self.s, self.source, self.banks, self.last_banks = nc, s, source, banks, last_banks
        self.xc = sb("xc", [P, TPC, D], F32)
        self.xn = sb("xn", [P, TPC, D], F32)
        self.xnT = sb("xnT", [P, DC, SEQ], F32)
        self.stats = sb("stats", [P, TPC, 6], F32)
        self.mv = sb("mv", [P, TPC, 2], F32)
        self.vareps = sb("vareps", [P, TPC], F32)
        self.rstd = sb("rstd", [P, TPC], F32)
        self.shift = sb("shift", [P, TPC], F32)
        self.ex = sb("ex", [P, TPC * E], F32)
        self.ex1 = sb("ex1", [P, TPC * E], F32)
        self.prob = sb("prob", [P, TPC * E], F32)
        self.top = sb("top", [P, TPC, 8], F32)
        self.idx = sb("idx", [P, TPC, 8], U32)
        self.idf = sb("idf", [P, TOPK, TPC], F32)
        self.sum1 = sb("sum1", [P, TPC], F32)
        self.sum2 = sb("sum2", [P, TPC], F32)
        self.rsum = sb("rsum", [P, TPC], F32)
        self.wt = sb("wt", [P, TOPK, TPC], F32)
        self.oh = sb("oh", [P, TOPK, TPC, E], F32)
        self.chosen = sb("chosen", [P, TPC, E], BF16)
        self.gt = sb("gt", [P, TOPK, TPC, E], F32)
        self.gate = sb("gate", [P, TPC, E], F32)
        self.taken = sb("taken", [P, E], BF16)
        self.rk = sb("rk", [P, TOPK, TPC, E], F32)
        self.rank = sb("rank", [P, TOPK, TPC], F32)
        self.rank_i = sb("rank_i", [P, TOPK, TPC], I32)
        self.high = sb("high", [P, TOPK, TPC], I32)
        self.low = sb("low", [P, TOPK, TPC], I32)
        self.lowf = sb("lowf", [P, TOPK, TPC], F32)
        self.over = sb("over", [P, TOPK, TPC], F32)
        self.tile1 = sb("tile1", [P, TOPK, TPC], F32)
        self.tilef = sb("tilef", [P, TOPK, TPC], F32)
        self.onehot_row = sb("onehot_row", [P, TPC, TOPK, P], F16)
        self.onehot_tile = sb("onehot_tile", [P, TPC, TOPK, NST], F16)
        self.taken_slot = sb("taken_slot", [P, NST], F32)

        self.x_in = [sem(f"x_in{h}") for h in range(2)]
        self.stat = sem("stat")
        self.meanvar = sem("meanvar")
        self.scaled = sem("scaled")
        self.normed = sem("normed")
        self.xn_out = sem("xn_out")
        self.turned = sem("turned")
        self.logits = sem("logits")
        self.chain = sem("chain")
        self.chosen_ok = sem("chosen_ok")
        self.gate_parts = sem("gate_parts")
        self.gate_ok = sem("gate_ok")
        self.gate_out = sem("gate_out")
        self.ranked = sem("ranked")
        self.onehots = sem("onehots")
        self.row_onehots = sem("row_onehots")
        self.listed = sem("listed")
        self.added = sem("added")
        self.carried = sem("carried")
        self.counted = sem("counted")
        self.read = [sem(f"read{u}") for u in range(7)]

    def banks_of(self, c):
        return self.last_banks if self.last_banks and isinstance(c, int) and c == CHUNKS - 1 else self.banks

    def bank(self, u, c):
        banks = self.banks_of(c)
        b = banks[u % len(banks)]
        return self.s.psum[:, b * BANK:(b + 1) * BANK]

    def wait_bank(self, pe, u, c):
        banks = self.banks_of(c)
        if banks is self.last_banks:
            return
        if len(banks) == 1 and u > 0:
            after(pe, self.read[u - 1], c + 1)
        else:
            after(pe, self.read[u if len(banks) > 1 else 6], c)

    def half(self, dram, c, h):
        return dram[bass.ds(c * SEQ + h * HALF * P, HALF * P), :].rearrange("(j p) d -> p j d", p=P)

    def load(self, sp, c, h):
        after(sp, self.normed, (c - 1) * TPC + (h + 1) * HALF)
        sp.dma_start(self.xc[:, h * HALF:(h + 1) * HALF, :], self.half(self.source, c, h)).then_inc(self.x_in[h], 16)

    def store_rows(self, sp, c):
        sp.wait_ge(self.normed, c * TPC + TPC)
        dst = self.s.rows[bass.ds(c * SEQ, SEQ), 0:D]
        sp.dma_start(dst.rearrange("(j p) d -> p j d", p=P), self.xn[:]).then_inc(self.xn_out, 16)

    def store_gates(self, sp, c):
        sp.wait_ge(self.gate_ok, c + 1)
        dst = self.s.rows[bass.ds(c * SEQ, SEQ), D:ROW]
        sp.dma_start(dst.rearrange("(j p) d -> p j d", p=P), self.gate[:]).then_inc(self.gate_out, 16)

    def dve_stats(self, dve, c, tiles=range(TPC)):
        for j in tiles:
            if j % HALF == 0:
                dve.wait_ge(self.x_in[j // HALF], c * 16 + 16)
            last = dve.bn_stats(self.stats[:, j, :], self.xc[:, j, :])
        if TPC - 1 in tiles:
            last.then_inc(self.stat, 1)
            self.dve_mean_var(dve, c)

    def dve_mean_var(self, dve, c):
        dve.wait_ge(self.stat, c + 1)
        after(dve, self.normed, c * TPC)
        stand_alone(dve, self.s)
        for j in range(TPC):
            last = dve.bn_aggr(self.mv[:, j, :], self.stats[:, j, :])
        last.then_inc(self.meanvar, 1)

    def pool_scale(self, pool, c):
        pool.wait_ge(self.meanvar, c + 1)
        norm_factors(pool, self.s, self.mv, self.vareps, self.rstd, self.shift, self.scaled, c)

    def act_norm(self, act, c, tiles=range(TPC)):
        if 0 in tiles:
            act.wait_ge(self.scaled, c * NORM_STEPS + NORM_STEPS)
            after(act, self.turned, c * 4)
            after(act, self.xn_out, c * 16)
        for j in tiles:
            act.activation(self.xn[:, j, :], self.xc[:, j, :], ACT.Identity, bias=self.shift[:, j:j + 1],
                           scale=self.rstd[:, j:j + 1]).then_inc(self.normed, 1)

    def pe_turn(self, pe, c, units=range(4)):
        for u in units:
            pe.wait_ge(self.normed, c * TPC + 2 * u + 2)
            self.wait_bank(pe, u, c)
            bank = self.bank(u, c)
            for k in range(4):
                d, j = k // 2, 2 * u + k % 2
                last = pe.transpose(bank[:, k * P:(k + 1) * P], self.xn[:, j, d * P:(d + 1) * P], self.s.ident[:])
            last.then_inc(self.turned, 1)

    def act_turn(self, act, c, units=range(4)):
        if 0 in units:
            after(act, self.logits, c)
        for u in units:
            act.wait_ge(self.turned, c * 4 + u + 1)
            act.activation(self.xnT[:, :, 2 * u * P:(2 * u + 2) * P],
                           self.bank(u, c).rearrange("p (d t) -> p d t", d=DC), ACT.Copy).then_inc(self.read[u], 1)

    def act_norm_turn(self, act, c):
        self.act_norm(act, c, range(0, 4))
        self.act_turn(act, c, [0])
        self.act_norm(act, c, range(4, 6))
        self.act_turn(act, c, [1])
        self.act_norm(act, c, range(6, 8))
        self.act_turn(act, c, [2, 3])

    def pe_logits(self, pe, c, units=range(4)):
        if 0 in units:
            self.wait_bank(pe, 4, c)
        for u in units:
            pe.wait_ge(self.read[u], c + 1)
            for j in (2 * u, 2 * u + 1):
                out = self.bank(4, c).rearrange("p (j n) -> p j n", j=TPC)[:, j, 0:WIDE * E]
                for d in range(DC):
                    last = pe.matmul(out.rearrange("p (w e) -> p w e", e=E), self.xnT[:, d, j * P:(j + 1) * P],
                                     self.s.gw[:, d:d + 1, :].to_broadcast([P, WIDE, E]),
                                     start=(d == 0), stop=(d == DC - 1))
        if 3 in units:
            last.then_inc(self.logits, 1)

    def pe_gate_start(self, pe, c):
        self.pe_turn(pe, c, [0, 1])
        self.pe_logits(pe, c, [0])
        self.pe_turn(pe, c, [2])
        self.pe_logits(pe, c, [1])

    def pe_gate_end(self, pe, c):
        self.pe_turn(pe, c, [3])
        self.pe_logits(pe, c, [2, 3])

    def act_exp(self, act, c):
        act.wait_ge(self.logits, c + 1)
        after(act, self.carried, c)
        logits = self.bank(4, c).rearrange("p (j n) -> p j n", j=TPC)[:, :, 0:E]
        act.activation(self.ex[:].rearrange("p (j e) -> p j e", e=E), logits, ACT.Exp,
                       scale=-1.0).then_inc(self.read[4], 1)

    def dve_link(self, dve, c):
        def link(ins):
            self.links += 1
            ins.then_inc(self.chain, 1)
            dve.wait_ge(self.chain, c * self.CHAIN + self.links)
        return link

    def dve_largest(self, dve, c):
        self.links = 0
        link = self.dve_link(dve, c)

        s = self.s
        dve.wait_ge(self.read[4], c + 1)
        link(dve.tensor_scalar(self.ex1[:], self.ex[:], 1.0, None, ALU.add))
        link(dve.reciprocal(self.prob[:], self.ex1[:]))
        stand_alone(dve, s)
        for j in range(TPC):
            last = dve.max(self.top[:, j, :], self.prob[:, j * E:(j + 1) * E])
        link(last)

    def dve_choose(self, dve, c):
        link = self.dve_link(dve, c)
        s = self.s
        dve.tensor_tensor(self.sum1[:], self.top[:, :, 0], self.top[:, :, 1], ALU.add)
        for j in range(TPC):
            last = dve.max_index(self.idx[:, j, :], self.top[:, j, :], self.prob[:, j * E:(j + 1) * E])
        link(last)
        dve.tensor_copy(self.idf[:], self.idx[:, :, 0:TOPK].rearrange("p j k -> p k j"))
        link(dve.tensor_scalar(self.sum2[:], self.sum1[:], 1e-6, None, ALU.add))
        link(dve.reciprocal(self.rsum[:], self.sum2[:]))
        after(dve, self.gate_ok, c)
        dve.scalar_tensor_tensor(self.wt[:], self.top[:, :, 0:TOPK].rearrange("p j k -> p k j"), 0.5,
                                 self.rsum[:].unsqueeze(1).to_broadcast([P, TOPK, TPC]), ALU.mult, ALU.mult)
        link(dve.tensor_tensor(
            self.oh[:].rearrange("p k j e -> p (k j) e"),
            s.iota_e[:].unsqueeze(1).to_broadcast([P, TOPK * TPC, E]),
            self.idf[:].rearrange("p k j -> p (k j)").unsqueeze(2).to_broadcast([P, TOPK * TPC, E]), ALU.is_equal))
        dve.tensor_tensor(self.chosen[:], self.oh[:, 0], self.oh[:, 1], ALU.add).then_inc(self.chosen_ok, 1)
        assert self.links == self.CHOSEN

    def pool_gates(self, pool, c):
        pool.wait_ge(self.chain, c * self.CHAIN + self.CHOSEN)
        pool.tensor_tensor(
            self.gt[:].rearrange("p k j e -> p (k j) e"), self.oh[:].rearrange("p k j e -> p (k j) e"),
            self.wt[:].rearrange("p k j -> p (k j)").unsqueeze(2).to_broadcast([P, TOPK * TPC, E]),
            ALU.mult).then_inc(self.gate_parts, 1)
        pool.wait_ge(self.gate_parts, c + 1)
        after(pool, self.gate_out, c * 16)
        stand_alone(pool, self.s)
        pool.tensor_tensor(self.gate[:], self.gt[:, 0], self.gt[:, 1], ALU.add).then_inc(self.gate_ok, 1)

    def pe_rank(self, pe, c):
        s = self.s
        pe.wait_ge(self.chosen_ok, c + 1)
        after(pe, self.carried, c)
        self.wait_bank(pe, 5, c)
        n = TPC * E
        bank = self.bank(5, c)
        pe.matmul(bank[:, 0:n], s.earlier[:], self.chosen[:].rearrange("p j e -> p (j e)"), start=True, stop=False)
        for j in range(TPC - 1):
            pe.matmul(bank[:, (j + 1) * E:n].rearrange("p (j e) -> p j e", e=E), s.ones_bf[:],
                      self.chosen[:, j:j + 1, :].to_broadcast([P, TPC - 1 - j, E]),
                      start=False, stop=False, skip_group_check=True)
        pe.matmul(bank[:, 0:n].rearrange("p (j e) -> p j e", e=E), s.ones_bf[:],
                  s.carry[:].unsqueeze(1).to_broadcast([P, TPC, E]), start=False, stop=True).then_inc(self.ranked, 1)

    def dve_place(self, dve, c):
        link = self.dve_link(dve, c)
        s = self.s
        dve.wait_ge(self.ranked, c + 1)
        counts = self.bank(5, c)[:, 0:TPC * E].rearrange("p (j e) -> p j e", e=E)
        for k in range(TOPK):
            last = dve.tensor_tensor(self.rk[:, k], self.oh[:, k], counts, ALU.mult)
        last.then_inc(self.read[5], 1)
        dve.wait_ge(self.read[5], c + 1)
        with self.nc.allow_low_precision("counts up to TPC per partition, exact in bfloat16"):
            dve.tensor_reduce(self.taken[:], self.chosen[:].rearrange("p j e -> p e j"), AX.X, ALU.add)
        link(dve.tensor_reduce(self.rank[:].rearrange("p k j -> p (k j)"),
                               self.rk[:].rearrange("p k j e -> p (k j) e"), AX.X, ALU.add))
        dve.tensor_tensor(s.carry[:], s.carry[:], self.taken[:], ALU.add).then_inc(self.carried, 1)
        dve.tensor_scalar(self.over[:], self.rank[:], float(CAP), 1000.0, ALU.is_ge, ALU.mult)
        link(dve.tensor_copy(self.rank_i[:], self.rank[:]))
        dve.tensor_scalar(self.high[:], self.rank_i[:], 7, None, ALU.arith_shift_right)
        dve.scalar_tensor_tensor(self.tile1[:], self.idf[:], float(TPE), self.over[:], ALU.mult, ALU.add)
        link(dve.tensor_scalar(self.low[:], self.rank_i[:], P - 1, None, ALU.bitwise_and))
        dve.tensor_copy(self.lowf[:], self.low[:])
        link(dve.tensor_tensor(self.tilef[:], self.high[:], self.tile1[:], ALU.add))
        assert self.links == self.CHAIN

    def dve_onehots(self, dve, c, tiles=range(TPC)):
        s = self.s
        if 0 in tiles:
            after(dve, self.listed, c)
        for j in tiles:
            dve.tensor_scalar(self.onehot_row[:, j, 0, :], s.iota_tile[:, 0:P], self.lowf[:, 0, j:j + 1],
                              None, ALU.is_equal)
            for k in range(TOPK):
                dve.tensor_scalar(self.onehot_tile[:, j, k, :], s.iota_tile[:], self.tilef[:, k, j:j + 1],
                                  s.token[:, j:j + 1], ALU.is_equal, ALU.mult).then_inc(self.onehots, 1)

    def pool_onehots(self, pool, c):
        pool.wait_ge(self.chain, c * self.CHAIN + self.CHAIN)
        after(pool, self.listed, c)
        stand_alone(pool, self.s)
        for j in range(TPC):
            pool.tensor_scalar(self.onehot_row[:, j, 1, :], self.s.iota_tile[:, 0:P],
                               self.lowf[:, 1, j:j + 1], None, ALU.is_equal).then_inc(self.row_onehots, 1)

    def pe_list(self, pe, c):
        self.wait_bank(pe, 6, c)
        n = TPC * TOPK
        for i in range(n):
            j, k = i // TOPK, i % TOPK
            pe.wait_ge(self.onehots, c * n + i + 1)
            if k == 1:
                pe.wait_ge(self.row_onehots, c * TPC + j + 1)
            last = pe.matmul(self.bank(6, c)[:, 0:NST], self.onehot_row[:, j, k, :], self.onehot_tile[:, j, k, :],
                             start=(i == 0), stop=(i == n - 1))
        last.then_inc(self.listed, 1)

    def pe_count(self, pe):
        pe.wait_ge(self.carried, CHUNKS)
        pe.matmul(self.bank(5, CHUNKS - 1)[:, BANK - E:BANK], self.s.ones_bf[:], self.s.carry[:], start=True,
                  stop=True).then_inc(self.counted, 1)

    def dve_list(self, dve, c):
        s = self.s
        dve.wait_ge(self.listed, c + 1)
        found = self.bank(6, c)[:, 0:NST]
        dve.tensor_scalar(self.taken_slot[:], found, 1.0, s.chunk_at[:, 0:1], ALU.min, ALU.mult)
        dve.tensor_tensor(s.slots[:], found, s.slots[:], ALU.add).then_inc(self.read[6], 1)
        dve.wait_ge(self.read[6], c + 1)
        dve.tensor_scalar(s.chunk_at[:], s.chunk_at[:], float(SEQ), None, ALU.add)
        dve.tensor_tensor(s.slots[:], s.slots[:], self.taken_slot[:], ALU.add).then_inc(self.added, 1)
        dve.wait_ge(self.added, c + 1)

    def dve_finish(self, dve, scratch):
        s = self.s
        tok, gat, emp = scratch
        base = CHUNKS * self.CHAIN
        n = 0

        def link(ins):
            nonlocal n
            n += 1
            ins.then_inc(self.chain, 1)
            dve.wait_ge(self.chain, base + n)

        dve.wait_ge(self.counted, 1)
        dve.tensor_copy(s.chosen_by[:], self.bank(5, CHUNKS - 1)[:, BANK - E:BANK])
        dve.tensor_scalar(gat[:], s.slots[:], -1.0, 0.0, ALU.add, ALU.max)
        link(dve.scalar_tensor_tensor(emp[:], s.slots[:], 0.0, s.spare[:], ALU.is_equal, ALU.mult))
        dve.tensor_copy(s.gather_idx[:], gat[:])
        link(dve.scalar_tensor_tensor(tok[:], s.slots[:], -1.0, emp[:], ALU.add, ALU.add))
        dve.tensor_copy(s.scatter_idx[:], tok[:])
        dve.memset(s.carry[:], 0.0)
        dve.memset(s.chunk_at[:], 0.0)
        link(dve.memset(s.slots[:], 0.0))


def route_phase(nc, s, name, source, stream):
    with ExitStack() as ctx:
        r = Router(nc, ctx, s, name, source, banks=list(range(7)))
        scratch = [ctx.enter_context(nc.sbuf_tensor(f"{name}_fin{i}", [P, NST], F32)) for i in range(3)]
        kept = [ctx.enter_context(nc.semaphore(f"{name}_kept{h}")) for h in range(2)]
        spare_zeroed = ctx.enter_context(nc.semaphore(f"{name}_spare_zeroed"))
        end = CHUNKS - 1

        def there(c, n):
            return not isinstance(c, int) or c + n <= end

        def chunks(eng, step):
            step(0)
            with eng.Fori(1, end - 1) as c:
                step(c)
            step(end - 1)
            step(end)

        with nc.Block() as block:
            @block.sync
            def _(sp):
                def keep(c, h):
                    sp.wait_ge(r.x_in[h], c * 16 + 16)
                    sp.dma_start(r.half(stream, c, h), r.xc[:, h * HALF:(h + 1) * HALF, :]).then_inc(kept[h], 16)

                def load(c, h):
                    after(sp, kept[h], c * 16)
                    stand_alone(sp, s)
                    r.load(sp, c, h)

                def step(c):
                    if there(c, 1):
                        keep(c + 1, 0)
                        keep(c + 1, 1)
                    if there(c, 2):
                        load(c + 2, 0)
                        load(c + 2, 1)
                    if there(c, 1):
                        r.store_rows(sp, c + 1)
                    r.store_gates(sp, c)

                load(0, 0)
                load(0, 1)
                keep(0, 0)
                keep(0, 1)
                load(1, 0)
                load(1, 1)
                r.store_rows(sp, 0)
                step(0)
                for spare in (s.x1[T:T + CAP, :], s.out[T:T + CAP, :]):
                    sp.dma_start(spare.rearrange("(j p) d -> p j d", p=P),
                                 s.zeros[:].unsqueeze(1).to_broadcast([P, TPE, D])).then_inc(spare_zeroed, 16)
                s.preload(sp)
                with sp.Fori(1, end - 1) as c:
                    step(c)
                step(end - 1)
                step(end)
                sp.wait_ge(s.preloaded, 16 * 2)
                sp.wait_ge(spare_zeroed, 16 * 2)
                for q in kept:
                    sp.wait_ge(q, 16 * CHUNKS)
                sp.wait_ge(r.xn_out, 16 * CHUNKS)
                sp.wait_ge(r.gate_out, 16 * CHUNKS)

            @block.gpsimd
            def _(pool):
                def step(c):
                    r.pool_gates(pool, c)
                    if there(c, 2):
                        r.pool_scale(pool, c + 2)
                    r.pool_onehots(pool, c)

                r.pool_scale(pool, 0)
                r.pool_scale(pool, 1)
                chunks(pool, step)

            @block.scalar
            def _(act):
                def step(c):
                    if there(c, 1):
                        r.act_turn(act, c + 1)
                        r.act_exp(act, c + 1)
                    if there(c, 2):
                        r.act_norm(act, c + 2)

                r.act_norm_turn(act, 0)
                r.act_exp(act, 0)
                r.act_norm(act, 1)
                chunks(act, step)

            @block.vector
            def _(dve):
                def step(c):
                    r.dve_largest(dve, c)
                    if not (isinstance(c, int) and c == 0):
                        r.dve_list(dve, c - 1)
                    r.dve_choose(dve, c)
                    if there(c, 2):
                        r.dve_stats(dve, c + 2)
                    r.dve_place(dve, c)
                    r.dve_onehots(dve, c)

                r.dve_stats(dve, 0)
                r.dve_stats(dve, 1)
                chunks(dve, step)
                r.dve_list(dve, end)
                r.dve_finish(dve, scratch)

            @block.tensor
            def _(pe):
                def step(c):
                    if there(c, 1):
                        r.pe_gate_start(pe, c + 1)
                    r.pe_rank(pe, c)
                    if there(c, 1):
                        r.pe_gate_end(pe, c + 1)
                    else:
                        r.pe_count(pe)
                    r.pe_list(pe, c)

                pe.wait_ge(s.gw_in, 16)
                r.pe_gate_start(pe, 0)
                r.pe_gate_end(pe, 0)
                chunks(pe, step)


def expert_phase(nc, s, name, stream):
    with ExitStack() as ctx:
        def sb(n, shape, dt):
            return ctx.enter_context(nc.sbuf_tensor(f"{name}_{n}", shape, dt))

        def sem(n):
            return s.sems.enter_context(nc.semaphore(f"{name}_{n}"))

        raw1 = [s.raw1_0, sb("raw1_1", [P, DC, FF], F32)]
        raw2 = [s.raw2_0, sb("raw2_1", [P, FC, D], F32)]
        w1h = [sb(f"w1h{i}", [P, DC, FF], F32R) for i in range(2)]
        w1l = [sb(f"w1l{i}", [P, DC, FF], F32R) for i in range(2)]
        w2h = [sb(f"w2h{i}", [P, FC, D], F32R) for i in range(2)]
        w2l = [sb(f"w2l{i}", [P, FC, D], F32R) for i in range(2)]
        xg = [sb(f"xg{i}", [P, GRP, ROW], F32) for i in range(NXG)]
        xh = [sb(f"xh{i}", [P, DC, GT], F32R) for i in range(2)]
        xl = [sb(f"xl{i}", [P, DC, GT], F32R) for i in range(2)]
        h = [sb(f"h{i}", [P, FC, GT], F32) for i in range(2)]
        hh = [sb(f"hh{i}", [P, FC, GT], F32R) for i in range(2)]
        hl = [sb(f"hl{i}", [P, FC, GT], F32R) for i in range(2)]
        yo = [sb(f"yo{i}", [P, GRP, D], F32) for i in range(NYO)]
        half = GPE * GRP
        gidx = [sb(f"gidx{i}", [P, half], U32) for i in range(2)]
        sidx = [sb(f"sidx{i}", [P, half], U32) for i in range(2)]

        w_in = [sem(f"w_in{i}") for i in range(2)]
        w_split = sem("w_split")
        gathered = [sem(f"gathered{i}") for i in range(NXG)]
        gidx_ok = sem("gidx_ok")
        sidx_ok = sem("sidx_ok")
        turned = sem("turned")
        x_hi = sem("x_hi")
        x_lo = sem("x_lo")
        up = sem("up")
        act_h = sem("act_h")
        h_hi = sem("h_hi")
        h_lo = sem("h_lo")
        down = sem("down")
        weighted = sem("weighted")
        scattered = [sem(f"scattered{i}") for i in range(NYO)]

        psum = s.psum
        px = [psum[:, i * BANK:(i + 1) * BANK] for i in (0, 1)]
        ph = [psum[:, (2 + 2 * i) * BANK:(4 + 2 * i) * BANK] for i in (0, 1)]
        po = [psum[:, i * BANK:(i + 1) * BANK] for i in (6, 7)]
        end = NPAIR - 1

        def ahead(i, j, n, part):
            if j + n < PAIR:
                part(i, j + n)
            elif i is not end:
                part(i + 1, j + n - PAIR)

        with nc.Block() as block:
            @block.sync
            def _(sp):
                def load(e, p):
                    after(sp, w_split, e * 4 - 4)
                    w1 = s.w1[bass.ds(e * D, D), :].rearrange("(c p) f -> p c f", p=P)
                    w2 = s.w2[bass.ds(e * FF, FF), :].rearrange("(c p) d -> p c d", p=P)
                    sp.dma_start(raw1[p][:], w1).then_inc(w_in[p], 16)
                    sp.dma_start(raw2[p][:], w2).then_inc(w_in[p], 16)

                def step(i):
                    load(i * 2, 0)
                    load(i * 2 + 1, 1)

                sp.wait_ge(gathered[1], 16 * GRP)
                load(1, 1)
                with sp.Fori(1, NPAIR) as i:
                    step(i)

            @block.gpsimd
            def _(pool):
                def gather(i, j):
                    b = j % NXG
                    after(pool, weighted, (i * PAIR + j + 1 - NXG) * GRP)
                    stand_alone(pool, s)
                    for t in range(GRP):
                        k = (j % GPE) * GRP + t
                        pool.indirect_dma_start(
                            xg[b][:, t, :], None, s.rows[:, :],
                            bass.IndirectOffsetOnAxis(gidx[j // GPE][:, k:k + 1], axis=0),
                        ).then_inc(gathered[b], 16)

                def scatter(i, j):
                    b = j % NYO
                    pool.wait_ge(weighted, (i * PAIR + j + 1) * GRP)
                    stand_alone(pool, s)
                    for t in range(GRP):
                        k = (j % GPE) * GRP + t
                        pool.indirect_dma_start(
                            stream[:, :],
                            bass.IndirectOffsetOnAxis(sidx[j // GPE][:, k:k + 1], axis=0),
                            yo[b][:, t, :], None, compute_op=ALU.add,
                        ).then_inc(scattered[b], 16)

                def gather_columns(i, w):
                    for q in gathered[w * GPE:(w + 1) * GPE]:
                        after(pool, q, i * 16 * GRP)
                    pool.tensor_copy(gidx[w][:], s.gather_idx[:, bass.ds((i * 2 + w) * half, half)]).then_inc(gidx_ok, 1)
                    pool.wait_ge(gidx_ok, i * 2 + w + 1)

                def scatter_columns(i, w):
                    for q in scattered:
                        after(pool, q, (i * 2 + w) * 16 * GRP)
                    pool.tensor_copy(sidx[w][:], s.scatter_idx[:, bass.ds((i * 2 + w) * half, half)]).then_inc(sidx_ok, 1)
                    pool.wait_ge(sidx_ok, i * 2 + w + 1)

                def body(i):
                    for j in range(PAIR):
                        if (j + AHEAD) % PAIR == GPE and (i is not end or j + AHEAD < PAIR):
                            gather_columns(i + (j + AHEAD) // PAIR, 1)
                        if (j + AHEAD) % PAIR == 0 and i is not end:
                            gather_columns(i + 1, 0)
                        ahead(i, j, AHEAD, gather)
                        if j % GPE == 0:
                            scatter_columns(i, j // GPE)
                        scatter(i, j)

                gather_columns(0, 0)
                for j in range(AHEAD):
                    if j == GPE:
                        gather_columns(0, 1)
                    gather(0, j)
                in_turn(pool, 0, end, body)
                for q in scattered:
                    pool.wait_ge(q, E * 16 * GRP)

            @block.tensor
            def _(pe):
                def where_taken(j, some, none):
                    if j % GPE < GPE - 1:
                        some(GRP)
                        return
                    with pe.If(chosen_by[j // GPE] > GT * (GPE - 1) + P):
                        some(GRP)
                    with pe.Else():
                        with pe.If(chosen_by[j // GPE] > GT * (GPE - 1)):
                            some(1)
                        with pe.Else():
                            none()

                def small(bank, sem):
                    pe.matmul(bank[:, 0:E], s.ones_bf[:], s.ident_bf[:, 0:E], start=True, stop=True).then_inc(sem, 1)

                def turn(i, j):
                    def some(tiles):
                        b = j % NXG
                        pe.wait_ge(gathered[b], (i + 1) * 16 * GRP)
                        after(pe, x_lo, i * PAIR + j - 1)
                        for d in range(DC):
                            for t in range(tiles):
                                k = d * GRP + t
                                last = pe.transpose(px[j % 2][:, k * P:(k + 1) * P],
                                                    xg[b][:, t, d * P:(d + 1) * P], s.ident[:])
                        last.then_inc(turned, 1)

                    def none():
                        pe.wait_ge(gathered[j % NXG], (i + 1) * 16 * GRP)
                        pe.wait_ge(x_lo, i * PAIR + j - 1)
                        small(px[j % 2], turned)

                    where_taken(j, some, none)

                def mm_up(i, j):
                    def some(tiles):
                        p, w, n_rows = j % 2, j // GPE, tiles * P
                        pe.wait_ge(x_lo, i * PAIR + j + 1)
                        if j % GPE == 0:
                            pe.wait_ge(w_split, (i * 2 + w) * 4 + 2)
                        for f in range(FC):
                            if f % 2 == 0:
                                after(pe, act_h, (i * PAIR + j - 2) * 2 + f // 2 + 1)
                            out = ph[p][:, f * GT:f * GT + n_rows]
                            n = 0
                            for a, b in ((w1h, xh), (w1h, xl), (w1l, xh)):
                                for d in range(DC):
                                    last = pe.matmul(out, a[w][:, d, f * P:(f + 1) * P], b[p][:, d, 0:n_rows],
                                                     start=(n == 0), stop=(n == 3 * DC - 1))
                                    n += 1
                            if f % 2:
                                last.then_inc(up, 1)

                    def none():
                        pe.wait_ge(x_lo, i * PAIR + j + 1)
                        for q in range(2):
                            pe.wait_ge(act_h, (i * PAIR + j - 2) * 2 + q + 1)
                            small(ph[j % 2][:, q * BANK:(q + 1) * BANK], up)

                    where_taken(j, some, none)

                def mm_down(i, j):
                    def some(tiles):
                        p, w = j % 2, j // GPE
                        pe.wait_ge(h_lo, (i * PAIR + j + 1) * 2)
                        after(pe, weighted, (i * PAIR + j - 1) * GRP)
                        if j % GPE == 0:
                            pe.wait_ge(w_split, (i * 2 + w) * 4 + 4)
                        for t in range(tiles):
                            out = po[p][:, t * D:(t + 1) * D]
                            n = 0
                            for f in range(FC):
                                for a, b in ((hh, w2h), (hh, w2l), (hl, w2h)):
                                    last = pe.matmul(out, a[p][:, f, t * P:(t + 1) * P], b[w][:, f, :],
                                                     start=(n == 0), stop=(n == 3 * FC - 1))
                                    n += 1
                        last.then_inc(down, 1)

                    def none():
                        pe.wait_ge(h_lo, (i * PAIR + j + 1) * 2)
                        pe.wait_ge(weighted, (i * PAIR + j - 1) * GRP)
                        small(po[j % 2], down)

                    where_taken(j, some, none)

                def body(i):
                    for w in range(2):
                        chosen_by[w] = pe.value_load(s.chosen_by[0:1, bass.ds(i * 2 + w, 1)], min_val=0,
                                                     max_val=T * TOPK)
                    for j in range(PAIR):
                        ahead(i, j, 2, turn)
                        ahead(i, j, 1, mm_up)
                        mm_down(i, j)

                chosen_by = [None, None]
                turn(0, 0)
                turn(0, 1)
                mm_up(0, 0)
                in_turn(pe, 0, end, body)

            @block.scalar
            def _(act):
                def x_high(i, j):
                    act.wait_ge(turned, i * PAIR + j + 1)
                    after(act, up, (i * PAIR + j - 1) * 2)
                    act.activation(xh[j % 2][:], px[j % 2].rearrange("p (d t) -> p d t", d=DC),
                                   ACT.Copy).then_inc(x_hi, 1)

                def gelu(i, j):
                    p = j % 2
                    for q in range(2):
                        act.wait_ge(up, (i * PAIR + j) * 2 + q + 1)
                        after(act, h_lo, (i * PAIR + j - 2) * 2 + q + 1)
                        act.activation(h[p][:, 2 * q:2 * q + 2, :],
                                       ph[p][:, q * BANK:(q + 1) * BANK].rearrange("p (f t) -> p f t", f=2),
                                       ACT.Gelu).then_inc(act_h, 1)

                def weight(i, j):
                    b, y, w = j % NXG, j % NYO, j // GPE
                    act.wait_ge(down, i * PAIR + j + 1)
                    after(act, scattered[y], (i * 2 + j // NYO) * 16 * GRP)
                    for t in range(GRP):
                        act.activation(yo[y][:, t, :], po[j % 2][:, t * D:(t + 1) * D], ACT.Copy,
                                       scale=xg[b][:, t, bass.ds(i * 2 + D + w, 1)]).then_inc(weighted, 1)

                def body(i):
                    for j in range(PAIR):
                        ahead(i, j, 2, x_high)
                        ahead(i, j, 1, gelu)
                        weight(i, j)

                x_high(0, 0)
                x_high(0, 1)
                gelu(0, 0)
                in_turn(act, 0, end, body)

            @block.vector
            def _(dve):
                def x_low(i, j):
                    dve.wait_ge(x_hi, i * PAIR + j + 1)
                    dve.tensor_tensor(xl[j % 2][:].rearrange("p d t -> p (d t)"), px[j % 2],
                                      xh[j % 2][:].bitcast(F32).rearrange("p d t -> p (d t)"),
                                      ALU.subtract).then_inc(x_lo, 1)

                def split_h(i, j):
                    p = j % 2
                    after(dve, down, i * PAIR + j - 1)
                    for q in range(2):
                        rows = slice(2 * q, 2 * q + 2)
                        dve.wait_ge(act_h, (i * PAIR + j) * 2 + q + 1)
                        dve.tensor_copy(hh[p][:, rows, :], h[p][:, rows, :]).then_inc(h_hi, 1)
                        dve.wait_ge(h_hi, (i * PAIR + j) * 2 + q + 1)
                        dve.tensor_tensor(hl[p][:, rows, :], h[p][:, rows, :], hh[p][:, rows, :].bitcast(F32),
                                          ALU.subtract).then_inc(h_lo, 1)

                def split_w(i, w, part):
                    if part == 0:
                        after(dve, w_in[w], i * 32 + (32 if w else 0))
                        after(dve, down, (i * 2 + w - 1) * GPE)
                    raw, hi, lo = ((raw1, w1h, w1l), (raw2, w2h, w2l))[part // 2]
                    if part % 2 == 0:
                        dve.tensor_copy(hi[w][:], raw[w][:]).then_inc(w_split, 1)
                    else:
                        dve.wait_ge(w_split, (i * 2 + w) * 4 + part)
                        dve.tensor_tensor(lo[w][:], raw[w][:], hi[w][:].bitcast(F32),
                                          ALU.subtract).then_inc(w_split, 1)

                def body(i):
                    for j in range(PAIR):
                        ahead(i, j, 2, x_low)
                        ahead(i, j, 1, split_h)
                        part = j % GPE - 1
                        if part >= 0 and j < GPE:
                            split_w(i, 1, part)
                        elif part >= 0 and i is not end:
                            split_w(i + 1, 0, part)

                for part in range(4):
                    split_w(0, 0, part)
                x_low(0, 0)
                x_low(0, 1)
                split_h(0, 0)
                in_turn(dve, 0, end, body)


def attention_phase(nc, s, name):
    with ExitStack() as ctx:
        def sb(n, shape, dt):
            return ctx.enter_context(nc.sbuf_tensor(f"{name}_{n}", shape, dt))

        def sem(n):
            return s.sems.enter_context(nc.semaphore(f"{name}_{n}"))

        r = Router(nc, ctx, s, f"{name}_route", s.out, banks=[7], last_banks=list(range(7)))
        xa = sb("xa", [P, TPC, D], F32)
        stats = sb("stats", [P, TPC, 6], F32)
        mv = sb("mv", [P, TPC, 2], F32)
        vareps = sb("vareps", [P, TPC], F32)
        rstd = sb("rstd", [P, TPC], F32)
        shift = sb("shift", [P, TPC], F32)
        xTh = sb("xTh", [P, DC, SEQ], F32R)
        xTl = sb("xTl", [P, DC, SEQ], F32R)
        wh = sb("wh", [P, DC, 3 * D], F32R)
        wl = sb("wl", [P, DC, 3 * D], F32R)
        bqk = sb("bqk", [P, 2 * DC], F32)
        bv = sb("bv", [P, D], F32)
        qkh = sb("qkh", [P, 2 * DC, SEQ], F32R)
        qkl = sb("qkl", [P, 2 * DC, SEQ], F32R)
        vh = sb("vh", [P, TPC, D], F32R)
        vl = sb("vl", [P, TPC, D], F32R)
        prob = [sb(f"prob{i}", [P, SEQ], F32) for i in range(2)]
        pTh = [sb(f"pTh{i}", [P, TPC, P], F32R) for i in range(2)]
        pTl = [sb(f"pTl{i}", [P, TPC, P], F32R) for i in range(2)]
        negmax = sb("negmax", [P, TPC], F32)
        rsum = sb("rsum", [P, TPC], F32)
        rinv = sb("rinv", [P, TPC], F32)
        xr = sb("xr", [P, TPC, D], F32)
        x2 = r.xc
        raw_w = sb("raw_w", [P, DC, 3 * D], F32)
        scratch = [sb(f"fin{i}", [P, NST], F32) for i in range(3)]

        w_in = sem("w_in")
        w_ok = sem("w_ok")
        xa_in = [sem(f"xa_in{h}") for h in range(2)]
        stat = sem("stat")
        meanvar = sem("meanvar")
        scaled = sem("scaled")
        normed = sem("normed")
        x_turned = sem("x_turned")
        x_hi = sem("x_hi")
        x_lo = sem("x_lo")
        turned = sem("turned")
        turned_hi = sem("turned_hi")
        turned_lo = sem("turned_lo")
        projected = sem("projected")
        split_hi = sem("split_hi")
        split_lo = sem("split_lo")
        scored = sem("scored")
        maxed = sem("maxed")
        exped = sem("exped")
        inverted = sem("inverted")
        mixed = sem("mixed")
        summed = sem("summed")
        xr_in = [sem(f"xr_in{h}") for h in range(2)]
        xr_biased = [sem(f"xr_biased{h}") for h in range(2)]
        x2_out = [sem(f"x2_out{h}") for h in range(2)]

        psum = s.psum
        bank = [psum[:, i * BANK:(i + 1) * BANK] for i in range(8)]
        score = [psum[:, 2 * i * BANK:2 * (i + 1) * BANK] for i in range(2)]
        tp = bank[4:6]
        po = bank[6]
        v_bank = [bank[1], bank[3]]
        end = BATCH - 1

        PROJ_QK, PROJ_V = 2 * DC * 2, TPC // 2
        PROJ = PROJ_QK + PROJ_V
        XT = TPC // 2
        XT_STEPS = (6, 7)
        PT = [(i + 4) // 4 for i in range(TPC)]
        TURNS = sum(PT)
        assert TURNS % 2 == 0

        def pt_number(b, i, k):
            return b * TURNS + sum(PT[:i]) + k

        def tp_of(i, k):
            return tp[(sum(PT[:i]) + k) % 2]

        def xt_units(i):
            k = XT_STEPS.index(i)
            return range(k * XT // 2, (k + 1) * XT // 2)

        def bodies(eng, body):
            body(0)
            body(1)
            with eng.Fori(2, end) as b:
                body(b)
            body(end)

        def routed(b):
            return not (isinstance(b, int) and b == 0)

        def listed_in(b):
            return not (isinstance(b, int) and b <= 1)


        with nc.Block() as block:
            @block.sync
            def _(sp):
                def load_xa(b):
                    if not (isinstance(b, int) and b == 0):
                        sp.wait_ge(x_turned, b * XT)
                    for h in range(2):
                        sp.dma_start(xa[:, h * HALF:(h + 1) * HALF, :], r.half(s.x1, b, h)).then_inc(xa_in[h], 16)

                def load_xr(b, h):
                    after(sp, summed, (b - 1) * TPC + (h + 1) * HALF)
                    sp.dma_start(xr[:, h * HALF:(h + 1) * HALF, :], r.half(s.x1, b, h)).then_inc(xr_in[h], 16)

                def store_x2(b, h):
                    sp.wait_ge(summed, b * TPC + (h + 1) * HALF)
                    sp.dma_start(r.half(s.out, b, h), x2[:, h * HALF:(h + 1) * HALF, :]).then_inc(x2_out[h], 16)

                def body(b):
                    load_xr(b, 1)
                    if routed(b):
                        r.store_rows(sp, b - 1)
                    store_x2(b, 0)
                    if b is not end:
                        load_xr(b + 1, 0)
                    if routed(b):
                        r.store_gates(sp, b - 1)
                    if not (isinstance(b, int) and b >= end - 1):
                        load_xa(b + 2)
                    store_x2(b, 1)

                load_xa(0)
                sp.dma_start(raw_w[:], s.wqkvT.rearrange("(c p) e -> p c e", p=P)).then_inc(w_in, 16)
                with nc.allow_non_contiguous_dma("a bias per partition, once"):
                    sp.dma_start(bqk[:], s.bqkv[0:2 * D].rearrange("(m p) -> p m", p=P)).then_inc(w_in, 16)
                sp.dma_start(bv[:], s.bqkv[2 * D:3 * D].partition_broadcast(P)).then_inc(w_in, 16)
                load_xr(0, 0)
                load_xa(1)
                body(0)
                s.preload(sp)
                body(1)
                with sp.Fori(2, end) as b:
                    body(b)
                body(end)
                sp.wait_ge(s.preloaded, 16 * 4)
                for q in x2_out:
                    sp.wait_ge(q, BATCH * 16)
                r.store_rows(sp, end)
                r.store_gates(sp, end)
                sp.wait_ge(r.xn_out, 16 * CHUNKS)
                sp.wait_ge(r.gate_out, 16 * CHUNKS)

            @block.gpsimd
            def _(pool):
                def scale(b):
                    pool.wait_ge(meanvar, b + 1)
                    norm_factors(pool, s, mv, vareps, rstd, shift, scaled, b)

                def bias(b, h):
                    pool.wait_ge(xr_in[h], b * 16 + 16)
                    rows = slice(h * HALF, (h + 1) * HALF)
                    pool.tensor_tensor(xr[:, rows, :], xr[:, rows, :],
                                       bv[:].unsqueeze(1).to_broadcast([P, HALF, D]),
                                       ALU.add).then_inc(xr_biased[h], 1)

                def body(b):
                    if routed(b):
                        r.pool_scale(pool, b - 1)
                    bias(b, 1)
                    if b is not end:
                        scale(b + 1)
                        bias(b + 1, 0)
                    else:
                        r.pool_scale(pool, b)
                    if routed(b):
                        r.pool_gates(pool, b - 1)
                        r.pool_onehots(pool, b - 1)

                scale(0)
                pool.wait_ge(w_in, 16 * 3)
                bias(0, 0)
                bodies(pool, body)
                r.pool_gates(pool, end)
                r.pool_onehots(pool, end)

            @block.tensor
            def _(pe):
                def turn_x(b, units=range(XT)):
                    for u in units:
                        pe.wait_ge(normed, b * TPC + 2 * u + 2)
                        if not (isinstance(b, int) and b == 0):
                            pe.wait_ge(exped, b * TPC - (1 if u < 2 else 0))
                        out = bank[u]
                        for k in range(4):
                            d, j = k // 2, 2 * u + k % 2
                            last = pe.transpose(out[:, k * P:(k + 1) * P], xa[:, j, d * P:(d + 1) * P], s.ident[:])
                        last.then_inc(x_turned, 1)

                def split_product(out, stat, mov, extra=None):
                    n, total = 0, 3 * len(stat)
                    for a, b in zip(stat, mov):
                        for x, y in ((0, 0), (0, 1), (1, 0)):
                            last = pe.matmul(out, a[x], b[y], start=(n == 0), stop=(n == total - 1))
                            if n == 0 and extra is not None:
                                pe.matmul(*extra, start=False, stop=False, skip_group_check=True)
                            n += 1
                    return last

                def qk(b, units=range(PROJ_QK)):
                    for u in units:
                        m, t = u % (2 * DC), u // (2 * DC)
                        if u < XT:
                            pe.wait_ge(x_lo, b * XT + max(XT // 2, u + 1))
                        if u >= 4:
                            pe.wait_ge(split_lo, b * PROJ + u - 3)
                        cols = slice(t * BANK, (t + 1) * BANK)
                        split_product(bank[u % 4],
                                      [(wh[:, d, m * P:(m + 1) * P], wl[:, d, m * P:(m + 1) * P]) for d in range(DC)],
                                      [(xTh[:, d, cols], xTl[:, d, cols]) for d in range(DC)]).then_inc(projected, 1)

                def v(b, units):
                    for u in units:
                        if u == 0:
                            pe.wait_ge(split_lo, b * PROJ + PROJ_QK)
                        if u >= 2:
                            pe.wait_ge(split_lo, b * PROJ + PROJ_QK + u - 1)
                        for k in range(2):
                            t = slice((2 * u + k) * P, (2 * u + k + 1) * P)
                            last = split_product(v_bank[u % 2][:, k * D:(k + 1) * D],
                                                 [(xTh[:, d, t], xTl[:, d, t]) for d in range(DC)],
                                                 [(wh[:, d, 2 * D:3 * D], wl[:, d, 2 * D:3 * D]) for d in range(DC)])
                        last.then_inc(projected, 1)

                def scores(b, i):
                    if i == BANK // P:
                        pe.wait_ge(split_lo, b * PROJ + PROJ)
                    if i >= 2:
                        pe.wait_ge(exped, b * TPC + i - 1)
                    q = slice(i * P, (i + 1) * P)
                    n = (i + 1) * P
                    for c in range(0, n, BANK):
                        w = min(BANK, n - c)
                        diagonal = (score[i % 2][:, n - P:n], s.ident_bf[:], s.causal[:]) if c + w == n else None
                        last = split_product(score[i % 2][:, c:c + w],
                                             [(qkh[:, d, q], qkl[:, d, q]) for d in range(DC)],
                                             [(qkh[:, DC + d, c:c + w], qkl[:, DC + d, c:c + w]) for d in range(DC)],
                                             extra=diagonal)
                    last.then_inc(scored, 1)

                def turn_p(b, i):
                    pe.wait_ge(exped, b * TPC + i + 1)
                    for u in range(PT[i]):
                        after(pe, turned_lo, pt_number(b, i, u) - 1)
                        out = tp_of(i, u)
                        for k in range(4 * u, min(4 * u + 4, i + 1)):
                            last = pe.transpose(out[:, (k % 4) * P:(k % 4 + 1) * P],
                                                prob[i % 2][:, k * P:(k + 1) * P], s.ident[:])
                        last.then_inc(turned, 1)

                def mix(b, i):
                    if i == 0:
                        pe.wait_ge(split_lo, b * PROJ + PROJ)
                    pe.wait_ge(turned_lo, pt_number(b, i, PT[i]))
                    after(pe, summed, b * TPC + i)
                    split_product(po[:, 0:D], [(pTh[i % 2][:, k, :], pTl[i % 2][:, k, :]) for k in range(i + 1)],
                                  [(vh[:, k, :], vl[:, k, :]) for k in range(i + 1)]).then_inc(mixed, 1)

                def body(b):
                    v(b, range(0, 2))
                    scores(b, 0)
                    scores(b, 1)
                    v(b, range(2, PROJ_V))
                    for i in range(TPC):
                        turn_p(b, i)
                        if routed(b) and i == 5:
                            r.pe_logits(pe, b - 1)
                        if i + 2 < TPC:
                            scores(b, i + 2)
                        if listed_in(b) and i == 0:
                            r.pe_list(pe, b - 2)
                        if i > 0:
                            mix(b, i - 1)
                        if routed(b) and 1 <= i < 5:
                            r.pe_turn(pe, b - 1, [i - 1])
                        if i in XT_STEPS and b is not end:
                            turn_x(b + 1, xt_units(i))
                    if b is not end:
                        qk(b + 1, range(0, 4))
                        if routed(b):
                            r.pe_rank(pe, b - 1)
                        qk(b + 1, range(4, PROJ_QK))
                    mix(b, TPC - 1)
                    if b is end:
                        r.pe_rank(pe, b - 1)

                turn_x(0)
                pe.wait_ge(w_ok, 3)
                qk(0)
                bodies(pe, body)
                r.pe_gate_start(pe, end)
                r.pe_list(pe, end - 1)
                r.pe_gate_end(pe, end)
                r.pe_rank(pe, end)
                r.pe_count(pe)
                r.pe_list(pe, end)

            @block.scalar
            def _(act):
                def norm(b, tiles):
                    if 0 in tiles:
                        act.wait_ge(scaled, b * NORM_STEPS + NORM_STEPS)
                    for j in tiles:
                        act.activation(xa[:, j, :], xa[:, j, :], ACT.Identity, bias=shift[:, j:j + 1],
                                       scale=rstd[:, j:j + 1]).then_inc(normed, 1)

                def high_x(b, units=range(XT)):
                    if 0 in units:
                        after(act, projected, b * PROJ)
                    for u in units:
                        act.wait_ge(x_turned, b * XT + u + 1)
                        act.activation(xTh[:, :, 2 * u * P:(2 * u + 2) * P],
                                       bank[u].rearrange("p (d t) -> p d t", d=DC),
                                       ACT.Copy).then_inc(x_hi, 1)

                def high_qk(b):
                    after(act, scored, b * TPC)
                    for u in range(PROJ_QK):
                        m, t = u % (2 * DC), u // (2 * DC)
                        cols = slice(t * BANK, (t + 1) * BANK)
                        act.wait_ge(projected, b * PROJ + u + 1)
                        act.activation(qkh[:, m, cols], bank[u % 4], ACT.Identity, bias=bqk[:, m:m + 1],
                                       scale=1.0).then_inc(split_hi, 1)

                def high_v(b, units):
                    if 0 in units:
                        after(act, mixed, b * TPC)
                    for u in units:
                        act.wait_ge(projected, b * PROJ + PROJ_QK + u + 1)
                        act.activation(vh[:, 2 * u:2 * u + 2, :],
                                       v_bank[u % 2].rearrange("p (t d) -> p t d", d=D),
                                       ACT.Copy).then_inc(split_hi, 1)

                def exp(b, i):
                    act.wait_ge(maxed, b * TPC + i + 1)
                    if i >= 2:
                        act.wait_ge(turned, pt_number(b, i - 2, PT[i - 2]))
                    n = (i + 1) * P
                    act.activation(prob[i % 2][:, 0:n], score[i % 2][:, 0:n], ACT.Exp, bias=negmax[:, i:i + 1],
                                   scale=1.0, accum_out=rsum[:, i:i + 1]).then_inc(exped, 1)

                def high_p(b, i):
                    after(act, mixed, b * TPC + i - 1)
                    for u in range(PT[i]):
                        act.wait_ge(turned, pt_number(b, i, u) + 1)
                        w = min(4, i + 1 - 4 * u)
                        act.activation(pTh[i % 2][:, 4 * u:4 * u + w, :],
                                       tp_of(i, u)[:, 0:w * P].rearrange("p (k q) -> p k q", q=P),
                                       ACT.Copy).then_inc(turned_hi, 1)

                def body(b):
                    high_v(b, range(0, 2))
                    exp(b, 0)
                    exp(b, 1)
                    high_v(b, range(2, PROJ_V))
                    for i in range(TPC):
                        high_p(b, i)
                        if routed(b) and i < 4:
                            r.act_norm(act, b - 1, range(2 * i, 2 * i + 2))
                        if routed(b) and 1 <= i < 5:
                            r.act_turn(act, b - 1, [i - 1])
                        if routed(b) and i == 5:
                            r.act_exp(act, b - 1)
                        if i in (4, 5) and b is not end:
                            norm(b + 1, range((i - 4) * HALF, (i - 3) * HALF))
                        if i + 2 < TPC:
                            exp(b, i + 2)
                        if i in XT_STEPS and b is not end:
                            high_x(b + 1, xt_units(i))
                    if b is not end:
                        high_qk(b + 1)

                norm(0, range(0, 4))
                high_x(0, [0, 1])
                norm(0, range(4, 8))
                high_x(0, [2, 3])
                act.wait_ge(w_ok, 1)
                high_qk(0)
                bodies(act, body)
                r.act_norm_turn(act, end)
                r.act_exp(act, end)

            @block.vector
            def _(dve):
                def norm_stats(b, tiles):
                    for j in tiles:
                        if j % HALF == 0:
                            dve.wait_ge(xa_in[j // HALF], b * 16 + 16)
                        last = dve.bn_stats(stats[:, j, :], xa[:, j, :])
                    if TPC - 1 in tiles:
                        last.then_inc(stat, 1)

                def norm_mean_var(b):
                    dve.wait_ge(stat, b + 1)
                    after(dve, normed, b * TPC)
                    stand_alone(dve, s)
                    for j in range(TPC):
                        last = dve.bn_aggr(mv[:, j, :], stats[:, j, :])
                    last.then_inc(meanvar, 1)

                def low_x(b, units=range(XT)):
                    for u in units:
                        dve.wait_ge(x_hi, b * XT + u + 1)
                        cols = slice(2 * u * P, (2 * u + 2) * P)
                        dve.tensor_tensor(xTl[:, :, cols],
                                          bank[u].rearrange("p (d t) -> p d t", d=DC),
                                          xTh[:, :, cols].bitcast(F32), ALU.subtract).then_inc(x_lo, 1)

                def low_qk(b, units=range(PROJ_QK)):
                    for u in units:
                        dve.wait_ge(split_hi, b * PROJ + u + 1)
                        m, t = u % (2 * DC), u // (2 * DC)
                        cols = slice(t * BANK, (t + 1) * BANK)
                        dve.scalar_tensor_tensor(qkl[:, m, cols], bank[u % 4], bqk[:, m:m + 1],
                                                 qkh[:, m, cols].bitcast(F32), ALU.add,
                                                 ALU.subtract).then_inc(split_lo, 1)

                def low_v(b, units):
                    for u in units:
                        dve.wait_ge(split_hi, b * PROJ + PROJ_QK + u + 1)
                        tiles = slice(2 * u, 2 * u + 2)
                        dve.tensor_tensor(vl[:, tiles, :], v_bank[u % 2].rearrange("p (t d) -> p t d", d=D),
                                          vh[:, tiles, :].bitcast(F32), ALU.subtract).then_inc(split_lo, 1)

                def maximum(b, i):
                    dve.wait_ge(scored, b * TPC + i + 1)
                    dve.tensor_reduce(negmax[:, i:i + 1], score[i % 2][:, 0:(i + 1) * P], AX.X, ALU.max,
                                      negate=True).then_inc(maxed, 1)

                def low_p(b, i):
                    for u in range(PT[i]):
                        dve.wait_ge(turned_hi, pt_number(b, i, u) + 1)
                        w = min(4, i + 1 - 4 * u)
                        dve.tensor_tensor(pTl[i % 2][:, 4 * u:4 * u + w, :],
                                          tp_of(i, u)[:, 0:w * P].rearrange("p (k q) -> p k q", q=P),
                                          pTh[i % 2][:, 4 * u:4 * u + w, :].bitcast(F32),
                                          ALU.subtract).then_inc(turned_lo, 1)

                def residual(b, i):
                    dve.wait_ge(exped, b * TPC + i + 1)
                    dve.reciprocal(rinv[:, i:i + 1], rsum[:, i:i + 1]).then_inc(inverted, 1)
                    dve.wait_ge(inverted, b * TPC + i + 1)
                    dve.wait_ge(xr_biased[i // HALF], b + 1)
                    if i % HALF == 0:
                        after(dve, x2_out[i // HALF], b * 16)
                    if routed(b):
                        dve.wait_ge(r.normed, (b - 1) * TPC + i + 1)
                    dve.wait_ge(mixed, b * TPC + i + 1)
                    dve.scalar_tensor_tensor(x2[:, i, :], po[:, 0:D], rinv[:, i:i + 1], xr[:, i, :],
                                             ALU.mult, ALU.add).then_inc(summed, 1)

                def route_stats(b, i):
                    dve.wait_ge(summed, b * TPC + i + 1)
                    last = dve.bn_stats(r.stats[:, i, :], x2[:, i, :])
                    if i == TPC - 1:
                        last.then_inc(r.stat, 1)
                        r.dve_mean_var(dve, b)

                def body(b):
                    for u in range(PROJ_V):
                        low_v(b, [u])
                        if u == 1:
                            maximum(b, 0)
                            maximum(b, 1)
                        if listed_in(b) and u < 3:
                            r.dve_onehots(dve, b - 2, range(2 + 2 * u, 4 + 2 * u))
                    for i in range(TPC):
                        low_p(b, i)
                        if routed(b) and i == 5:
                            r.dve_largest(dve, b - 1)
                        if i + 2 < TPC:
                            maximum(b, i + 2)
                        if listed_in(b) and i == 0:
                            r.dve_list(dve, b - 2)
                        if i > 0:
                            residual(b, i - 1)
                        if i in (2, 3) and b is not end:
                            norm_stats(b + 1, range((i - 2) * HALF, (i - 1) * HALF))
                            if i == 3:
                                norm_mean_var(b + 1)
                        if routed(b) and b is not end and i == 7:
                            r.dve_choose(dve, b - 1)
                        if i in XT_STEPS and b is not end:
                            low_x(b + 1, xt_units(i))
                        if i > 1:
                            route_stats(b, i - 2)
                    if b is not end:
                        low_qk(b + 1, range(0, 4))
                        if routed(b):
                            r.dve_place(dve, b - 1)
                        low_qk(b + 1, range(4, PROJ_QK))
                        if routed(b):
                            r.dve_onehots(dve, b - 1, range(0, 2))
                    route_stats(b, TPC - 2)
                    residual(b, TPC - 1)
                    route_stats(b, TPC - 1)
                    if b is end:
                        r.dve_choose(dve, b - 1)
                        r.dve_place(dve, b - 1)
                        r.dve_onehots(dve, b - 1)

                norm_stats(0, range(TPC))
                norm_mean_var(0)
                dve.wait_ge(w_in, 16 * 3)
                dve.tensor_scalar(bqk[:, 0:DC], bqk[:, 0:DC], SCALE, None, ALU.mult)
                dve.tensor_scalar(raw_w[:, :, 0:D], raw_w[:, :, 0:D], SCALE, None, ALU.mult).then_inc(w_ok, 1)
                dve.wait_ge(w_ok, 1)
                dve.tensor_copy(wh[:], raw_w[:]).then_inc(w_ok, 1)
                dve.wait_ge(w_ok, 2)
                dve.tensor_tensor(wl[:], raw_w[:], wh[:].bitcast(F32), ALU.subtract).then_inc(w_ok, 1)
                low_x(0)
                low_qk(0)
                bodies(dve, body)
                r.dve_list(dve, end - 1)
                r.dve_largest(dve, end)
                r.dve_choose(dve, end)
                r.dve_place(dve, end)
                r.dve_onehots(dve, end)
                r.dve_list(dve, end)
                r.dve_finish(dve, scratch)


def macaron(nc, x, wqkvT, bqkv, gate_wT, w1, w2, rows, x1, out):
    s = Shared()
    s.x, s.wqkvT, s.bqkv, s.w1, s.w2, s.rows, s.x1, s.out = x, wqkvT, bqkv, w1, w2, rows, x1, out
    with ExitStack() as ctx:
        s.sems = ctx
        setup_constants(nc, ctx, s, gate_wT)
        route_phase(nc, s, "r1", s.x, s.x1)
        expert_phase(nc, s, "m1", s.x1)
        attention_phase(nc, s, "at")
        expert_phase(nc, s, "m2", s.out)


def kernel(L0_attn_x, L0_attn_W_qkv, L0_attn_b_qkv, L0_ffn_gate_w, L0_ffn_w1, L0_ffn_w2):
    import concourse.bacc as bacc
    from concourse.bass_utils import run_bass_kernel_spmd

    arrays = {
        "x": np.ascontiguousarray(L0_attn_x).reshape(T, D),
        "wqkvT": np.ascontiguousarray(np.asarray(L0_attn_W_qkv).T),
        "bqkv": np.ascontiguousarray(L0_attn_b_qkv),
        "gate_wT": np.ascontiguousarray(np.asarray(L0_ffn_gate_w).T),
        "w1": np.ascontiguousarray(L0_ffn_w1).reshape(E * D, FF),
        "w2": np.ascontiguousarray(L0_ffn_w2).reshape(E * FF, D),
    }
    nc = bacc.Bacc("TRN2", target_bir_lowering=False, num_devices=1)
    aps = {n: nc.dram_tensor(n, a.shape, F32, kind="ExternalInput").ap() for n, a in arrays.items()}
    rows = nc.dram_tensor("rows", (T, ROW), F32, kind="Internal").ap()
    x1 = nc.dram_tensor("x1", (T + CAP, D), F32, kind="Internal").ap()
    out = nc.dram_tensor("out", (T + CAP, D), F32, kind="ExternalOutput").ap()
    macaron(nc, rows=rows, x1=x1, out=out, **aps)
    result = run_bass_kernel_spmd(nc, [arrays], core_ids=[0])
    return result.results[0]["out"][:T].reshape(BATCH, SEQ, D)
```
